# Optimizing a Trainium2 kernel written in Bass

```python
import numpy as np
import jax
import jax.numpy as jnp

def _softmax(x, axis=-1):
    return jax.nn.softmax(x, axis=axis)

def _gelu(x):
    return jax.nn.gelu(x, approximate=True)

def _silu(x):
    return jax.nn.silu(x)

def _sigmoid(x):
    return jax.nn.sigmoid(x)

def _layernorm(x, axis=-1, eps=1e-05):
    m = jnp.mean(x, axis=axis, keepdims=True)
    v = jnp.var(x, axis=axis, keepdims=True)
    return (x - m) / jnp.sqrt(v + eps)

def _scatter_add(tgt, idx, src, axis=0):
    return tgt.at[idx].add(src)

def _segment_sum(src, seg, n):
    return jax.ops.segment_sum(src, seg, n)
kernel_name = 'mk_flamingo_gated_d2_seqx_r8_786ae6'

def setup_inputs(seed: int=0):
    np.random.seed(seed)
    _w = jnp.asarray

    def _rec_inputs():
        import jax
        import jax.numpy as jnp
        _rk = jax.random.key(seed)
        x = -0.0003929 + 0.9999 * jax.random.normal(jax.random.fold_in(_rk, 1), (16, 56, 128), jnp.float32)
        _lenS = 56 - jax.random.randint(jax.random.fold_in(_rk, 7), (16,), 0, max(1, 56 // 4) + 1, jnp.int32)
        _lenS2 = 1500 - jax.random.randint(jax.random.fold_in(_rk, 8), (16,), 0, max(1, 1500 // 4) + 1, jnp.int32)
        _ctx_1024P = jax.random.normal(jax.random.fold_in(_rk, 11), (16, 16, 128), jnp.float32)
        _ctx_1024c = jax.random.dirichlet(jax.random.fold_in(_rk, 511), 0.3 * jnp.ones((16,), jnp.float32), (16, 1500))
        _ctx_1024t = jnp.einsum('bsk,bkd->bsd', _ctx_1024c, _ctx_1024P)
        _ctx_1024t = _ctx_1024t * jax.lax.rsqrt(jnp.mean(jnp.square(_ctx_1024t)) + 1e-12) * 0.953939
        ctx_1024 = 2.81802e-05 + 1.00001 * (_ctx_1024t + 0.3 * jax.random.normal(jax.random.fold_in(_rk, 611), (16, 1500, 128), jnp.float32))
        _validS = jnp.arange(56)[None, :] < _lenS[:, None]
        _validS2 = jnp.arange(1500)[None, :] < _lenS2[:, None]
        _causal = jnp.tril(jnp.ones((56, 56), dtype=bool))
        mask_BxS2_ff1 = jnp.where(jnp.ones((16, 1500), dtype=bool), 1.0, 0.0).astype(jnp.float32)
        mask_BxS2_if1 = jnp.where(jnp.ones((16, 1500), dtype=bool), 1, 0).astype(jnp.int32)
        _g = jax.random.normal(jax.random.fold_in(_rk, 9001), (2, 2), jnp.float32)
        _g = jnp.sign(_g) * jnp.maximum(jnp.abs(_g), 1.0) + (_g == 0) * 1.0
        g_xattn = _g[0]
        g_ffn = _g[1]
        return (x, ctx_1024, mask_BxS2_ff1, mask_BxS2_if1, g_xattn, g_ffn)
    x, ctx_1024, mask_BxS2_ff1, mask_BxS2_if1, g_xattn, g_ffn = _rec_inputs()

    def _L0_xattn_setup():
        import jax, jax.numpy as jnp
        import numpy as np
        D_MODEL = 128
        HEADS = 16
        DEPTH = D_MODEL // HEADS
        B, S = (4, 512)
        EPS_K = 1e-06
        EPS_LN = 1e-06

        def _layernorm(x, g, b):
            m = jnp.mean(x, axis=-1, keepdims=True)
            var = jnp.var(x, axis=-1, keepdims=True)
            return (x - m) * jax.lax.rsqrt(var + EPS_LN) * g + b

        def _split_heads(x):
            bsz, sl, _ = x.shape
            return x.reshape(bsz, sl, HEADS, DEPTH).transpose(0, 2, 1, 3)
        key = jax.random.key(seed)
        ks = jax.random.split(key, 8)
        lecun = 1.0 / np.sqrt(D_MODEL)
        glorot = np.sqrt(2.0 / (D_MODEL + D_MODEL))
        return {'q': jax.random.normal(ks[0], (B, S, D_MODEL), jnp.float32), 'k': jax.random.normal(ks[1], (B, S, D_MODEL), jnp.float32), 'v': jax.random.normal(ks[2], (B, S, D_MODEL), jnp.float32), 'mask': jnp.ones((B, S), jnp.float32), 'wq': jax.random.normal(ks[3], (D_MODEL, D_MODEL), jnp.float32) * lecun, 'wk': jax.random.normal(ks[4], (D_MODEL, D_MODEL), jnp.float32) * lecun, 'wv': jax.random.normal(ks[5], (D_MODEL, D_MODEL), jnp.float32) * lecun, 'ln_gamma': jnp.ones((D_MODEL,), jnp.float32), 'ln_beta': jnp.zeros((D_MODEL,), jnp.float32), 'dense_w': jax.random.normal(ks[6], (D_MODEL, D_MODEL), jnp.float32) * glorot, 'dense_b': jnp.zeros((D_MODEL,), jnp.float32)}
    _L0_xattn_all = _L0_xattn_setup()
    _L0_xattn_in = {k: v for k, v in _L0_xattn_all.items() if k in ('wq', 'wk', 'wv', 'ln_gamma', 'ln_beta', 'dense_w', 'dense_b')}
    del _L0_xattn_all

    def _L0_ffn_setup():
        import jax, jax.numpy as jnp
        import numpy as np
        HIDDEN = 128
        INNER = 512

        def _weight_quant(w):
            scale = 1.0 / jnp.clip(jnp.mean(jnp.abs(w)), 1e-05)
            wq = jnp.clip(jnp.round(w * scale), -1.0, 1.0) / scale
            return w + jax.lax.stop_gradient(wq - w)

        def _act_quant(x):
            scale = 127.0 / jnp.clip(jnp.max(jnp.abs(x), axis=-1, keepdims=True), 1e-05)
            xq = jnp.clip(jnp.round(x * scale), -128.0, 127.0) / scale
            return x + jax.lax.stop_gradient(xq - x)

        def _bitlinear(x, w):
            return jnp.einsum('bsi,oi->bso', _act_quant(x), _weight_quant(w))
        key = jax.random.key(seed)
        k0, k1, k2, k3 = jax.random.split(key, 4)
        x = jax.random.normal(k0, (4, 256, HIDDEN), dtype=jnp.float32)
        w_gate = jax.random.normal(k1, (INNER, HIDDEN), dtype=jnp.float32) / np.sqrt(HIDDEN)
        w_up = jax.random.normal(k2, (INNER, HIDDEN), dtype=jnp.float32) / np.sqrt(HIDDEN)
        w_down = jax.random.normal(k3, (HIDDEN, INNER), dtype=jnp.float32) / np.sqrt(INNER)
        return {'x': x, 'w_gate': w_gate, 'w_up': w_up, 'w_down': w_down}
    _L0_ffn_all = _L0_ffn_setup()
    _L0_ffn_in = {k: v for k, v in _L0_ffn_all.items() if k in ('w_gate', 'w_up', 'w_down')}
    del _L0_ffn_all

    def _L1_xattn_setup():
        import jax, jax.numpy as jnp
        import numpy as np
        D_MODEL = 128
        NUM_HEADS = 16
        D_K = D_MODEL // NUM_HEADS
        NEG_INF = -1000000000.0
        key = jax.random.key(seed)
        ks = jax.random.split(key, 12)
        B, S = (2, 256)
        scale = 1.0 / np.sqrt(D_MODEL)
        inp = {'q': jax.random.normal(ks[0], (B, S, D_MODEL), jnp.float32), 'k': jax.random.normal(ks[1], (B, S, D_MODEL), jnp.float32), 'v': jax.random.normal(ks[2], (B, S, D_MODEL), jnp.float32), 'mask': jnp.ones((B, S), jnp.int32), 'W_q': jax.random.normal(ks[3], (D_MODEL, D_MODEL), jnp.float32) * scale, 'b_q': jnp.zeros((D_MODEL,), jnp.float32), 'W_k': jax.random.normal(ks[4], (D_MODEL, D_MODEL), jnp.float32) * scale, 'b_k': jnp.zeros((D_MODEL,), jnp.float32), 'W_v': jax.random.normal(ks[5], (D_MODEL, D_MODEL), jnp.float32) * scale, 'b_v': jnp.zeros((D_MODEL,), jnp.float32), 'W_o': jax.random.normal(ks[6], (D_MODEL, D_MODEL), jnp.float32) * scale, 'b_o': jnp.zeros((D_MODEL,), jnp.float32)}
        return inp
    _L1_xattn_all = _L1_xattn_setup()
    _L1_xattn_in = {k: v for k, v in _L1_xattn_all.items() if k in ('W_q', 'b_q', 'W_k', 'b_k', 'W_v', 'b_v', 'W_o', 'b_o')}
    del _L1_xattn_all

    def _L1_ffn_setup():
        import jax, jax.numpy as jnp
        import numpy as np
        NUM_EXPERTS = 8
        TOP_K = 2
        key = jax.random.key(seed)
        ks = jax.random.split(key, 6)
        B, S, D, F = (2, 256, 128, 512)
        E = NUM_EXPERTS
        sd = 1.0 / np.sqrt(D)
        sf = 1.0 / np.sqrt(F)
        return {'x': jax.random.normal(ks[0], (B, S, D), dtype=jnp.float32), 'gate_w': jax.random.normal(ks[1], (E, D), dtype=jnp.float32) * sd, 'w1': jax.random.uniform(ks[2], (F, E, D), dtype=jnp.float32, minval=-sd, maxval=sd), 'b1': jax.random.uniform(ks[3], (E, F), dtype=jnp.float32, minval=-sd, maxval=sd), 'w2': jax.random.uniform(ks[4], (D, E, F), dtype=jnp.float32, minval=-sf, maxval=sf), 'b2': jax.random.uniform(ks[5], (E, D), dtype=jnp.float32, minval=-sf, maxval=sf)}
    _L1_ffn_all = _L1_ffn_setup()
    _L1_ffn_in = {k: v for k, v in _L1_ffn_all.items() if k in ('gate_w', 'w1', 'b1', 'w2', 'b2')}
    del _L1_ffn_all
    return {'x': x, 'ctx_1024': ctx_1024, 'mask_BxS2_ff1': mask_BxS2_ff1, 'mask_BxS2_if1': mask_BxS2_if1, 'g_xattn': g_xattn, 'g_ffn': g_ffn, 'L0_xattn_wq': _L0_xattn_in['wq'], 'L0_xattn_wk': _L0_xattn_in['wk'], 'L0_xattn_wv': _L0_xattn_in['wv'], 'L0_xattn_ln_gamma': _L0_xattn_in['ln_gamma'], 'L0_xattn_ln_beta': _L0_xattn_in['ln_beta'], 'L0_xattn_dense_w': _L0_xattn_in['dense_w'], 'L0_xattn_dense_b': _L0_xattn_in['dense_b'], 'L0_ffn_w_gate': _L0_ffn_in['w_gate'], 'L0_ffn_w_up': _L0_ffn_in['w_up'], 'L0_ffn_w_down': _L0_ffn_in['w_down'], 'L1_xattn_W_q': _L1_xattn_in['W_q'], 'L1_xattn_b_q': _L1_xattn_in['b_q'], 'L1_xattn_W_k': _L1_xattn_in['W_k'], 'L1_xattn_b_k': _L1_xattn_in['b_k'], 'L1_xattn_W_v': _L1_xattn_in['W_v'], 'L1_xattn_b_v': _L1_xattn_in['b_v'], 'L1_xattn_W_o': _L1_xattn_in['W_o'], 'L1_xattn_b_o': _L1_xattn_in['b_o'], 'L1_ffn_gate_w': _L1_ffn_in['gate_w'], 'L1_ffn_w1': _L1_ffn_in['w1'], 'L1_ffn_b1': _L1_ffn_in['b1'], 'L1_ffn_w2': _L1_ffn_in['w2'], 'L1_ffn_b2': _L1_ffn_in['b2']}

def reference(x, ctx_1024, mask_BxS2_ff1, mask_BxS2_if1, g_xattn, g_ffn, L0_xattn_wq, L0_xattn_wk, L0_xattn_wv, L0_xattn_ln_gamma, L0_xattn_ln_beta, L0_xattn_dense_w, L0_xattn_dense_b, L0_ffn_w_gate, L0_ffn_w_up, L0_ffn_w_down, L1_xattn_W_q, L1_xattn_b_q, L1_xattn_W_k, L1_xattn_b_k, L1_xattn_W_v, L1_xattn_b_v, L1_xattn_W_o, L1_xattn_b_o, L1_ffn_gate_w, L1_ffn_w1, L1_ffn_b1, L1_ffn_w2, L1_ffn_b2):
    import jax
    import jax.numpy as jnp

    def _L0_xattn_ref(q, k, v, mask, wq, wk, wv, ln_gamma, ln_beta, dense_w, dense_b):
        import jax, jax.numpy as jnp
        import numpy as np
        D_MODEL = 128
        HEADS = 16
        DEPTH = D_MODEL // HEADS
        B, S = (4, 512)
        EPS_K = 1e-06
        EPS_LN = 1e-06

        def _layernorm(x, g, b):
            m = jnp.mean(x, axis=-1, keepdims=True)
            var = jnp.var(x, axis=-1, keepdims=True)
            return (x - m) * jax.lax.rsqrt(var + EPS_LN) * g + b

        def _split_heads(x):
            bsz, sl, _ = x.shape
            return x.reshape(bsz, sl, HEADS, DEPTH).transpose(0, 2, 1, 3)
        bsz = q.shape[0]
        em = mask[:, None, :, None]
        qh = _split_heads(_layernorm(q @ wq, ln_gamma, ln_beta))
        kh = _split_heads(_layernorm(k @ wk, ln_gamma, ln_beta))
        vh = _split_heads(_layernorm(v @ wv, ln_gamma, ln_beta))
        q_prime = jax.nn.relu(qh) + EPS_K
        k_prime = (jax.nn.relu(kh) + EPS_K) * em
        vh = vh * em
        kv = jnp.einsum('bhnd,bhne->bhde', k_prime, vh)
        z = 1.0 / (jnp.einsum('bhnd,bhd->bhn', q_prime, k_prime.sum(axis=-2)) + EPS_K)
        att = jnp.einsum('bhnd,bhde,bhn->bhne', q_prime, kv, z)
        att = att.reshape(bsz, -1, D_MODEL)
        out = att @ dense_w + dense_b
        return _layernorm(out, ln_gamma, ln_beta)

    def _L0_ffn_ref(x, w_gate, w_up, w_down):
        import jax, jax.numpy as jnp
        import numpy as np
        HIDDEN = 128
        INNER = 512

        def _weight_quant(w):
            scale = 1.0 / jnp.clip(jnp.mean(jnp.abs(w)), 1e-05)
            wq = jnp.clip(jnp.round(w * scale), -1.0, 1.0) / scale
            return w + jax.lax.stop_gradient(wq - w)

        def _act_quant(x):
            scale = 127.0 / jnp.clip(jnp.max(jnp.abs(x), axis=-1, keepdims=True), 1e-05)
            xq = jnp.clip(jnp.round(x * scale), -128.0, 127.0) / scale
            return x + jax.lax.stop_gradient(xq - x)

        def _bitlinear(x, w):
            return jnp.einsum('bsi,oi->bso', _act_quant(x), _weight_quant(w))
        gate = jax.nn.silu(_bitlinear(x, w_gate))
        up = _bitlinear(x, w_up)
        return _bitlinear(gate * up, w_down)

    def _L1_xattn_ref(q, k, v, mask, W_q, b_q, W_k, b_k, W_v, b_v, W_o, b_o):
        import jax, jax.numpy as jnp
        import numpy as np
        D_MODEL = 128
        NUM_HEADS = 16
        D_K = D_MODEL // NUM_HEADS
        NEG_INF = -1000000000.0
        B, S, _ = q.shape

        def proj(x, W, b):
            y = x @ W.T + b
            return y.reshape(B, -1, NUM_HEADS, D_K).transpose(0, 2, 1, 3)
        qh = proj(q, W_q, b_q)
        kh = proj(k, W_k, b_k)
        vh = proj(v, W_v, b_v)
        scores = jnp.einsum('bhqd,bhkd->bhqk', qh, kh) / jnp.sqrt(jnp.float32(D_K))
        m = mask[:, None, None, :]
        scores = jnp.where(m == 0, jnp.float32(NEG_INF), scores)
        attn = jax.nn.softmax(scores, axis=-1)
        context = jnp.einsum('bhqk,bhkd->bhqd', attn, vh)
        context = context.transpose(0, 2, 1, 3).reshape(B, S, D_MODEL)
        return context @ W_o.T + b_o

    def _L1_ffn_ref(x, gate_w, w1, b1, w2, b2):
        import jax, jax.numpy as jnp
        import numpy as np
        NUM_EXPERTS = 8
        TOP_K = 2
        logits = jnp.einsum('bsd,ed->bse', x, gate_w)
        probs = jax.nn.softmax(logits, axis=-1)
        topk_probs, topk_idx = jax.lax.top_k(probs, TOP_K)
        oh = jax.nn.one_hot(topk_idx, NUM_EXPERTS, dtype=x.dtype)
        h = jnp.einsum('bsd,fed,bske->bskf', x, w1, oh)
        h = h + jnp.take(b1, topk_idx, axis=0)
        h = jax.nn.gelu(h)
        y = jnp.einsum('bskf,def,bske->bskd', h, w2, oh)
        y = y + jnp.take(b2, topk_idx, axis=0)
        out = jnp.sum(y * topk_probs[..., None], axis=-2)
        return out
    x = x + jnp.tanh(g_xattn[0]) * _L0_xattn_ref(_layernorm(x, axis=-1), ctx_1024, ctx_1024, mask_BxS2_ff1, L0_xattn_wq, L0_xattn_wk, L0_xattn_wv, L0_xattn_ln_gamma, L0_xattn_ln_beta, L0_xattn_dense_w, L0_xattn_dense_b)
    x = x + jnp.tanh(g_ffn[0]) * _L0_ffn_ref(_layernorm(x, axis=-1), L0_ffn_w_gate, L0_ffn_w_up, L0_ffn_w_down)
    x = x + jnp.tanh(g_xattn[1]) * _L1_xattn_ref(_layernorm(x, axis=-1), ctx_1024, ctx_1024, mask_BxS2_if1, L1_xattn_W_q, L1_xattn_b_q, L1_xattn_W_k, L1_xattn_b_k, L1_xattn_W_v, L1_xattn_b_v, L1_xattn_W_o, L1_xattn_b_o)
    x = x + jnp.tanh(g_ffn[1]) * _L1_ffn_ref(_layernorm(x, axis=-1), L1_ffn_gate_w, L1_ffn_w1, L1_ffn_b1, L1_ffn_w2, L1_ffn_b2)
    return x

_drawn_inputs = setup_inputs


def setup_inputs(seed=0):
    import zlib

    import numpy as np

    out = dict(_drawn_inputs(seed))
    spreads = {'g_ffn': (-1.0, 0.6),
     'L0_xattn_ln_gamma': (1.0, 0.2),
     'L0_xattn_ln_beta': (0.0, 0.1),
     'L0_xattn_dense_b': (0.0, 0.1),
     'L1_xattn_b_q': (0.0, 0.606),
     'L1_xattn_b_k': (0.0, 0.8),
     'L1_xattn_b_v': (0.0, 0.1),
     'L1_xattn_b_o': (0.0, 0.1)}
    factors = {'L1_ffn_b1': 8.0, 'L1_ffn_b2': 8.0}
    for name, (base, spread) in spreads.items():
        noise = np.random.default_rng([zlib.crc32(name.encode()), seed]).standard_normal(out[name].shape)
        drawn = base * np.exp(spread * noise) if base else spread * noise
        out[name] = jnp.asarray(drawn.astype(out[name].dtype))
    for name, factor in factors.items():
        out[name] = (out[name] * factor).astype(out[name].dtype)
    return out
```

```python
from contextlib import ExitStack

import concourse.bass as bass
from concourse import mybir

ALU = mybir.AluOpType
ACT = mybir.ActivationFunctionType
AX = mybir.AxisListType
F32 = mybir.dt.float32
BF16 = mybir.dt.bfloat16
I32 = mybir.dt.int32

B, S, D = 16, 56, 128
S2 = 1500
H, DK = 16, 8
T, TK = 12, 125
GT, NG = 4, 3
NT = B // 2
HALF = 64
COLS = NT * 128
INNER = 512
FC = INNER // 128
E = 8
HQ = H * S
HQ2 = HQ // 2
CH = HQ // 128
KC = 3
KCW = S2 // KC
PAIRW = 2 * S
PW = 32
NPAIR = H // 2
SLOTS = 2 * NG
KVW = D + H
EPS_LN, EPS_IN = 1e-5, 1e-6
ROUND = 12582912.0
SCALE = 1.0 / float(DK) ** 0.5

MXS = [f"MX{n}" for n in range(CH * KC)]
PREP = ["K0", "K1", "K2", "V0", "V1", "V2"] + MXS + ["SH"]
FULL = ["K0", "K1", "K2", "DEN", "V0", "V1", "V2", "WO"] + MXS + ["SH"]


def aux_at(w, unit, full):
    if not full:
        return (0 if isinstance(w, int) and w < 0 else len(PREP)) + PREP.index(unit)
    if isinstance(w, int) and w >= B - 1:
        return 2 * len(PREP) + len(FULL) * (B - 2) + 2 * (w - (B - 1)) + ["DEN", "WO"].index(unit)
    return w * len(FULL) + (2 * len(PREP) - len(FULL)) + FULL.index(unit)


def prepared(b):
    return len(PREP) if isinstance(b, int) and b == 0 else len(FULL) * b + (2 * len(PREP) - len(FULL))


def loads(b, par):
    return 8 * b + (16 - 8 * par)


def in_pairs(eng, body, pairs):
    body(0)
    with eng.Fori(1, pairs - 1) as i:
        body(i)
    body(pairs - 1)


def build(nc, xh, ctxT, m0, m1, gates, rows, bq, bk, wkv0, wq0, dense0, wg0, wu0, wd0, wq1, wk1, wv1, wo1,
          gatew, w1, b1, w2, b2, ident_in, hmask_in, den_sel_in, rank_in, out):
    with ExitStack() as ctx:
        def sb(name, shape, dt=F32):
            return ctx.enter_context(nc.sbuf_tensor(name, shape, dt))

        sems = {}

        def sem(name):
            if name not in sems:
                sems[name] = ctx.enter_context(nc.semaphore(name))
            return sems[name]

        x = sb("x", [128, NT, D])
        xn = sb("xn", [128, NT, D])
        t0 = sb("t0", [128, NT, D])
        att = sb("att", [128, NT, D])
        xT = sb("xT", [128, COLS])
        qT = sb("qT", [128, COLS])
        stats = sb("stats", [128, NT, 6])
        mv = sb("mv", [128, NT, 2])
        sd = sb("sd", [128, NT])
        rstd = sb("rstd", [128, NT])
        ident = sb("ident", [128, 128])
        identb = sb("identb", [128, 128], BF16)
        onesf = sb("onesf", [128, 128])
        hmask = sb("hmask", [128, H])
        den_sel = sb("den_sel", [128, 128])
        rank = sb("rank", [128, NT, E])
        eps_ln = sb("eps_ln", [128, 1])
        eps_in = sb("eps_in", [128, 1])
        gate_sb = sb("gate_sb", [128, 4])
        th = sb("th", [128, 4])
        row = sb("row", [128, 5, D])
        GAMMA, BETA, DENSE_B, B_V, B_O = range(5)
        gmask = sb("gmask", [128, D])
        bmask = sb("bmask", [128, D])
        wkv = sb("wkv", [128, 2, D])
        wkv_mean = sb("wkv_mean", [128, 2])
        wq0_sb = sb("wq0_sb", [128, D])
        dense_sb = sb("dense_sb", [128, D])
        bq_sb = sb("bq_sb", [128, 1])
        bk_sb = sb("bk_sb", [128, 1])
        wq1_sb = sb("wq1_sb", [128, D])
        wk1_sb = sb("wk1_sb", [128, D])
        wv1_sb = sb("wv1_sb", [128, D])
        wo1_sb = sb("wo1_sb", [128, 4, D])
        em = sb("em", [128, B * T])
        em2 = sb("em2", [128, B * T])
        emcat = sb("emcat", [128, B * T, 2])
        mi = sb("mi", [128, B * T], I32)
        keep = sb("keep", [128, B * T])
        kscale = sb("kscale", [128, B * T])
        kbias = sb("kbias", [128, B * T])
        kept = sb("kept", [128, B])
        anykept = sb("anykept", [128, B])
        cT = [sb(f"cT{n}", [128, S2]) for n in range(2)]
        kvall = sb("kvall", [128, B, KVW])
        kvtmp = sb("kvtmp", [128, 2, D])
        ss = sb("ss", [128, 2, 2 * GT])
        sdk = sb("sdk", [128, 2, 2 * GT])
        rk = sb("rk", [128, 2, GT, 2])
        wv = sb("wv", [128, 2, GT])
        arena = sb("arena", [128, 8240])
        KN = arena[:, 0:3072].rearrange("p (s t d) -> p s t d", s=6, t=GT)
        VN = arena[:, 3072:6192].rearrange("p (s t d) -> p s t d", s=6, t=GT)
        SQ = arena[:, 6192:8240].rearrange("p (s n) -> p s n", s=2)
        hid = arena[:, 0:4096].rearrange("p (t n) -> p t n", t=NT)
        hqb = arena[:, 4096:6144].bitcast(BF16).rearrange("p (t n) -> p t n", t=NT)
        hqT = arena[:, 6144:8192].bitcast(BF16).rearrange("p (t c n) -> p t c n", t=NT, c=FC)
        hT = arena[:, 0:8192].rearrange("p (s c n) -> p s c n", s=2, c=FC)
        KT = [[sb(f"KT{n}_{k}", [128, S2]) for k in range(2)] for n in range(2)]
        QH = [[sb(f"QH{n}_{k}", [128, H // 2, S]) for k in range(2)] for n in range(2)]
        Kb = [sb(f"Kb{n}", [128, S2], BF16) for n in range(2)]
        Qb = [sb(f"Qb{n}", [128, H, S], BF16) for n in range(2)]
        Vp = [sb(f"Vp{n}", [128, T, NPAIR, PW]) for n in range(2)]
        P = [sb(f"P{n}", [128, HQ]) for n in range(2)]
        mx = sb("mx", [128, CH, KC])
        mneg = sb("mneg", [128, CH], BF16)
        O = sb("O", [128, 2 * PAIRW])
        rden = sb("rden", [128, 2 * PAIRW])
        On = sb("On", [128, 2 * PAIRW])
        wgu = sb("wgu", [128, 2, INNER])
        wdn = sb("wdn", [128, FC, D])
        wgub = sb("wgub", [128, 2, INNER], BF16)
        wdnb = sb("wdnb", [128, FC, D], BF16)
        wabs = sb("wabs", [128, 3])
        wmean = sb("wmean", [128, 3])
        wscale = sb("wscale", [128, 3])
        xqb = sb("xqb", [128, NT, D], BF16)
        xqT = sb("xqT", [128, COLS], BF16)
        amax = sb("amax", [128, NT])
        qs = sb("qs", [128, NT])
        cg = sb("cg", [128, NT])
        cu = sb("cu", [128, NT])
        cd = sb("cd", [128, NT])
        silu = sb("silu", [128, 2, INNER])
        gw_sb = sb("gw_sb", [128, E])
        b1_sb = [sb(f"b1_{n}", [128, FC]) for n in range(2)]
        b2_sb = sb("b2_sb", [64, NT, D])
        w1_sb = [sb(f"w1_{n}", [128, INNER]) for n in range(2)]
        w2_sb = [sb(f"w2_{n}", [128, FC, D]) for n in range(2)]
        pr = sb("pr", [128, NT, E])
        pc = sb("pc", [128, NT, E])
        ph = sb("ph", [128, NT, E])
        pg = sb("pg", [128, NT, E])
        pm = sb("pm", [128, NT])
        pd = sb("pd", [128, NT])
        pgT = sb("pgT", [64, 128])

        ps = ctx.enter_context(nc.psum_tensor("ps", [128, 8, 512], F32))
        ps2 = ps[:, :, :].rearrange("p b n -> p (b n)")

        def bank4(k):
            return ps2[:, 512 * k:512 * k + 1024].rearrange("p (t d) -> p t d", t=NT)

        mixed = nc.dram_tensor("mixed", (B, H * S, DK), F32, kind="Internal").ap()

        block = ctx.enter_context(nc.Block())

        def bc(ap, n, shape):
            return ap.unsqueeze(n).broadcast_to(shape)

        @block.sync
        def _(sp):
            sp.dma_start(x[:], xh).then_inc(sem("x_in"), 16)
            sp.dma_start(ident[:], ident_in).then_inc(sem("x_in"), 16)
            sp.dma_start(wkv[:], wkv0).then_inc(sem("wkv_in"), 16)
            sp.dma_start(row[:], rows).then_inc(sem("setup_in"), 16)
            sp.dma_start(wq0_sb[:], wq0).then_inc(sem("setup_in"), 16)
            sp.dma_start(em[0:TK, :], m0).then_inc(sem("setup_in"), 16)
            sp.dma_start(hmask[:], hmask_in).then_inc(sem("setup_in"), 16)
            sp.dma_start(gate_sb[:], gates).then_inc(sem("setup_in"), 16)

            def load_ctx0(b, par, wait):
                if wait:
                    sp.wait_ge(sem("y_ready"), NG * (b - 1))
                sp.dma_start(cT[par][:], ctxT[:, bass.ds(b * S2, S2)]).then_inc(sem(f"ctx0_in{par}"), 16)

            def pair0(i):
                for par in range(2):
                    load_ctx0(2 * i + par, par, not (isinstance(i, int) and i == 0))

            pair0(0)
            with sp.Fori(1, B // 2) as i:
                pair0(i)
            for dst, src in ((dense_sb[:], dense0), (wgu[:, 0, :], wg0), (wgu[:, 1, :], wu0), (wdn[:], wd0),
                             (mi[0:TK, :], m1), (bq_sb[:], bq), (bk_sb[:], bk), (wq1_sb[:], wq1), (wk1_sb[:], wk1),
                             (wv1_sb[:], wv1), (wo1_sb[:], wo1), (den_sel[:], den_sel_in), (rank[:], rank_in),
                             (gw_sb[:], gatew), (b2_sb[:], b2)):
                sp.dma_start(dst, src).then_inc(sem("late_in"), 16)

            sp.wait_ge(sem("att0_ready"), 1)
            for b in range(B):
                r = HALF * (b % 2)
                sp.dma_start(mixed[b].rearrange("(h s) e -> s h e", h=H),
                             att[r:r + S, b // 2, :].rearrange("s (h e) -> s h e", h=H)).then_inc(sem("mix_out"), 16)
            sp.wait_ge(sem("mix_out"), 16 * B)
            for par in range(2):
                sp.dma_start(att[HALF * par:HALF * par + S, :, :],
                             mixed.rearrange("(i two) (s j) e -> two s i (j e)", two=2, s=S)[par]
                             ).then_inc(sem("mix_in"), 16)

            def pair1(i):
                for par in range(2):
                    b = 2 * i + par
                    if isinstance(i, int) and i == 0:
                        sp.wait_ge(sem("y_ready"), NG * (B - 1 + par))
                    else:
                        sp.wait_ge(sem("aux_free"), len(FULL) * (b - 2) + len(PREP))
                    sp.dma_start(cT[par][:], ctxT[:, bass.ds(b * S2, S2)]).then_inc(sem(f"ctx1_in{par}"), 16)

            pair1(0)
            with sp.Fori(1, B // 2) as i:
                pair1(i)

            def experts(i):
                for par in range(2):
                    e = 2 * i + par
                    if not (isinstance(i, int) and i == 0):
                        sp.wait_ge(sem("down_ready"), 2 * (e - 1))
                    sp.dma_start(w1_sb[par][:], w1[:, bass.ds(e * INNER, INNER)]).then_inc(sem(f"w1_in{par}"), 16)
                    sp.dma_start(b1_sb[par][:], b1[:, bass.ds(e * FC, FC)]).then_inc(sem(f"b1_in{par}"), 16)
                    sp.dma_start(w2_sb[par][:], w2[:, bass.ds(e * INNER, INNER)]).then_inc(sem(f"w2_in{par}"), 16)

            experts(0)
            with sp.Fori(1, E // 2) as i:
                experts(i)
            sp.wait_ge(sem("moe_done"), 2 * E)
            for par in range(2):
                sp.dma_start(out.rearrange("(i two) s d -> two s i d", two=2)[par],
                             x[HALF * par:HALF * par + S, :, :]).then_inc(sem("out_done"), 16)
            sp.wait_ge(sem("out_done"), 32)

        LATE = 15 * 16

        @block.tensor
        def _(pe):
            def transpose_tiles(src, bank, done):
                for t in range(NT):
                    ins = nc.tensor.transpose(bank4(bank)[:, t, :], src[:, t, :], ident[:])
                ins.then_inc(sem(done), 1)

            def project_tiles(lhs, w, bank, done):
                for t in range(NT):
                    ins = nc.tensor.matmul(bank4(bank)[:, t, :], lhs[:, 128 * t:128 * t + 128], w,
                                           start=True, stop=True)
                ins.then_inc(sem(done), 1)

            pe.wait_ge(sem("x_in"), 32)
            pe.wait_ge(sem("ln_done"), 1)
            transpose_tiles(xn, 0, "xT0_ps")
            pe.wait_ge(sem("xT0_ready"), 1)
            pe.wait_ge(sem("setup_in"), 80)
            project_tiles(xT, wq0_sb[:], 2, "q0_ps")
            pe.wait_ge(sem("q0_ready"), 1)
            transpose_tiles(t0, 4, "q0T_ps")

            def y_group(b, par, g, first):
                n = NG * b + g
                if g == 0:
                    pe.wait_ge(sem(f"ctx0_in{par}"), loads(b, par))
                if first:
                    if g == 0:
                        pe.wait_ge(sem("wkv_ready"), 1)
                        pe.wait_ge(sem("q0T_ready"), 1)
                else:
                    pe.wait_ge(sem("kn_ready"), n - 2)
                    pe.wait_ge(sem("vn_ready"), n - 2)
                for t in range(GT):
                    c0 = (GT * g + t) * TK
                    ins = nc.tensor.matmul(ps2[0:TK, 1024 * g + 256 * t:1024 * g + 256 * t + 256],
                                           cT[par][:, c0:c0 + TK], wkv[:].rearrange("p k d -> p (k d)"),
                                           start=True, stop=True)
                ins.then_inc(sem("y_ready"), 1)

            def kv_group(b, par, g, first):
                n = NG * b + g
                if g == 0 and not first:
                    pe.wait_ge(sem("kv_read"), b - 1)
                pe.wait_ge(sem("kp_ready"), n + 1)
                pe.wait_ge(sem("vn_ready"), n + 1)
                pe.wait_ge(sem("emc_ready"), n + 1)
                s6 = NG * par + g
                for t in range(GT):
                    ins = nc.tensor.matmul(ps[:, 6 + par, 0:D + 2], KN[0:TK, s6, t, :], VN[0:TK, s6, t, :],
                                           start=(g == 0 and t == 0), stop=(g == NG - 1 and t == GT - 1))
                ins.then_inc(sem("kv_done"), 1)

            pe.sem_inc(sem("kv_done"), SLOTS)
            for g in range(NG):
                y_group(0, 0, g, True)

            def pair(i):
                first = isinstance(i, int) and i == 0
                last = isinstance(i, int) and i == B // 2 - 1
                for g in range(NG):
                    y_group(2 * i + 1, 1, g, False)
                    kv_group(2 * i, 0, g, first)
                for g in range(NG):
                    if not last:
                        y_group(2 * i + 2, 0, g, False)
                    kv_group(2 * i + 1, 1, g, first)

            in_pairs(pe, pair, B // 2)

            pe.wait_ge(sem("kv_read"), B)
            for b in range(B):
                t, r = b // 2, HALF * (b % 2)
                ins = nc.tensor.matmul(ps[r:r + HALF, t // 3, KVW * (t % 3):KVW * (t % 3) + KVW],
                                       qT[:, HALF * b:HALF * b + HALF], kvall[:, b, :], start=True, stop=True)
            ins.then_inc(sem("nd_ready"), 1)
            pe.wait_ge(sem("mix_in"), 32)
            transpose_tiles(att, 4, "attT_ps")
            pe.wait_ge(sem("attT_ready"), 1)
            pe.wait_ge(sem("late_in"), LATE)
            project_tiles(xT, dense_sb[:], 6, "dense_ps")

            pe.wait_ge(sem("wabs_ready"), 1)
            nc.tensor.matmul(ps[:, 3, 0:3], onesf[:], wabs[:], start=True, stop=True).then_inc(sem("wsum_ps"), 1)
            pe.wait_ge(sem("kept_ready"), 1)
            nc.tensor.matmul(ps[:, 0, 0:B], onesf[0:TK, :], kept[0:TK, :], start=True,
                             stop=True).then_inc(sem("kept_ps"), 1)
            pe.wait_ge(sem("xq_ready"), 1)
            for t in range(NT):
                ins = nc.tensor.transpose(ps[:, 4, :].bitcast(BF16)[:, 128 * t:128 * t + 128], xqb[:, t, :], identb[:])
            ins.then_inc(sem("xqT_ps"), 1)
            pe.wait_ge(sem("xqT_ready"), 1)
            pe.wait_ge(sem("wq_ready"), 1)
            for t in range(NT):
                for k in range(2):
                    if t >= 2:
                        pe.wait_ge(sem("hid_ready"), t - 1)
                    ins = nc.tensor.matmul(ps[:, 2 * k + t % 2, :], xqT[:, 128 * t:128 * t + 128], wgub[:, k, :],
                                           start=True, stop=True)
                ins.then_inc(sem("gu_ps"), 1)
            for t in range(NT):
                pe.wait_ge(sem("hq_ready"), t + 1)
                if t >= 2:
                    pe.wait_ge(sem("hqT_ready"), t - 1)
                for c in range(FC):
                    ins = nc.tensor.transpose(ps[:, 4 + t % 2, :].bitcast(BF16)[:, 128 * c:128 * c + 128],
                                              hqb[:, t, 128 * c:128 * c + 128], identb[:])
                ins.then_inc(sem("hqT_ps"), 1)
            for t in range(NT):
                pe.wait_ge(sem("hqT_ready"), t + 1)
                for c in range(FC):
                    ins = nc.tensor.matmul(bank4(6)[:, t, :], hqT[:, t, c, :], wdnb[:, c, :],
                                           start=(c == 0), stop=(c == FC - 1), skip_group_check=True)
            ins.then_inc(sem("ffn_ps"), 1)

            pe.wait_ge(sem("ln_done"), 2)
            transpose_tiles(xn, 0, "xT1_ps")
            pe.wait_ge(sem("xT1_ready"), 1)
            for k in range(2):
                ins = nc.tensor.matmul(ps[:, 2 + k, :], wq1_sb[:], xT[:, 512 * k:512 * k + 512], start=True, stop=True)
            ins.then_inc(sem("q1_ps"), 1)

            def fill(w, unit, full, b, par):
                u = aux_at(w, unit, full)
                bank = 4 + (PREP if not full else ["DEN", "WO"] if isinstance(w, int) and w >= B - 1 else FULL
                            ).index(unit) % 2
                if not (isinstance(w, int) and w < 0 and unit in ("K0", "K1")):
                    pe.wait_ge(sem("aux_free"), u - 1)
                if unit[0] == "K":
                    k = int(unit[1])
                    if k == 0:
                        pe.wait_ge(sem(f"ctx1_in{par}"), loads(b, par))
                    ins = nc.tensor.matmul(ps[:, bank, 0:KCW], wk1_sb[:], cT[par][:, KCW * k:KCW * k + KCW],
                                           start=True, stop=True)
                elif unit[0] == "V":
                    g = int(unit[1])
                    for t in range(GT):
                        c0 = (GT * g + t) * TK
                        ins = nc.tensor.matmul(ps[0:TK, bank, 128 * t:128 * t + 128], cT[par][:, c0:c0 + TK],
                                               wv1_sb[:], start=True, stop=True)
                elif unit[:2] == "MX":
                    c, k = divmod(int(unit[2:]), KC)
                    if c == 0 and k == 0:
                        pe.wait_ge(sem("q_ready"), b + 1)
                        pe.wait_ge(sem("kb_copied"), b + 1)
                    q = Qb[par][:].rearrange("p h s -> p (h s)")
                    ins = nc.tensor.matmul(ps[:, bank, 0:KCW], q[:, 128 * c:128 * c + 128],
                                           Kb[par][:, KCW * k:KCW * k + KCW], start=True, stop=True)
                elif unit == "SH":
                    pe.wait_ge(sem("mneg_ready"), b + 1)
                    for c in range(CH):
                        for k in range(2):
                            lo, hi = max(128 * c, HQ2 * k), min(128 * c + 128, HQ2 * k + HQ2)
                            if lo < hi:
                                r = HALF - HALF * k
                                ins = nc.tensor.matmul(ps[r:r + 1, bank, lo - HQ2 * k:hi - HQ2 * k],
                                                       mneg[:, c:c + 1], identb[:, lo - 128 * c:hi - 128 * c],
                                                       start=True, stop=True)
                elif unit == "DEN":
                    pe.wait_ge(sem("o_ready"), b + 1)
                    ins = nc.tensor.matmul(ps[:, bank, 0:2 * PAIRW], den_sel[:], O[:], start=True, stop=True)
                else:
                    pe.wait_ge(sem("on_ready"), b + 1)
                    for c in range(2):
                        for k in range(2):
                            lhs = On[:, PAIRW * c + S * k:PAIRW * c + S * k + S]
                            ins = nc.tensor.matmul(ps[HALF * par:HALF * par + S, bank, 0:D], lhs,
                                                   wo1_sb[:, 2 * c + k, :], start=(c + k == 0), stop=(c + k == 2))
                ins.then_inc(sem("aux_ready"), 1)

            def scores(b, par, t, k, first):
                n = b * T + t
                if t == 0 and k == 0:
                    pe.wait_ge(sem("aux_free"), prepared(b))
                if k == 0 and not (first and t < 2):
                    pe.wait_ge(sem("p_ready"), n - 1)
                ins = nc.tensor.matmul(ps[0:TK, 2 * (t % 2) + k, 0:HQ2], KT[par][k][:, TK * t:TK * t + TK],
                                       QH[par][k][:].rearrange("p h s -> p (h s)"), start=True, stop=True)
                if k == 1:
                    ins.then_inc(sem("sc_ready"), 1)

            def weigh(b, par, t, first):
                n = b * T + t
                pe.wait_ge(sem("p_ready"), n + 1)
                if t == 0 and not first:
                    pe.wait_ge(sem("o_ready"), b - 1)
                for p in range(NPAIR):
                    r, c = PW * (p % 4), PAIRW * (p // 4)
                    ins = nc.tensor.matmul(ps[r:r + PW, 6 + par, c:c + PAIRW], Vp[par][0:TK, t, p, :],
                                           P[t % 2][0:TK, PAIRW * p:PAIRW * p + PAIRW],
                                           start=(t == 0 and p < 4), stop=(t == T - 1), skip_group_check=True)
                ins.then_inc(sem("pv_done"), 1)

            def window(b, par, first_pair, last):
                full = not (first_pair and par == 0)

                def unit_at(t, place):
                    unit = UNITS_AT[t][place]
                    if unit in ("DEN", "WO"):
                        if full:
                            fill(b, unit, full, b - 1, 1 - par)
                    elif unit and not last:
                        fill(b, unit, full, b + 1, 1 - par)

                for t in range(T):
                    scores(b, par, t, 0, first_pair and par == 0)
                    unit_at(t, 0)
                    scores(b, par, t, 1, first_pair and par == 0)
                    unit_at(t, 1)
                    if t > 0:
                        weigh(b, par, t - 1, first_pair)
                    elif full:
                        weigh(b - 1, 1 - par, T - 1, first_pair)
                    unit_at(t, 2)

            order = ["K0", "K1", None, "K2", None, "DEN", "V0", "V1", "V2", "WO"] + MXS
            order += [None] * (3 * (T - 1) - len(order)) + ["SH", None, None]
            UNITS_AT = [order[3 * t:3 * t + 3] for t in range(T)]
            pe.wait_ge(sem("q1T_ready"), 1)
            for unit in PREP:
                fill(-1, unit, False, 0, 0)

            def pair1(i):
                fixed = isinstance(i, int)
                window(2 * i, 0, fixed and i == 0, False)
                window(2 * i + 1, 1, fixed and i == 0, fixed and i == B // 2 - 1)

            in_pairs(pe, pair1, B // 2)
            weigh(B - 1, 1, T - 1, False)
            fill(B, "DEN", True, B - 1, 1)
            fill(B, "WO", True, B - 1, 1)

            pe.wait_ge(sem("ln_done"), 3)
            transpose_tiles(xn, 0, "xT2_ps")
            pe.wait_ge(sem("xT2_ready"), 1)
            for t in range(NT):
                ins = nc.tensor.matmul(ps[:, 2, E * t:E * t + E], xT[:, 128 * t:128 * t + 128], gw_sb[:],
                                       start=True, stop=True)
            ins.then_inc(sem("logit_ps"), 1)

            def up(e, par, first):
                pe.wait_ge(sem(f"w1_in{par}"), loads(e, par))
                xv = xT[:].rearrange("p (b q) -> p b q", q=HALF)
                for c in range(FC):
                    for k in range(2):
                        u = 2 * c + k
                        if not (first and u < 4):
                            pe.wait_ge(sem("h_ready"), 8 * e + u - 3)
                        nc.tensor.matmul(ps[:, u % 4, 0:8 * S], w1_sb[par][:, 128 * c:128 * c + 128],
                                         xv[:, 8 * k:8 * k + 8, 0:S], start=True, stop=True).then_inc(sem("up_ps"), 1)

            def down(e, par, first):
                pe.wait_ge(sem(f"w2_in{par}"), loads(e, par))
                pe.wait_ge(sem("h_ready"), 8 * e + 8)
                for k in range(2):
                    if not first:
                        pe.wait_ge(sem("moe_done"), 2 * e + k - 3)
                    for t in range(4):
                        for c in range(FC):
                            lhs = hT[:, par, c, 512 * k + 128 * t:512 * k + 128 * t + 128]
                            ins = nc.tensor.matmul(ps[:, 4 + 2 * par + k, 128 * t:128 * t + 128], lhs,
                                                   w2_sb[par][:, c, :], start=(c == 0), stop=(c == FC - 1),
                                                   skip_group_check=True)
                    ins.then_inc(sem("down_ready"), 1)

            pe.wait_ge(sem("pads_ready"), 1)
            pe.wait_ge(sem("pg_ready"), 1)
            nc.tensor.transpose(ps[0:64, 3, 0:128], pg[:].rearrange("p t e -> p (t e)"),
                                ident[:]).then_inc(sem("pgT_ps"), 1)
            pe.wait_ge(sem("pgT_ready"), 1)
            for k in range(2):
                ins = nc.tensor.matmul(ps[:, 4 + k, :], pgT[:], b2_sb[:, 4 * k:4 * k + 4, :], start=True, stop=True)
            ins.then_inc(sem("b2_ps"), 1)
            pe.wait_ge(sem("b2_done"), 1)
            up(0, 0, True)

            def pair2(i):
                fixed = isinstance(i, int)
                first, last = fixed and i == 0, fixed and i == E // 2 - 1
                up(2 * i + 1, 1, False)
                down(2 * i, 0, first)
                if not last:
                    up(2 * i + 2, 0, False)
                down(2 * i + 1, 1, first)

            in_pairs(pe, pair2, E // 2)

        @block.scalar
        def _(act):
            def ln_std(n, eps):
                act.wait_ge(sem("ln_var"), n)
                nc.scalar.activation(sd[:], mv[:, :, 1], ACT.Sqrt, bias=eps[:]).then_inc(sem("ln_std"), 1)

            act.wait_ge(sem("setup_done"), 1)
            act.wait_ge(sem("setup_in"), 80)
            nc.scalar.activation(th[:], gate_sb[:], ACT.Tanh).then_inc(sem("th_ready"), 1)
            ln_std(1, eps_ln)
            act.wait_ge(sem("xT0_ps"), 1)
            nc.scalar.copy(xT[:], ps2[:, 0:1024]).then_inc(sem("xT0_ready"), 1)
            ln_std(2, eps_in)
            act.wait_ge(sem("q0T_ps"), 1)
            nc.scalar.copy(qT[:], ps2[:, 2048:3072]).then_inc(sem("q0T_ready"), 1)

            def square(b, par, g, first_pair):
                n, k = NG * b + g, NG * par + g
                act.wait_ge(sem("y_ready"), n + 1)
                if not (first_pair and k < 2):
                    act.wait_ge(sem("ss_ready"), n - 1)
                nc.scalar.activation(SQ[0:TK, k % 2, :], ps2[0:TK, 1024 * g:1024 * g + 1024], ACT.Square,
                                     scale=float(D) ** -0.5).then_inc(sem("sq_ready"), 1)

            def deviation(n, k):
                act.wait_ge(sem("ss_ready"), n + 1)
                nc.scalar.activation(sdk[0:TK, k % 2, :], ss[0:TK, k % 2, :], ACT.Sqrt,
                                     bias=eps_in[0:TK, :]).then_inc(sem("sdk_ready"), 1)

            def values(n, k):
                act.wait_ge(sem("kn_ready"), n + 1)
                act.wait_ge(sem("kv_done"), n + 1)
                for t in range(GT):
                    c0 = 1024 * (k % NG) + 256 * t + D
                    ins = nc.scalar.activation(VN[0:TK, k, t, 0:D], ps2[0:TK, c0:c0 + D], ACT.Copy,
                                               scale=wv[0:TK, k % 2, t:t + 1])
                ins.then_inc(sem("vn_ready"), 1)

            def pair(i):
                first = isinstance(i, int) and i == 0
                for par in range(2):
                    for g in range(NG):
                        k = NG * par + g
                        n = NG * (2 * i + par) + g
                        square(2 * i + par, par, g, first)
                        if not (first and k < 1):
                            values(n - 1, (k - 1) % SLOTS)
                        deviation(n, k)

            in_pairs(act, pair, B // 2)
            values(NG * B - 1, SLOTS - 1)

            act.wait_ge(sem("attT_ps"), 1)
            nc.scalar.copy(xT[:], ps2[:, 2048:3072]).then_inc(sem("attT_ready"), 1)
            ln_std(3, eps_in)
            ln_std(4, eps_ln)
            act.wait_ge(sem("xqT_ps"), 1)
            nc.scalar.copy(xqT[:], ps[:, 4, :].bitcast(BF16)).then_inc(sem("xqT_ready"), 1)
            act.wait_ge(sem("cgu_ready"), 1)
            for t in range(NT):
                act.wait_ge(sem("gu_ps"), t + 1)
                if t >= 2:
                    act.wait_ge(sem("hid_ready"), t - 1)
                nc.scalar.activation(silu[:, t % 2, :], ps[:, t % 2, :], ACT.Silu,
                                     scale=cg[:, t:t + 1]).then_inc(sem("silu_ready"), 1)
            for t in range(NT):
                act.wait_ge(sem("hqT_ps"), t + 1)
                nc.scalar.copy(hqT[:, t, :, :].rearrange("p c n -> p (c n)"),
                               ps[:, 4 + t % 2, :].bitcast(BF16)[:, 0:INNER]).then_inc(sem("hqT_ready"), 1)
            ln_std(5, eps_ln)
            act.wait_ge(sem("xT1_ps"), 1)
            nc.scalar.copy(xT[:], ps2[:, 0:1024]).then_inc(sem("xT1_ready"), 1)
            act.wait_ge(sem("q1_ps"), 1)
            nc.scalar.activation(qT[:], ps2[:, 1024:2048], ACT.Identity, bias=bq_sb[:]).then_inc(sem("q1T_ready"), 1)

            def keys_copy(w, full, b, par):
                act.wait_ge(sem("aux_free"), aux_at(w, "K2", full) + 1)
                if not (isinstance(b, int) and b < 2):
                    act.wait_ge(sem("mneg_ready"), b - 1)
                for k in range(2):
                    rows = slice(HALF * k, HALF * k + HALF)
                    ins = nc.scalar.copy(Kb[par][rows, :], KT[par][k][rows, :])
                ins.then_inc(sem("kb_copied"), 1)

            def exponentials(b, par, t, first):
                n = b * T + t
                act.wait_ge(sem("sc_ready"), n + 1)
                if not (first and t < 2):
                    act.wait_ge(sem("pv_done"), n - 1)
                act.wait_ge(sem("kb_ready"), 1)
                src = ps[0:TK, 2 * (t % 2):2 * (t % 2) + 2, 0:HQ2]
                nc.scalar.activation(P[t % 2][0:TK, :].rearrange("p (k n) -> p k n", k=2), src, ACT.Exp,
                                     scale=kscale[0:TK, bass.ds(n, 1)],
                                     bias=kbias[0:TK, bass.ds(n, 1)]).then_inc(sem("p_ready"), 1)

            keys_copy(-1, False, 0, 0)

            def pair1(i):
                fixed = isinstance(i, int)
                for par in range(2):
                    first = fixed and i == 0 and par == 0
                    for t in range(T):
                        exponentials(2 * i + par, par, t, first)
                        if t == 1 and not (fixed and 2 * i + par == B - 1):
                            keys_copy(2 * i + par, not first, 2 * i + par + 1, 1 - par)

            in_pairs(act, pair1, B // 2)

            ln_std(6, eps_ln)
            act.wait_ge(sem("xT2_ps"), 1)
            nc.scalar.copy(xT[:], ps2[:, 0:1024]).then_inc(sem("xT2_ready"), 1)
            act.wait_ge(sem("logit_ready"), 1)
            nc.scalar.activation(pr[:], pr[:], ACT.Exp).then_inc(sem("pexp_ready"), 1)

            def inner(e, par, first_pair):
                act.wait_ge(sem(f"b1_in{par}"), loads(e, par))
                if first_pair and par == 0:
                    act.wait_ge(sem("pads_ready"), 1)
                for u in range(8):
                    c, k = divmod(u, 2)
                    act.wait_ge(sem("up_ps"), 8 * e + u + 1)
                    if u == 0 and not first_pair:
                        act.wait_ge(sem("down_ready"), 2 * (e - 1))
                    dst = hT[:, par, c, 512 * k:512 * k + 512].rearrange("p (b q) -> p b q", q=HALF)[:, :, 0:S]
                    nc.scalar.activation(dst, ps[:, u % 4, 0:8 * S].rearrange("p (b q) -> p b q", q=S),
                                         ACT.Gelu_apprx_tanh,
                                         bias=b1_sb[par][:, c:c + 1]).then_inc(sem("h_ready"), 1)

            def pair2(i):
                for par in range(2):
                    inner(2 * i + par, par, isinstance(i, int) and i == 0)

            in_pairs(act, pair2, E // 2)

        @block.gpsimd
        def _(pool):
            def keys(b, par, g, first):
                n, k = NG * b + g, NG * par + g
                pool.wait_ge(sem("kv_done"), n + 1)
                pool.wait_ge(sem("em_ready"), 1)
                nc.gpsimd.tensor_copy(VN[0:TK, k, :, D:D + 2],
                                      emcat[0:TK, bass.ds(b * T + GT * g, GT), :]).then_inc(sem("emc_ready"), 1)
                pool.wait_ge(sem("kn_ready"), n + 1)
                kn = KN[0:TK, k, :, :]
                nc.gpsimd.tensor_tensor(kn, kn, bc(row[0:TK, GAMMA, :], 1, [TK, GT, D]),
                                        ALU.mult).then_inc(sem("kg_ready"), 1)
                pool.wait_ge(sem("kg_ready"), n + 1)
                nc.gpsimd.tensor_tensor(kn, kn, bc(row[0:TK, BETA, :], 1, [TK, GT, D]),
                                        ALU.add).then_inc(sem("kb0_ready"), 1)

            def pair(i):
                for par in range(2):
                    for g in range(NG):
                        keys(2 * i + par, par, g, isinstance(i, int) and i == 0)

            in_pairs(pool, pair, B // 2)

            def prep(b, par, first_pair):
                if not first_pair:
                    pool.wait_ge(sem("sc_ready"), T * (b - 1))
                pool.wait_ge(sem("q1T_ready"), 1)
                for k in range(2):
                    rows = slice(HALF * k, HALF * k + HALF)
                    shape = [HALF, H // 2, S]
                    nc.gpsimd.tensor_tensor(QH[par][k][rows, :, :], bc(qT[rows, bass.ds(b * HALF, S)], 1, shape),
                                            bc(hmask[rows, H // 2 * k:H // 2 * k + H // 2], 2, shape), ALU.mult)
                    shape = [HALF, H, S]
                    ins = nc.gpsimd.tensor_tensor(Qb[par][rows, :, :], bc(qT[rows, bass.ds(b * HALF, S)], 1, shape),
                                                  bc(hmask[rows, :], 2, shape), ALU.mult)
                ins.then_inc(sem("q_ready"), 1)

            def pair1(i):
                for par in range(2):
                    prep(2 * i + par, par, isinstance(i, int) and i == 0)

            in_pairs(pool, pair1, B // 2)

        @block.vector
        def _(dve):
            v = nc.vector
            steps = [0]

            def step(ins):
                steps[0] += 1
                ins.then_inc(sem("dve_step"), 1)
                dve.wait_ge(sem("dve_step"), steps[0])

            def layernorm(n, src, dst, signal=None):
                for t in range(NT):
                    ins = v.bn_stats(stats[:, t, :], src[:, t, :])
                step(ins)
                for t in range(NT):
                    ins = v.bn_aggr(mv[:, t, :], stats[:, t, :])
                ins.then_inc(sem("ln_var"), 1)
                dve.wait_ge(sem("ln_std"), n)
                step(v.reciprocal(rstd[:], sd[:]))
                for t in range(NT):
                    ins = v.tensor_scalar(dst[:, t, :], src[:, t, :], mv[:, t, 0:1], rstd[:, t:t + 1],
                                          ALU.subtract, ALU.mult)
                if signal:
                    ins.then_inc(sem(signal), 1)
                else:
                    step(ins)

            def rows_of(k):
                return bc(row[:, k, :], 1, [128, NT, D])

            v.memset(onesf[:], 1.0)
            v.memset(eps_ln[:], EPS_LN)
            v.memset(eps_in[:], EPS_IN)
            for n in range(2):
                v.memset(Vp[n][:], 0.0)
            step(v.memset(att[:], 0.0))
            for n in range(2):
                v.memset(Vp[n][:, :, :, 0:1], 1.0)
            for n in range(2):
                for k in range(2):
                    data, spare = slice(HALF * k, HALF * k + HALF), slice(HALF - HALF * k, 128 - HALF * k)
                    v.memset(KT[n][k][spare, :], 1.0)
                    ins = v.memset(QH[n][k][spare, :, :], 0.0)
            ins.then_inc(sem("setup_done"), 1)

            dve.wait_ge(sem("x_in"), 32)
            layernorm(1, x, xn, "ln_done")
            step(v.tensor_copy(identb[:], ident[:]))
            dve.wait_ge(sem("wkv_in"), 16)
            step(v.tensor_reduce(wkv_mean[:], wkv[:], AX.X, ALU.add, negate=True))
            step(v.tensor_scalar(wkv_mean[:], wkv_mean[:], 1.0 / D, None, ALU.mult))
            for k in range(2):
                ins = v.tensor_scalar(wkv[:, k, :], wkv[:, k, :], wkv_mean[:, k:k + 1], None, ALU.add)
            ins.then_inc(sem("wkv_ready"), 1)
            dve.wait_ge(sem("setup_in"), 80)
            step(v.tensor_tensor(em2[0:TK, :], em[0:TK, :], em[0:TK, :], ALU.mult))
            v.tensor_copy(emcat[0:TK, :, 0], em2[0:TK, :])
            v.tensor_copy(emcat[0:TK, :, 1], em[0:TK, :]).then_inc(sem("em_ready"), 1)
            hm3 = bc(hmask[:], 2, [128, H, DK])
            v.tensor_tensor(gmask[:].rearrange("p (h d) -> p h d", h=H),
                            row[:, GAMMA, :].rearrange("p (h d) -> p h d", h=H), hm3, ALU.mult)
            step(v.tensor_tensor(bmask[:].rearrange("p (h d) -> p h d", h=H),
                                 row[:, BETA, :].rearrange("p (h d) -> p h d", h=H), hm3, ALU.mult))
            dve.wait_ge(sem("q0_ps"), 1)
            layernorm(2, bank4(2), t0)
            step(v.tensor_tensor(t0[:], t0[:], rows_of(GAMMA), ALU.mult))
            step(v.tensor_tensor(t0[:], t0[:], rows_of(BETA), ALU.add))
            v.tensor_scalar(t0[:], t0[:], 0.0, EPS_IN, ALU.max, ALU.add).then_inc(sem("q0_ready"), 1)

            def norms(n, k):
                dve.wait_ge(sem("sq_ready"), n + 1)
                v.tensor_reduce(ss[0:TK, k % 2, :], SQ[0:TK, k % 2, :].rearrange("p (j d) -> p j d", d=D),
                                AX.X, ALU.add).then_inc(sem("ss_ready"), 1)

            def keys(b, n, k, first_pair):
                g = k % NG
                dve.wait_ge(sem("sdk_ready"), n + 1)
                r = rk[0:TK, k % 2, :, :]
                v.reciprocal(r.rearrange("p t j -> p (t j)"), sdk[0:TK, k % 2, :]).then_inc(sem("rk_ready"), 1)
                dve.wait_ge(sem("rk_ready"), n + 1)
                if not (first_pair and k < 2):
                    dve.wait_ge(sem("vn_ready"), n - 1)
                v.tensor_tensor(wv[0:TK, k % 2, :], r[:, :, 1], em2[0:TK, bass.ds(b * T + GT * g, GT)],
                                ALU.mult)
                dve.wait_ge(sem("kv_done"), n + 1)
                y = ps2[0:TK, 1024 * g:1024 * g + 1024].rearrange("p (t n) -> p t n", t=GT)[:, :, 0:D]
                v.tensor_tensor(KN[0:TK, k, :, :], y, bc(r[:, :, 0], 2, [TK, GT, D]),
                                ALU.mult).then_inc(sem("kn_ready"), 1)

            def relu(n, k):
                dve.wait_ge(sem("kb0_ready"), n + 1)
                kn = KN[0:TK, k, :, :]
                v.tensor_scalar(kn, kn, 0.0, EPS_IN, ALU.max, ALU.add).then_inc(sem("kp_ready"), 1)

            def state(b, par):
                dve.wait_ge(sem("kv_done"), NG * (b + 1) + SLOTS)
                kv = ps[:, 6 + par, :]
                v.tensor_tensor(kvtmp[:, par, :], kv[:, 0:D], gmask[:], ALU.mult).then_inc(sem("kvt_ready"), 1)
                v.tensor_scalar(kvall[:, bass.ds(b, 1), D:KVW], hmask[:].unsqueeze(1), kv[:, D + 1:D + 2], None,
                                ALU.mult)
                dve.wait_ge(sem("kvt_ready"), b + 1)
                v.scalar_tensor_tensor(kvall[:, bass.ds(b, 1), 0:D], bmask[:].unsqueeze(1), kv[:, D:D + 1],
                                       kvtmp[:, par, :].unsqueeze(1), ALU.mult, ALU.add).then_inc(sem("kv_read"), 1)

            def pair(i):
                first = isinstance(i, int) and i == 0
                for par in range(2):
                    b = 2 * i + par
                    for g in range(NG):
                        n, k = NG * b + g, NG * par + g
                        norms(n, k)
                        if not (first and k < 2):
                            relu(n - 2, (k - 2) % SLOTS)
                        if g == 0 and not first:
                            state(b - 2, par)
                        keys(b, n, k, first)

            in_pairs(dve, pair, B // 2)
            last = NG * B - 1
            relu(last - 1, SLOTS - 2)
            relu(last, SLOTS - 1)
            state(B - 2, 0)
            state(B - 1, 1)

            dve.wait_ge(sem("nd_ready"), 1)

            def nd(t):
                return ps[:, t // 3, KVW * (t % 3):KVW * (t % 3) + KVW]

        
            for t in range(NT):
                ins = v.tensor_scalar(xn[:, t, 0:H], nd(t)[:, D:KVW], EPS_IN, None, ALU.add)
            step(ins)
            step(v.reciprocal(xn[:, :, H:2 * H], xn[:, :, 0:H]))
            for t in range(NT):
                ins = v.tensor_tensor(att[:, t, :].rearrange("p (h d) -> p h d", h=H),
                                      nd(t)[:, 0:D].rearrange("p (h d) -> p h d", h=H),
                                      bc(xn[:, t, H:2 * H], 2, [128, H, DK]), ALU.mult)
            ins.then_inc(sem("att0_ready"), 1)
            dve.wait_ge(sem("late_in"), LATE)
            v.tensor_reduce(wabs[:, 0:2], wgu[:], AX.X, ALU.add, apply_absolute_value=True)
            v.tensor_reduce(wabs[:, 2:3], wdn[:].rearrange("p c n -> p (c n)"), AX.X, ALU.add,
                            apply_absolute_value=True).then_inc(sem("wabs_ready"), 1)
            step(v.tensor_scalar(keep[0:TK, :], mi[0:TK, :], 0.0, None, ALU.not_equal))
            v.tensor_reduce(kept[0:TK, :], keep[0:TK, :].rearrange("p (b t) -> p b t", b=B), AX.X,
                            ALU.max).then_inc(sem("kept_ready"), 1)
            dve.wait_ge(sem("kept_ps"), 1)
            step(v.tensor_scalar(anykept[:], ps[:, 0, 0:B], 0.0, 1e9, ALU.is_gt, ALU.mult))
            v.tensor_scalar(kscale[0:TK, :], keep[0:TK, :], SCALE, None, ALU.mult)
            step(v.tensor_scalar(keep[0:TK, :], keep[0:TK, :], 1.0, None, ALU.subtract))
            v.tensor_tensor(kbias[0:TK, :].rearrange("p (b t) -> p b t", b=B),
                            keep[0:TK, :].rearrange("p (b t) -> p b t", b=B),
                            bc(anykept[0:TK, :], 2, [TK, B, T]), ALU.mult).then_inc(sem("kb_ready"), 1)
            dve.wait_ge(sem("wsum_ps"), 1)
            step(v.tensor_scalar(wmean[:], ps[:, 3, 0:3], 1.0 / (INNER * D), 1e-5, ALU.mult, ALU.max))
            step(v.reciprocal(wscale[:], wmean[:]))
            for k in range(2):
                v.tensor_scalar(wgu[:, k, :], wgu[:, k, :], wscale[:, k:k + 1], ROUND, ALU.mult, ALU.add)
            step(v.tensor_scalar(wdn[:], wdn[:], wscale[:, 2:3], ROUND, ALU.mult, ALU.add))
            v.tensor_scalar(wgu[:], wgu[:], ROUND, -1.0, ALU.subtract, ALU.max)
            step(v.tensor_scalar(wdn[:], wdn[:], ROUND, -1.0, ALU.subtract, ALU.max))
            v.tensor_scalar(wgub[:], wgu[:], 1.0, None, ALU.min)
            v.tensor_scalar(wdnb[:], wdn[:], 1.0, None, ALU.min).then_inc(sem("wq_ready"), 1)

            dve.wait_ge(sem("dense_ps"), 1)
            step(v.tensor_tensor(t0[:], bank4(6), rows_of(DENSE_B), ALU.add))
            layernorm(3, t0, t0)
            step(v.tensor_tensor(t0[:], t0[:], rows_of(GAMMA), ALU.mult))
            step(v.tensor_tensor(t0[:], t0[:], rows_of(BETA), ALU.add))
            dve.wait_ge(sem("th_ready"), 1)
            step(v.scalar_tensor_tensor(x[:], t0[:], th[:, 0:1], x[:], ALU.mult, ALU.add))

            def quantise(src, dst, n0, n1, scratch, signal):
                a = amax[:, n0:n1]
                step(v.tensor_reduce(a, src, AX.X, ALU.max, apply_absolute_value=True))
                step(v.tensor_scalar(a, a, 1e-5, None, ALU.max))
                step(v.reciprocal(qs[:, n0:n1], a))
                step(v.tensor_scalar(qs[:, n0:n1], qs[:, n0:n1], 127.0, None, ALU.mult))
                v.tensor_scalar(a, a, 1.0 / 127.0, None, ALU.mult)
                for t in range(n0, n1):
                    ins = v.tensor_scalar(scratch[:, t - n0, :], src[:, t - n0, :], qs[:, t:t + 1], ROUND,
                                          ALU.mult, ALU.add)
                step(ins)
                step(v.tensor_scalar(scratch, scratch, ROUND, -128.0, ALU.subtract, ALU.max))
                v.tensor_scalar(dst, scratch, 127.0, None, ALU.min).then_inc(sem(signal), 1)

            layernorm(4, x, xn)
            quantise(xn[:], xqb[:], 0, NT, t0[:], "xq_ready")
            dve.wait_ge(sem("xq_ready"), 1)
            v.tensor_scalar(cg[:], amax[:], wmean[:, 0:1], None, ALU.mult)
            v.tensor_scalar(cu[:], amax[:], wmean[:, 1:2], None, ALU.mult).then_inc(sem("cgu_ready"), 1)
            for t in range(NT):
                dve.wait_ge(sem("silu_ready"), t + 1)
                v.scalar_tensor_tensor(hid[:, t, :], ps[:, 2 + t % 2, :], cu[:, t:t + 1], silu[:, t % 2, :],
                                       ALU.mult, ALU.mult).then_inc(sem("hid_ready"), 1)
            dve.wait_ge(sem("hid_ready"), NT)
            for t in range(NT):
                quantise(hid[:, t:t + 1, :], hqb[:, t:t + 1, :], t, t + 1, hid[:, t:t + 1, :], "hq_ready")
            step(v.tensor_scalar(cd[:], amax[:], wmean[:, 2:3], th[:, 2:3], ALU.mult, ALU.mult))
            dve.wait_ge(sem("ffn_ps"), 1)
            for t in range(NT):
                ins = v.scalar_tensor_tensor(x[:, t, :], bank4(6)[:, t, :], cd[:, t:t + 1], x[:, t, :],
                                             ALU.mult, ALU.add)
            step(ins)
            layernorm(5, x, xn, "ln_done")

            def empty(w, unit, full, b, par):
                u = aux_at(w, unit, full)
                bank = 4 + (PREP if not full else ["DEN", "WO"] if isinstance(w, int) and w >= B - 1 else FULL
                            ).index(unit) % 2
                dve.wait_ge(sem("aux_ready"), u + 1)
                early = isinstance(b, int) and b < 2
                if unit[0] == "K":
                    k = int(unit[1])
                    if k == 0 and not early:
                        dve.wait_ge(sem("sc_ready"), T * (b - 1))
                    for j in range(2):
                        rows = slice(HALF * j, HALF * j + HALF)
                        ins = v.tensor_scalar(KT[par][j][rows, KCW * k:KCW * k + KCW], ps[rows, bank, 0:KCW],
                                              bk_sb[rows, :], None, ALU.add)
                elif unit[0] == "V":
                    g = int(unit[1])
                    if g == 0 and not early:
                        dve.wait_ge(sem("pv_done"), T * (b - 1))
                    dst = Vp[par][0:TK, GT * g:GT * g + GT, :, 1:1 + 2 * DK]
                    src = ps[0:TK, bank, :].rearrange("p (t j d) -> p t j d", t=GT, j=NPAIR)
                    bias = bc(row[0:TK, B_V, :].rearrange("p (j d) -> p j d", j=NPAIR), 1, [TK, GT, NPAIR, 2 * DK])
                    ins = v.tensor_tensor(dst, src, bias, ALU.add)
                elif unit[:2] == "MX":
                    c, k = divmod(int(unit[2:]), KC)
                    ins = v.tensor_reduce(mx[:, c, k:k + 1], ps[:, bank, 0:KCW], AX.X, ALU.max)
                elif unit == "SH":
                    for k in range(2):
                        r = HALF - HALF * k
                        ins = v.tensor_copy(QH[par][k][r:r + 1, :, :].rearrange("p h s -> p (h s)"),
                                            ps[r:r + 1, bank, 0:HQ2])
                elif unit == "DEN":
                    ins = v.reciprocal(rden[:], ps[:, bank, 0:2 * PAIRW])
                else:
                    dst = att[HALF * par:HALF * par + S, bass.ds(TILE_OF(b, par), 1), :]
                    ins = v.tensor_copy(dst, ps[HALF * par:HALF * par + S, bank, 0:D].unsqueeze(1))
                ins.then_inc(sem("aux_free"), 1)
                if unit == "DEN":
                    dve.wait_ge(sem("aux_free"), u + 1)
                    v.tensor_tensor(On[:], O[:], rden[:], ALU.mult).then_inc(sem("on_ready"), 1)

            def TILE_OF(b, par):
                return b // 2

            def take_sums(b, par):
                dve.wait_ge(sem("pv_done"), T * (b + 1))
                v.tensor_copy(O[:], ps[:, 6 + par, 0:2 * PAIRW]).then_inc(sem("o_ready"), 1)

            def maxima(w, full):
                dve.wait_ge(sem("aux_free"), aux_at(w, MXS[-1], full) + 1)
                v.tensor_reduce(mneg[:], mx[:], AX.X, ALU.max, negate=True).then_inc(sem("mneg_ready"), 1)

            for unit in PREP:
                if unit == "SH":
                    maxima(-1, False)
                empty(-1, unit, False, 0, 0)

            def pair1(i):
                fixed = isinstance(i, int)
                for par in range(2):
                    w = 2 * i + par
                    full = not (fixed and w == 0)
                    last = fixed and w == B - 1
                    if full:
                        take_sums(w - 1, 1 - par)
                    for unit in (["DEN", "WO"] if last else FULL if full else PREP):
                        if unit in ("DEN", "WO"):
                            empty(w, unit, full, w - 1, 1 - par)
                        else:
                            if unit == "SH":
                                maxima(w, full)
                            empty(w, unit, full, w + 1, 1 - par)

            in_pairs(dve, pair1, B // 2)
            take_sums(B - 1, 1)
            empty(B, "DEN", True, B - 1, 1)
            empty(B, "WO", True, B - 1, 1)
            dve.wait_ge(sem("aux_free"), aux_at(B, "WO", True) + 1)
            step(v.tensor_tensor(att[:], att[:], rows_of(B_O), ALU.add))
            step(v.scalar_tensor_tensor(x[:], att[:], th[:, 1:2], x[:], ALU.mult, ALU.add))

            layernorm(6, x, xn, "ln_done")
            v.memset(hT[:, :, :, :].rearrange("p s c (b q) -> p (s c b) q", q=HALF)[:, :, S:HALF],
                     0.0).then_inc(sem("pads_ready"), 1)
            dve.wait_ge(sem("logit_ps"), 1)
            lg = ps[:, 2, 0:NT * E].rearrange("p (t e) -> p t e", e=E)
            full3 = [128, NT, E]
            step(v.tensor_reduce(pm[:], lg, AX.X, ALU.max))
            v.tensor_tensor(pr[:], lg, bc(pm[:], 2, full3), ALU.subtract).then_inc(sem("logit_ready"), 1)
            dve.wait_ge(sem("pexp_ready"), 1)
            step(v.tensor_reduce(pd[:], pr[:], AX.X, ALU.add))
            step(v.reciprocal(pd[:], pd[:]))
            step(v.tensor_tensor(pr[:], pr[:], bc(pd[:], 2, full3), ALU.mult))
            step(v.tensor_copy(pc[:], pr[:]))
            for k in range(2):
                step(v.tensor_reduce(pm[:], pc[:], AX.X, ALU.max))
                step(v.tensor_tensor(ph[:], pc[:], bc(pm[:], 2, full3), ALU.is_equal))
                step(v.tensor_tensor(ph[:], ph[:], rank[:], ALU.mult))
                step(v.tensor_reduce(pm[:], ph[:], AX.X, ALU.max))
                step(v.tensor_tensor(ph[:], rank[:], bc(pm[:], 2, full3), ALU.is_equal))
                if k == 0:
                    step(v.tensor_copy(pg[:], ph[:]))
                    step(v.scalar_tensor_tensor(pc[:], ph[:], -2.0, pc[:], ALU.mult, ALU.add))
            step(v.tensor_tensor(pg[:], pg[:], ph[:], ALU.add))
            step(v.tensor_tensor(pg[:], pg[:], pr[:], ALU.mult))
            v.tensor_scalar(pg[:], pg[:], th[:, 3:4], None, ALU.mult).then_inc(sem("pg_ready"), 1)
            dve.wait_ge(sem("pgT_ps"), 1)
            v.tensor_copy(pgT[:], ps[0:64, 3, 0:128]).then_inc(sem("pgT_ready"), 1)
            dve.wait_ge(sem("b2_ps"), 1)
            v.tensor_tensor(x[:], x[:], bank4(4), ALU.add).then_inc(sem("b2_done"), 1)

            def add_expert(e, par, first_pair):
                for k in range(2):
                    dve.wait_ge(sem("down_ready"), 2 * e + k + 1)
                    if first_pair and par == 0:
                        dve.wait_ge(sem("b2_done"), 1)
                    else:
                        dve.wait_ge(sem("moe_done"), 2 * e + k - 1)
                    for t in range(4):
                        ins = v.scalar_tensor_tensor(x[:, 4 * k + t, :], ps[:, 4 + 2 * par + k, 128 * t:128 * t + 128],
                                                     pg[:, 4 * k + t, bass.ds(e, 1)], x[:, 4 * k + t, :],
                                                     ALU.mult, ALU.add)
                    ins.then_inc(sem("moe_done"), 1)

            def pair2(i):
                for par in range(2):
                    add_expert(2 * i + par, par, isinstance(i, int) and i == 0)

            in_pairs(dve, pair2, E // 2)


def _layout(v):
    import numpy as np
    f = np.float32
    xh = np.zeros((128, NT, D), f)
    x4 = v["x"].reshape(NT, 2, S, D)
    xh[0:S] = x4[:, 0].transpose(1, 0, 2)
    xh[HALF:HALF + S] = x4[:, 1].transpose(1, 0, 2)

    def rep(a):
        return np.broadcast_to(a, (128,) + a.shape)

    wo = np.zeros((4, PW, 2, 2, D), f)
    woT = v["L1_xattn_W_o"].T.reshape(2, 4, 2, DK, D)
    for k in range(2):
        wo[:, 1 + DK * k:1 + DK * k + DK, :, k, :] = woT[:, :, k].transpose(1, 2, 0, 3)
    b2 = np.zeros((NT, E, NT, D), f)
    for t in range(NT):
        b2[t, :, t] = v["L1_ffn_b2"]
    sel = np.zeros((128, 128), f)
    for j in range(4):
        sel[PW * j, PW * j:PW * j + PW] = 1.0
    mask = lambda m: m.reshape(B, T, TK).transpose(2, 0, 1).reshape(TK, B * T)
    return {
        "xh": xh,
        "ctxT": v["ctx_1024"].reshape(B * S2, D).T,
        "m0": mask(v["mask_BxS2_ff1"]),
        "m1": mask(v["mask_BxS2_if1"]),
        "gates": rep(np.concatenate([v["g_xattn"], v["g_ffn"]])),
        "rows": rep(np.stack([v["L0_xattn_ln_gamma"], v["L0_xattn_ln_beta"], v["L0_xattn_dense_b"],
                              v["L1_xattn_b_v"], v["L1_xattn_b_o"]])),
        "bq": v["L1_xattn_b_q"].reshape(D, 1),
        "bk": v["L1_xattn_b_k"].reshape(D, 1),
        "wkv0": np.stack([v["L0_xattn_wk"], v["L0_xattn_wv"]], axis=1),
        "wq0": v["L0_xattn_wq"],
        "dense0": v["L0_xattn_dense_w"],
        "wg0": v["L0_ffn_w_gate"].T,
        "wu0": v["L0_ffn_w_up"].T,
        "wd0": v["L0_ffn_w_down"].T.reshape(FC, 128, D).transpose(1, 0, 2),
        "wq1": v["L1_xattn_W_q"].T,
        "wk1": v["L1_xattn_W_k"].T,
        "wv1": v["L1_xattn_W_v"].T,
        "wo1": wo.reshape(128, 4, D),
        "gatew": v["L1_ffn_gate_w"].T,
        "w1": v["L1_ffn_w1"].transpose(2, 1, 0).reshape(D, E * INNER),
        "b1": v["L1_ffn_b1"].reshape(E * FC, 128).T,
        "w2": v["L1_ffn_w2"].transpose(1, 2, 0).reshape(E, FC, 128, D).transpose(2, 0, 1, 3).reshape(128, E * INNER),
        "b2": b2.reshape(NT * E, NT, D),
        "ident_in": np.eye(128, dtype=f),
        "hmask_in": np.repeat(np.eye(H, dtype=f), DK, axis=0),
        "den_sel_in": sel,
        "rank_in": np.broadcast_to(np.arange(E, 0, -1).astype(f), (128, NT, E)),
    }


def kernel(**inputs):
    import numpy as np
    import concourse.bacc as bacc
    from concourse.bass_utils import run_bass_kernel_spmd

    laid = {n: np.ascontiguousarray(a) for n, a in _layout({k: np.asarray(a) for k, a in inputs.items()}).items()}
    nc = bacc.Bacc("TRN2", target_bir_lowering=False, num_devices=1)
    args = {n: nc.dram_tensor(n + "_dram", a.shape, mybir.dt.from_np(a.dtype), kind="ExternalInput").ap()
            for n, a in laid.items()}
    out = nc.dram_tensor("out_dram", (B, S, D), F32, kind="ExternalOutput").ap()
    build(nc, out=out, **args)
    r = run_bass_kernel_spmd(nc, [{n + "_dram": a for n, a in laid.items()}], core_ids=[0])
    return r.results[0]["out_dram"]
```

```python
from contextlib import ExitStack

import concourse.bass as bass
from concourse import mybir

ALU = mybir.AluOpType
ACT = mybir.ActivationFunctionType
AX = mybir.AxisListType
F32 = mybir.dt.float32
BF16 = mybir.dt.bfloat16
I32 = mybir.dt.int32

B, S, D = 16, 56, 128
S2 = 1500
H, DK = 16, 8
T, TK = 12, 125
GT, NG = 4, 3
NT = B // 2
HALF = 64
COLS = NT * 128
INNER = 512
FC = INNER // 128
E = 8
HQ = H * S
HQ2 = HQ // 2
CH = HQ // 128
KC = 3
KCW = S2 // KC
PAIRW = 2 * S
PW = 32
NPAIR = H // 2
SLOTS = 2 * NG
KVW = D + H
EPS_LN, EPS_IN = 1e-5, 1e-6
ROUND = 12582912.0
SCALE = 1.0 / float(DK) ** 0.5

KEY_PART = (0, 0, 0, 1, 1, 2)
QUERY_PART = (0, 1, 2, 0, 1, 0)
STACK = len(KEY_PART)
ROWS = 2 * DK
ONES = STACK * ROWS
KSW = NPAIR * S2 + 128 - TK

MXS = [f"MX{n}" for n in range(CH * KC)]
PLACES = [["MX0", "MX1", "V0"], ["MX2", "DEN", None], [None, "MX3", "V1"], ["MX4", "MX5", "V2"],
          ["WO", "MX6", "K0"], ["MX7", "MX8", "MX9"], ["MX10", "MX11", "K1"], ["MX12", "MX13", "MX14"],
          ["MX15", "MX16", "K2"], ["MX17", "MX18", "MX19"], ["MX20", None, None], ["SH", None, None]]
ALL = [u for places in PLACES for u in places if u]
ENDS = ["DEN", "WO"]
EARLY = ["K0", "K1", "K2", "K0'", "K1'", "K2'", "V0", "V1", "V2"]


REST_LATER = 3


def kind(unit):
    return "side" if unit[0] in "KV" else "aux"


def units(w, of=None):
    if not isinstance(w, int):
        now = ALL
    elif w < 0:
        now = EARLY + MXS + ["SH"]
    elif w >= B - 1:
        now = ENDS
    else:
        now = [u for u in ALL if not (w == 0 and u in ENDS) and not (w == B - 2 and u[0] == "K")]
    return [u for u in now if of is None or kind(u) == of]


def count_at(w, unit):
    k = kind(unit)
    n = units(w, k).index(unit)
    if isinstance(w, int):
        return 0, n + sum(len(units(j, k)) for j in range(-1, w))
    each = len(units(w, k))
    return each, n + len(units(-1, k)) + len(units(0, k)) - each


def filled(w, unit):
    m, c = count_at(w, unit)
    return c + 1 if m == 0 else w * m + (c + 1)


def bank_of(w, unit):
    return 6 if kind(unit) == "side" else 4 + count_at(w, unit)[1] % 2


def free_of(w, unit):
    return "side_free" if kind(unit) == "side" else f"aux_free{bank_of(w, unit)}"


def emptied(w, unit):
    m, c = count_at(w, unit)
    if kind(unit) == "aux":
        m, c = m // 2, c // 2
    return c + 1 if m == 0 else w * m + (c + 1)


def loads(b, par, n=1):
    return 8 * n * b + (16 - 8 * par) * n


def in_pairs(eng, body, pairs):
    body(0)
    with eng.Fori(1, pairs - 1) as i:
        body(i)
    body(pairs - 1)


def build(nc, xh, ctxT, m0, m1, gates, rows, bq, bk, wkv0, wq0, dense0, wg0, wu0, wd0, wq1, wk1, wv1, wo1,
          gatew, w1, b1, w2, b2, bv, ident_in, hmask_in, hmask1_in, pmask_in,
          den_sel_in, rank_in, out):
    with ExitStack() as ctx:
        def sb(name, shape, dt=F32):
            return ctx.enter_context(nc.sbuf_tensor(name, shape, dt))

        sems = {}

        def sem(name):
            if name not in sems:
                sems[name] = ctx.enter_context(nc.semaphore(name))
            return sems[name]

        x = sb("x", [128, NT, D])
        xn = sb("xn", [128, NT, D])
        t0 = sb("t0", [128, NT, D])
        att = sb("att", [128, NT, D])
        xT = sb("xT", [128, COLS])
        qT = sb("qT", [128, COLS])
        stats = sb("stats", [128, NT, 6])
        mv = sb("mv", [128, NT, 2])
        sd = sb("sd", [128, NT])
        rstd = sb("rstd", [128, NT])
        ident = sb("ident", [128, 128])
        identb = sb("identb", [128, 128], BF16)
        onesf = sb("onesf", [128, 128])
        hmask = sb("hmask", [128, H])
        hmask1 = sb("hmask1", [128, H])
        pmask = sb("pmask", [128, 2])
        bv_sb = sb("bv_sb", [128, 2])
        den_sel = sb("den_sel", [128, 128])
        rank = sb("rank", [128, NT, E])
        eps_ln = sb("eps_ln", [128, 1])
        eps_in = sb("eps_in", [128, 1])
        gate_sb = sb("gate_sb", [128, 4])
        th = sb("th", [128, 4])
        row = sb("row", [128, 4, D])
        GAMMA, BETA, DENSE_B, B_O = range(4)
        gmask = sb("gmask", [128, D])
        bmask = sb("bmask", [128, D])
        wkv = sb("wkv", [128, 2, D])
        wkv_mean = sb("wkv_mean", [128, 2])
        wq0_sb = sb("wq0_sb", [128, D])
        dense_sb = sb("dense_sb", [128, D])
        bq_sb = sb("bq_sb", [128, 1])
        bk_sb = sb("bk_sb", [128, 1])
        wq1_sb = sb("wq1_sb", [128, D])
        wk1_sb = sb("wk1_sb", [128, D])
        wv1_sb = sb("wv1_sb", [128, D])
        wo1_sb = sb("wo1_sb", [128, 4, D])
        em = sb("em", [128, B * T])
        em2 = sb("em2", [128, B * T])
        emcat = sb("emcat", [128, B * T, 2])
        mi = sb("mi", [128, B * T], I32)
        keep = sb("keep", [128, B * T])
        kscale = sb("kscale", [128, B * T])
        kbias = sb("kbias", [128, B * T])
        kept = sb("kept", [128, B])
        anykept = sb("anykept", [128, B])
        cT = [sb(f"cT{n}", [128, S2]) for n in range(2)]
        kvall = sb("kvall", [128, B, KVW])
        kvtmp = sb("kvtmp", [128, 2, D])
        ss = sb("ss", [128, 2, 2 * GT])
        sdk = sb("sdk", [128, 2, 2 * GT])
        rk = sb("rk", [128, 2, GT, 2])
        wv = sb("wv", [128, 2, GT])
        arena = sb("arena", [128, 8240])
        KN = arena[:, 0:3072].rearrange("p (s t d) -> p s t d", s=6, t=GT)
        VN = arena[:, 3072:6192].rearrange("p (s t d) -> p s t d", s=6, t=GT)
        SQ = arena[:, 6192:8240].rearrange("p (s n) -> p s n", s=2)
        hid = arena[:, 0:4096].rearrange("p (t n) -> p t n", t=NT)
        hqb = arena[:, 4096:6144].bitcast(BF16).rearrange("p (t n) -> p t n", t=NT)
        hqT = arena[:, 6144:8192].bitcast(BF16).rearrange("p (t c n) -> p t c n", t=NT, c=FC)
        hT = arena[:, 0:8192].rearrange("p (s c n) -> p s c n", s=2, c=FC)
        wgu = sb("wgu", [128, 2, INNER])
        wdn = sb("wdn", [128, FC, D])
        wgub = sb("wgub", [128, 2, INNER], BF16)
        wdnb = sb("wdnb", [128, FC, D], BF16)
        wabs = sb("wabs", [128, 3])
        wmean = sb("wmean", [128, 3])
        wscale = sb("wscale", [128, 3])
        xqb = sb("xqb", [128, NT, D], BF16)
        xqT = sb("xqT", [128, COLS], BF16)
        amax = sb("amax", [128, NT])
        qs = sb("qs", [128, NT])
        cg = sb("cg", [128, NT])
        cu = sb("cu", [128, NT])
        cd = sb("cd", [128, NT])
        silu = sb("silu", [128, 2, INNER])
        KP = [[sb(f"KP{n}_{k}", [128, S2], BF16) for k in range(3)] for n in range(2)]
        krest = kvall[:, :, :].rearrange("p b n -> p (b n)")[:, 0:S2]
        QP = [wgub[:].rearrange("p k n -> p (k n)"), xqb[:].rearrange("p t d -> p (t d)"), xqT[:]]
        QD = [[sb(f"QD{n}_{k}", [128, 2, S], BF16) for k in range(3)] for n in range(2)]
        KS = [sb("KS0", [128, KSW], BF16)[:], arena[:, 0:KSW // 2 + 1].bitcast(BF16)[:, 0:KSW]]
        QS = [sb(f"QS{n}", [128, HQ], BF16) for n in range(2)]
        Qb = [sb(f"Qb{n}", [128, H, S], BF16) for n in range(2)]
        Vp = [sb(f"Vp{n}", [128, T, NPAIR, PW]) for n in range(2)]
        P = [sb(f"P{n}", [128, HQ]) for n in range(2)]
        mx = sb("mx", [128, CH, KC])
        mneg = sb("mneg", [128, CH], BF16)
        O = sb("O", [128, 2 * PAIRW])
        rden = sb("rden", [128, 2 * PAIRW])
        On = sb("On", [128, 2 * PAIRW])
        gw_sb = sb("gw_sb", [128, E])
        b1_sb = [sb(f"b1_{n}", [128, FC]) for n in range(2)]
        b2_sb = sb("b2_sb", [64, NT, D])
        w1_sb = [wgu[:, n, :] for n in range(2)]
        w2_sb = [silu[:, n, :].rearrange("p (c d) -> p c d", c=FC) for n in range(2)]
        pr = sb("pr", [128, NT, E])
        pc = sb("pc", [128, NT, E])
        ph = sb("ph", [128, NT, E])
        pg = sb("pg", [128, NT, E])
        pm = sb("pm", [128, NT])
        pd = sb("pd", [128, NT])
        pgT = sb("pgT", [64, 128])

        ps = ctx.enter_context(nc.psum_tensor("ps", [128, 8, 512], F32))
        ps2 = ps[:, :, :].rearrange("p b n -> p (b n)")

        def bank4(k):
            return ps2[:, 512 * k:512 * k + 1024].rearrange("p (t d) -> p t d", t=NT)

        mixed = nc.dram_tensor("mixed", (B, H * S, DK), F32, kind="Internal").ap()

        block = ctx.enter_context(nc.Block())

        def bc(ap, n, shape):
            return ap.unsqueeze(n).broadcast_to(shape)

        @block.sync
        def _(sp):
            sp.dma_start(x[:], xh).then_inc(sem("x_in"), 16)
            sp.dma_start(ident[:], ident_in).then_inc(sem("x_in"), 16)
            sp.dma_start(wkv[:], wkv0).then_inc(sem("wkv_in"), 16)
            sp.dma_start(row[:], rows).then_inc(sem("setup_in"), 16)
            sp.dma_start(wq0_sb[:], wq0).then_inc(sem("setup_in"), 16)
            sp.dma_start(em[0:TK, :], m0).then_inc(sem("setup_in"), 16)
            sp.dma_start(hmask[:], hmask_in).then_inc(sem("setup_in"), 16)
            sp.dma_start(gate_sb[:], gates).then_inc(sem("setup_in"), 16)

            def load_ctx0(b, par, wait):
                if wait:
                    sp.wait_ge(sem("y_ready"), NG * (b - 1))
                sp.dma_start(cT[par][:], ctxT[:, bass.ds(b * S2, S2)]).then_inc(sem(f"ctx0_in{par}"), 16)

            def pair0(i):
                for par in range(2):
                    load_ctx0(2 * i + par, par, not (isinstance(i, int) and i == 0))

            pair0(0)
            with sp.Fori(1, B // 2) as i:
                pair0(i)
            for dst, src in ((dense_sb[:], dense0), (wgu[:, 0, :], wg0), (wgu[:, 1, :], wu0), (wdn[:], wd0),
                             (mi[0:TK, :], m1), (hmask1[:], hmask1_in), (pmask[:], pmask_in),
                             (bv_sb[:], bv), (bq_sb[:], bq), (bk_sb[:], bk), (wq1_sb[:], wq1), (wk1_sb[:], wk1),
                             (wv1_sb[:], wv1), (wo1_sb[:], wo1), (den_sel[:], den_sel_in), (rank[:], rank_in),
                             (gw_sb[:], gatew), (b2_sb[:], b2)):
                sp.dma_start(dst, src).then_inc(sem("late_in"), 16)

            for par in range(2):
                sp.wait_ge(sem("y_ready"), NG * (B - 1 + par))
                sp.dma_start(cT[par][:], ctxT[:, S2 * par:S2 * par + S2]).then_inc(sem(f"ctx1_in{par}"), 16)

            sp.wait_ge(sem("att0_ready"), 1)
            for b in range(B):
                r = HALF * (b % 2)
                sp.dma_start(mixed[b].rearrange("(h s) e -> s h e", h=H),
                             att[r:r + S, b // 2, :].rearrange("s (h e) -> s h e", h=H)).then_inc(sem("mix_out"), 16)
            sp.wait_ge(sem("mix_out"), 16 * B)
            for par in range(2):
                sp.dma_start(att[HALF * par:HALF * par + S, :, :],
                             mixed.rearrange("(i two) (s j) e -> two s i (j e)", two=2, s=S)[par]
                             ).then_inc(sem("mix_in"), 16)

            def load_ctx1(w, par):
                sp.wait_ge(sem("side_ready"), filled(w - 1, "V2"))
                sp.dma_start(cT[par][:], ctxT[:, bass.ds((w + 2) * S2, S2)]).then_inc(sem(f"ctx1_in{par}"), 16)

            def stack(b, par, first_pair):
                if not first_pair:
                    sp.wait_ge(sem("sc_ready"), T * (b - 1))
                sp.wait_ge(sem("kp3_ready"), b + 1)
                for j, part in enumerate(KEY_PART):
                    sp.dma_start(KS[par][ROWS * j:ROWS * j + ROWS, 0:NPAIR * S2].rearrange("r (p n) -> r p n", p=NPAIR),
                                 KP[par][part][:]).then_inc(sem(f"stacked{par}"), 16)
                sp.wait_ge(sem("q_ready"), b + 1)
                for j, part in enumerate(QUERY_PART):
                    sp.dma_start(QS[par][ROWS * j:ROWS * j + ROWS, :].rearrange("r (p n) -> r p n", p=NPAIR),
                                 QD[par][part][:].rearrange("p k s -> p (k s)")).then_inc(sem(f"stacked{par}"), 16)

            def pair1(i):
                fixed = isinstance(i, int)
                for par in range(2):
                    w = 2 * i + par
                    if not (fixed and w + 2 >= B):
                        load_ctx1(w, par)
                    if not (fixed and w == B - 1):
                        if fixed and w == 0:
                            sp.wait_ge(sem("ks1_ready"), 1)
                        stack(w + 1, 1 - par, fixed and w == 0)

            stack(0, 0, True)
            in_pairs(sp, pair1, B // 2)

            def experts(i):
                for par in range(2):
                    e = 2 * i + par
                    if not (isinstance(i, int) and i == 0):
                        sp.wait_ge(sem("down_ready"), 2 * (e - 1))
                    sp.dma_start(w1_sb[par], w1[:, bass.ds(e * INNER, INNER)]).then_inc(sem(f"w1_in{par}"), 16)
                    sp.dma_start(b1_sb[par][:], b1[:, bass.ds(e * FC, FC)]).then_inc(sem(f"b1_in{par}"), 16)
                    sp.dma_start(w2_sb[par], w2[:, bass.ds(e * INNER, INNER)]).then_inc(sem(f"w2_in{par}"), 16)

            experts(0)
            with sp.Fori(1, E // 2) as i:
                experts(i)
            sp.wait_ge(sem("moe_done"), 2 * E)
            for par in range(2):
                sp.dma_start(out.rearrange("(i two) s d -> two s i d", two=2)[par],
                             x[HALF * par:HALF * par + S, :, :]).then_inc(sem("out_done"), 16)
            sp.wait_ge(sem("out_done"), 32)

        LATE = 18 * 16

        @block.tensor
        def _(pe):
            def transpose_tiles(src, bank, done):
                for t in range(NT):
                    ins = nc.tensor.transpose(bank4(bank)[:, t, :], src[:, t, :], ident[:])
                ins.then_inc(sem(done), 1)

            def project_tiles(lhs, w, bank, done):
                for t in range(NT):
                    ins = nc.tensor.matmul(bank4(bank)[:, t, :], lhs[:, 128 * t:128 * t + 128], w,
                                           start=True, stop=True)
                ins.then_inc(sem(done), 1)

            pe.wait_ge(sem("x_in"), 32)
            pe.wait_ge(sem("ln_done"), 1)
            transpose_tiles(xn, 0, "xT0_ps")
            pe.wait_ge(sem("xT0_ready"), 1)
            pe.wait_ge(sem("setup_in"), 80)
            project_tiles(xT, wq0_sb[:], 2, "q0_ps")
            pe.wait_ge(sem("q0_ready"), 1)
            transpose_tiles(t0, 4, "q0T_ps")

            def y_group(b, par, g, first):
                n = NG * b + g
                if g == 0:
                    pe.wait_ge(sem(f"ctx0_in{par}"), loads(b, par))
                if first:
                    if g == 0:
                        pe.wait_ge(sem("wkv_ready"), 1)
                        pe.wait_ge(sem("q0T_ready"), 1)
                else:
                    pe.wait_ge(sem("kn_ready"), n - 2)
                    pe.wait_ge(sem("vn_ready"), n - 2)
                for t in range(GT):
                    c0 = (GT * g + t) * TK
                    ins = nc.tensor.matmul(ps2[0:TK, 1024 * g + 256 * t:1024 * g + 256 * t + 256],
                                           cT[par][:, c0:c0 + TK], wkv[:].rearrange("p k d -> p (k d)"),
                                           start=True, stop=True)
                ins.then_inc(sem("y_ready"), 1)

            def kv_group(b, par, g, first):
                n = NG * b + g
                if g == 0 and not first:
                    pe.wait_ge(sem("kv_read"), b - 1)
                pe.wait_ge(sem("kp_ready"), n + 1)
                pe.wait_ge(sem("vn_ready"), n + 1)
                pe.wait_ge(sem("emc_ready"), n + 1)
                s6 = NG * par + g
                for t in range(GT):
                    ins = nc.tensor.matmul(ps[:, 6 + par, 0:D + 2], KN[0:TK, s6, t, :], VN[0:TK, s6, t, :],
                                           start=(g == 0 and t == 0), stop=(g == NG - 1 and t == GT - 1))
                ins.then_inc(sem("kv_done"), 1)

            pe.sem_inc(sem("kv_done"), SLOTS)
            for g in range(NG):
                y_group(0, 0, g, True)

            def pair(i):
                first = isinstance(i, int) and i == 0
                last = isinstance(i, int) and i == B // 2 - 1
                for g in range(NG):
                    y_group(2 * i + 1, 1, g, False)
                    kv_group(2 * i, 0, g, first)
                for g in range(NG):
                    if not last:
                        y_group(2 * i + 2, 0, g, False)
                    kv_group(2 * i + 1, 1, g, first)

            in_pairs(pe, pair, B // 2)

            def fill(w, unit, b, par):
                bank = bank_of(w, unit)
                before = emptied(w, unit) - 1
                if not isinstance(before, int) or before > 0:
                    pe.wait_ge(sem(free_of(w, unit)), before)
                if unit[0] == "K":
                    k = int(unit[1])
                    if unit[-1] == "'":
                        b, par = 1, 1
                    if k == 0:
                        if isinstance(b, int) and b == 0:
                            pe.wait_ge(sem("late_in"), LATE)
                        pe.wait_ge(sem(f"ctx1_in{par}"), loads(b, par))
                    ins = nc.tensor.matmul(ps[:, bank, 0:KCW], wk1_sb[:], cT[par][:, KCW * k:KCW * k + KCW],
                                           start=True, stop=True)
                elif unit[0] == "V":
                    g = int(unit[1])
                    for t in range(GT):
                        c0 = (GT * g + t) * TK
                        ins = nc.tensor.matmul(ps[0:TK, bank, 128 * t:128 * t + 128], cT[par][:, c0:c0 + TK],
                                               wv1_sb[:], start=True, stop=True)
                elif unit[:2] == "MX":
                    c, k = divmod(int(unit[2:]), KC)
                    if c == 0 and k == 0:
                        pe.wait_ge(sem("q_ready"), b + 1)
                        pe.wait_ge(sem("kp1_ready"), KC * (b + 1))
                    q = Qb[par][:].rearrange("p h s -> p (h s)")
                    ins = nc.tensor.matmul(ps[:, bank, 0:KCW], q[:, 128 * c:128 * c + 128],
                                           KP[par][0][:, KCW * k:KCW * k + KCW], start=True, stop=True)
                elif unit == "SH":
                    pe.wait_ge(sem("mneg_ready"), b + 1)
                    for c in range(CH):
                        for k in range(2):
                            lo, hi = max(128 * c, HQ2 * k), min(128 * c + 128, HQ2 * k + HQ2)
                            if lo < hi:
                                r = ONES - 32 * k
                                ins = nc.tensor.matmul(ps[r:r + 1, bank, lo - HQ2 * k:hi - HQ2 * k],
                                                       mneg[:, c:c + 1], identb[:, lo - 128 * c:hi - 128 * c],
                                                       start=True, stop=True)
                elif unit == "DEN":
                    pe.wait_ge(sem("o_ready"), b + 1)
                    ins = nc.tensor.matmul(ps[:, bank, 0:2 * PAIRW], den_sel[:], O[:], start=True, stop=True)
                else:
                    pe.wait_ge(sem("on_ready"), b + 1)
                    for c in range(2):
                        for k in range(2):
                            lhs = On[:, PAIRW * c + S * k:PAIRW * c + S * k + S]
                            ins = nc.tensor.matmul(ps[HALF * par:HALF * par + S, bank, 0:D], lhs,
                                                   wo1_sb[:, 2 * c + k, :], start=(c + k == 0), stop=(c + k == 2))
                ins.then_inc(sem(kind(unit) + "_ready"), 1)

            pe.wait_ge(sem("kv_read"), B)
            for b in range(B):
                t, r = b // 2, HALF * (b % 2)
                ins = nc.tensor.matmul(ps[r:r + HALF, t // 3, KVW * (t % 3):KVW * (t % 3) + KVW],
                                       qT[:, HALF * b:HALF * b + HALF], kvall[:, b, :], start=True, stop=True)
            ins.then_inc(sem("nd_ready"), 1)
            for unit in EARLY:
                fill(-1, unit, 0, 0)
            pe.wait_ge(sem("mix_in"), 32)
            transpose_tiles(att, 4, "attT_ps")
            pe.wait_ge(sem("attT_ready"), 1)
            pe.wait_ge(sem("late_in"), LATE)
            pe.wait_ge(sem("side_free"), emptied(-1, "V2"))
            project_tiles(xT, dense_sb[:], 6, "dense_ps")

            pe.wait_ge(sem("wabs_ready"), 1)
            nc.tensor.matmul(ps[:, 3, 0:3], onesf[:], wabs[:], start=True, stop=True).then_inc(sem("wsum_ps"), 1)
            pe.wait_ge(sem("kept_ready"), 1)
            nc.tensor.matmul(ps[:, 0, 0:B], onesf[0:TK, :], kept[0:TK, :], start=True,
                             stop=True).then_inc(sem("kept_ps"), 1)
            pe.wait_ge(sem("xq_ready"), 1)
            for t in range(NT):
                ins = nc.tensor.transpose(ps[:, 4, :].bitcast(BF16)[:, 128 * t:128 * t + 128], xqb[:, t, :], identb[:])
            ins.then_inc(sem("xqT_ps"), 1)
            pe.wait_ge(sem("xqT_ready"), 1)
            pe.wait_ge(sem("wq_ready"), 1)
            for t in range(NT):
                for k in range(2):
                    if t >= 2:
                        pe.wait_ge(sem("hid_ready"), t - 1)
                    ins = nc.tensor.matmul(ps[:, 2 * k + t % 2, :], xqT[:, 128 * t:128 * t + 128], wgub[:, k, :],
                                           start=True, stop=True)
                ins.then_inc(sem("gu_ps"), 1)
            for t in range(NT):
                pe.wait_ge(sem("hq_ready"), t + 1)
                if t >= 2:
                    pe.wait_ge(sem("hqT_ready"), t - 1)
                for c in range(FC):
                    ins = nc.tensor.transpose(ps[:, 4 + t % 2, :].bitcast(BF16)[:, 128 * c:128 * c + 128],
                                              hqb[:, t, 128 * c:128 * c + 128], identb[:])
                ins.then_inc(sem("hqT_ps"), 1)
            for t in range(NT):
                pe.wait_ge(sem("hqT_ready"), t + 1)
                for c in range(FC):
                    ins = nc.tensor.matmul(bank4(6)[:, t, :], hqT[:, t, c, :], wdnb[:, c, :],
                                           start=(c == 0), stop=(c == FC - 1), skip_group_check=True)
            ins.then_inc(sem("ffn_ps"), 1)

            pe.wait_ge(sem("ln_done"), 2)
            transpose_tiles(xn, 0, "xT1_ps")
            pe.wait_ge(sem("xT1_ready"), 1)
            for k in range(2):
                ins = nc.tensor.matmul(ps[:, 2 + k, :], wq1_sb[:], xT[:, 512 * k:512 * k + 512], start=True, stop=True)
            ins.then_inc(sem("q1_ps"), 1)

            def scores(b, par, t, k, first):
                n = b * T + t
                if t == 0 and k == 0:
                    pe.wait_ge(sem(f"stacked{par}"), loads(b, par, 2 * STACK))
                    pe.wait_ge(sem(free_of(b - 1, "SH")), emptied(b - 1, "SH"))
                if k == 0 and not (first and t < 2):
                    pe.wait_ge(sem("p_ready"), n - 1)
                for p in range(4 * k, 4 * k + 4):
                    c0 = S2 * p + TK * t
                    ins = nc.tensor.matmul(ps[:, 2 * (t % 2) + k, PAIRW * (p % 4):PAIRW * (p % 4) + PAIRW],
                                           KS[par][:, c0:c0 + 128], QS[par][:, PAIRW * p:PAIRW * p + PAIRW],
                                           start=True, stop=True)
                if k == 1:
                    ins.then_inc(sem("sc_ready"), 1)

            def weigh(b, par, t, first):
                n = b * T + t
                pe.wait_ge(sem("p_ready"), n + 1)
                if t == 0 and not (first and par == 0):
                    pe.wait_ge(sem("o_ready"), b)
                for p in range(NPAIR):
                    r, c = PW * (p % 4), PAIRW * (p // 4)
                    ins = nc.tensor.matmul(ps[r:r + PW, 7, c:c + PAIRW], Vp[par][0:TK, t, p, :],
                                           P[t % 2][0:TK, PAIRW * p:PAIRW * p + PAIRW],
                                           start=(t == 0 and p < 4), stop=(t == T - 1), skip_group_check=True)
                ins.then_inc(sem("pv_done"), 1)

            def window(w, par, first_pair):
                def unit_at(t, place):
                    unit = PLACES[t][place]
                    if unit in units(w):
                        b = w - 1 if unit in ENDS else w + 2 if unit[0] == "K" else w + 1
                        fill(w, unit, b, par if unit[0] == "K" else 1 - par)

                first = first_pair and par == 0
                for t in range(T):
                    scores(w, par, t, 0, first)
                    unit_at(t, 0)
                    scores(w, par, t, 1, first)
                    unit_at(t, 1)
                    if t > 0:
                        weigh(w, par, t - 1, first_pair)
                    elif not first:
                        weigh(w - 1, 1 - par, T - 1, first_pair)
                    unit_at(t, 2)

            for unit in MXS + ["SH"]:
                fill(-1, unit, 0, 0)

            def pair1(i):
                fixed = isinstance(i, int)
                for par in range(2):
                    window(2 * i + par, par, fixed and i == 0)

            in_pairs(pe, pair1, B // 2)
            weigh(B - 1, 1, T - 1, False)
            fill(B, "DEN", B - 1, 1)
            fill(B, "WO", B - 1, 1)

            pe.wait_ge(sem("ln_done"), 3)
            transpose_tiles(xn, 0, "xT2_ps")
            pe.wait_ge(sem("xT2_ready"), 1)
            for t in range(NT):
                ins = nc.tensor.matmul(ps[:, 2, E * t:E * t + E], xT[:, 128 * t:128 * t + 128], gw_sb[:],
                                       start=True, stop=True)
            ins.then_inc(sem("logit_ps"), 1)

            def up(e, par, first):
                pe.wait_ge(sem(f"w1_in{par}"), loads(e, par))
                xv = xT[:].rearrange("p (b q) -> p b q", q=HALF)
                for c in range(FC):
                    for k in range(2):
                        u = 2 * c + k
                        if not (first and u < 4):
                            pe.wait_ge(sem("h_ready"), 8 * e + u - 3)
                        nc.tensor.matmul(ps[:, u % 4, 0:8 * S], w1_sb[par][:, 128 * c:128 * c + 128],
                                         xv[:, 8 * k:8 * k + 8, 0:S], start=True, stop=True).then_inc(sem("up_ps"), 1)

            def down(e, par, first):
                pe.wait_ge(sem(f"w2_in{par}"), loads(e, par))
                pe.wait_ge(sem("h_ready"), 8 * e + 8)
                for k in range(2):
                    if not first:
                        pe.wait_ge(sem("moe_done"), 2 * e + k - 3)
                    for t in range(4):
                        for c in range(FC):
                            lhs = hT[:, par, c, 512 * k + 128 * t:512 * k + 128 * t + 128]
                            ins = nc.tensor.matmul(ps[:, 4 + 2 * par + k, 128 * t:128 * t + 128], lhs,
                                                   w2_sb[par][:, c, :], start=(c == 0), stop=(c == FC - 1),
                                                   skip_group_check=True)
                    ins.then_inc(sem("down_ready"), 1)

            pe.wait_ge(sem("pads_ready"), 1)
            pe.wait_ge(sem("pg_ready"), 1)
            nc.tensor.transpose(ps[0:64, 3, 0:128], pg[:].rearrange("p t e -> p (t e)"),
                                ident[:]).then_inc(sem("pgT_ps"), 1)
            pe.wait_ge(sem("pgT_ready"), 1)
            for k in range(2):
                ins = nc.tensor.matmul(ps[:, 4 + k, :], pgT[:], b2_sb[:, 4 * k:4 * k + 4, :], start=True, stop=True)
            ins.then_inc(sem("b2_ps"), 1)
            pe.wait_ge(sem("b2_done"), 1)
            up(0, 0, True)

            def pair2(i):
                fixed = isinstance(i, int)
                first, last = fixed and i == 0, fixed and i == E // 2 - 1
                up(2 * i + 1, 1, False)
                down(2 * i, 0, first)
                if not last:
                    up(2 * i + 2, 0, False)
                down(2 * i + 1, 1, first)

            in_pairs(pe, pair2, E // 2)

        @block.scalar
        def _(act):
            def ln_std(n, eps):
                act.wait_ge(sem("ln_var"), n)
                nc.scalar.activation(sd[:], mv[:, :, 1], ACT.Sqrt, bias=eps[:]).then_inc(sem("ln_std"), 1)

            act.wait_ge(sem("setup_done"), 1)
            act.wait_ge(sem("setup_in"), 80)
            nc.scalar.activation(th[:], gate_sb[:], ACT.Tanh).then_inc(sem("th_ready"), 1)
            ln_std(1, eps_ln)
            act.wait_ge(sem("xT0_ps"), 1)
            nc.scalar.copy(xT[:], ps2[:, 0:1024]).then_inc(sem("xT0_ready"), 1)
            ln_std(2, eps_in)
            act.wait_ge(sem("q0T_ps"), 1)
            nc.scalar.copy(qT[:], ps2[:, 2048:3072]).then_inc(sem("q0T_ready"), 1)

            def square(b, par, g, first_pair):
                n, k = NG * b + g, NG * par + g
                act.wait_ge(sem("y_ready"), n + 1)
                if not (first_pair and k < 2):
                    act.wait_ge(sem("ss_ready"), n - 1)
                nc.scalar.activation(SQ[0:TK, k % 2, :], ps2[0:TK, 1024 * g:1024 * g + 1024], ACT.Square,
                                     scale=float(D) ** -0.5).then_inc(sem("sq_ready"), 1)

            def deviation(n, k):
                act.wait_ge(sem("ss_ready"), n + 1)
                nc.scalar.activation(sdk[0:TK, k % 2, :], ss[0:TK, k % 2, :], ACT.Sqrt,
                                     bias=eps_in[0:TK, :]).then_inc(sem("sdk_ready"), 1)

            def values(n, k):
                act.wait_ge(sem("kn_ready"), n + 1)
                act.wait_ge(sem("kv_done"), n + 1)
                for t in range(GT):
                    c0 = 1024 * (k % NG) + 256 * t + D
                    ins = nc.scalar.activation(VN[0:TK, k, t, 0:D], ps2[0:TK, c0:c0 + D], ACT.Copy,
                                               scale=wv[0:TK, k % 2, t:t + 1])
                ins.then_inc(sem("vn_ready"), 1)

            def pair(i):
                first = isinstance(i, int) and i == 0
                for par in range(2):
                    for g in range(NG):
                        k = NG * par + g
                        n = NG * (2 * i + par) + g
                        square(2 * i + par, par, g, first)
                        if not (first and k < 1):
                            values(n - 1, (k - 1) % SLOTS)
                        deviation(n, k)

            in_pairs(act, pair, B // 2)
            values(NG * B - 1, SLOTS - 1)

            def values1(w, g, b, par):
                act.wait_ge(sem("side_ready"), filled(w, f"V{g}"))
                if g == 0 and not (isinstance(b, int) and b < 2):
                    act.wait_ge(sem("pv_done"), T * (b - 1))
                nc.scalar.copy(Vp[par][0:TK, GT * g:GT * g + GT, :, 1:1 + 2 * DK],
                               ps[0:TK, bank_of(w, f"V{g}"), :].rearrange("p (t j d) -> p t j d", t=GT, j=NPAIR)
                               ).then_inc(sem("side_free"), 1)

            def key_part1(w, unit, b, par):
                k = int(unit[1])
                act.wait_ge(sem("side_ready"), filled(w, unit))
                nc.scalar.activation(KP[par][0][:, KCW * k:KCW * k + KCW], ps[:, bank_of(w, unit), 0:KCW],
                                     ACT.Identity, bias=bk_sb[:]).then_inc(sem("kp1_ready"), 1)

            def key_part2(w, prime, b, par):
                act.wait_ge(sem("side_free"), emptied(w, "K2" + prime))
                nc.scalar.copy(KP[par][1][:], krest).then_inc(sem("kp2_ready"), 1)

            for unit in EARLY:
                if unit[0] == "K":
                    b = 1 if unit[-1] == "'" else 0
                    key_part1(-1, unit, b, b)
                    if unit[1] == "2":
                        key_part2(-1, unit[2:], b, b)
                else:
                    values1(-1, int(unit[1]), 0, 0)

            act.wait_ge(sem("attT_ps"), 1)
            nc.scalar.copy(xT[:], ps2[:, 2048:3072]).then_inc(sem("attT_ready"), 1)
            ln_std(3, eps_in)
            ln_std(4, eps_ln)
            act.wait_ge(sem("xqT_ps"), 1)
            nc.scalar.copy(xqT[:], ps[:, 4, :].bitcast(BF16)).then_inc(sem("xqT_ready"), 1)
            act.wait_ge(sem("cgu_ready"), 1)
            for t in range(NT):
                act.wait_ge(sem("gu_ps"), t + 1)
                if t >= 2:
                    act.wait_ge(sem("hid_ready"), t - 1)
                nc.scalar.activation(silu[:, t % 2, :], ps[:, t % 2, :], ACT.Silu,
                                     scale=cg[:, t:t + 1]).then_inc(sem("silu_ready"), 1)
            for t in range(NT):
                act.wait_ge(sem("hqT_ps"), t + 1)
                nc.scalar.copy(hqT[:, t, :, :].rearrange("p c n -> p (c n)"),
                               ps[:, 4 + t % 2, :].bitcast(BF16)[:, 0:INNER]).then_inc(sem("hqT_ready"), 1)
            ln_std(5, eps_ln)
            act.wait_ge(sem("xT1_ps"), 1)
            nc.scalar.copy(xT[:], ps2[:, 0:1024]).then_inc(sem("xT1_ready"), 1)
            act.wait_ge(sem("q1_ps"), 1)
            nc.scalar.activation(qT[:], ps2[:, 1024:2048], ACT.Identity, bias=bq_sb[:]).then_inc(sem("q1T_ready"), 1)

            def exponentials(b, par, t, first):
                n = b * T + t
                act.wait_ge(sem("sc_ready"), n + 1)
                if not (first and t < 2):
                    act.wait_ge(sem("pv_done"), n - 1)
                act.wait_ge(sem("kb_ready"), 1)
                src = ps[0:TK, 2 * (t % 2):2 * (t % 2) + 2, 0:HQ2]
                nc.scalar.activation(P[t % 2][0:TK, :].rearrange("p (k n) -> p k n", k=2), src, ACT.Exp,
                                     scale=kscale[0:TK, bass.ds(n, 1)],
                                     bias=kbias[0:TK, bass.ds(n, 1)]).then_inc(sem("p_ready"), 1)

            def take_sums(b):
                act.wait_ge(sem("pv_done"), T * (b + 1))
                if not (isinstance(b, int) and b == 0):
                    act.wait_ge(sem("on_ready"), b)
                nc.scalar.copy(O[:], ps[:, 7, 0:2 * PAIRW]).then_inc(sem("o_ready"), 1)

            def pair1(i):
                fixed = isinstance(i, int)
                for par in range(2):
                    w = 2 * i + par
                    has = units(w)
                    for t in range(T):
                        exponentials(w, par, t, fixed and w == 0)
                        if t == 0 and "DEN" in has:
                            take_sums(w - 1)
                        unit = PLACES[t][2]
                        if unit in has and unit[0] == "V":
                            values1(w, int(unit[1]), w + 1, 1 - par)
                        elif unit in has and unit[0] == "K":
                            key_part1(w, unit, w + 2, par)
                        elif t == 10 and "K2" in has:
                            key_part2(w, "", w + 2, par)

            in_pairs(act, pair1, B // 2)
            take_sums(B - 1)

            ln_std(6, eps_ln)
            act.wait_ge(sem("xT2_ps"), 1)
            nc.scalar.copy(xT[:], ps2[:, 0:1024]).then_inc(sem("xT2_ready"), 1)
            act.wait_ge(sem("logit_ready"), 1)
            nc.scalar.activation(pr[:], pr[:], ACT.Exp).then_inc(sem("pexp_ready"), 1)

            def inner(e, par, first_pair):
                act.wait_ge(sem(f"b1_in{par}"), loads(e, par))
                if first_pair and par == 0:
                    act.wait_ge(sem("pads_ready"), 1)
                for u in range(8):
                    c, k = divmod(u, 2)
                    act.wait_ge(sem("up_ps"), 8 * e + u + 1)
                    if u == 0 and not first_pair:
                        act.wait_ge(sem("down_ready"), 2 * (e - 1))
                    dst = hT[:, par, c, 512 * k:512 * k + 512].rearrange("p (b q) -> p b q", q=HALF)[:, :, 0:S]
                    nc.scalar.activation(dst, ps[:, u % 4, 0:8 * S].rearrange("p (b q) -> p b q", q=S),
                                         ACT.Gelu_apprx_tanh,
                                         bias=b1_sb[par][:, c:c + 1]).then_inc(sem("h_ready"), 1)

            def pair2(i):
                for par in range(2):
                    inner(2 * i + par, par, isinstance(i, int) and i == 0)

            in_pairs(act, pair2, E // 2)

        @block.gpsimd
        def _(pool):
            def keys(b, par, g, first):
                n, k = NG * b + g, NG * par + g
                pool.wait_ge(sem("kv_done"), n + 1)
                pool.wait_ge(sem("em_ready"), 1)
                nc.gpsimd.tensor_copy(VN[0:TK, k, :, D:D + 2],
                                      emcat[0:TK, bass.ds(b * T + GT * g, GT), :]).then_inc(sem("emc_ready"), 1)
                pool.wait_ge(sem("kn_ready"), n + 1)
                kn = KN[0:TK, k, :, :]
                nc.gpsimd.tensor_tensor(kn, kn, bc(row[0:TK, GAMMA, :], 1, [TK, GT, D]),
                                        ALU.mult).then_inc(sem("kg_ready"), 1)
                pool.wait_ge(sem("kg_ready"), n + 1)
                nc.gpsimd.tensor_tensor(kn, kn, bc(row[0:TK, BETA, :], 1, [TK, GT, D]),
                                        ALU.add).then_inc(sem("kb0_ready"), 1)

            def pair(i):
                for par in range(2):
                    for g in range(NG):
                        keys(2 * i + par, par, g, isinstance(i, int) and i == 0)

            in_pairs(pool, pair, B // 2)

            def key_part3(b, par):
                pool.wait_ge(sem("kp2_ready"), b + 1)
                nc.gpsimd.tensor_tensor(KP[par][2][:], krest, KP[par][1][:], ALU.subtract).then_inc(sem("kp3_ready"), 1)

            def queries(b, par, first_pair):
                if not first_pair:
                    pool.wait_ge(sem("aux_ready"), filled(b - 3, MXS[-1]))
                    pool.wait_ge(sem(f"stacked{par}"), loads(b - 2, par, 2 * STACK))
                for k in range(3):
                    nc.gpsimd.tensor_tensor(QD[par][k][:], bc(QP[k][:, bass.ds(b * HALF, S)], 1, [128, 2, S]),
                                            bc(pmask[:], 2, [128, 2, S]), ALU.mult)
                nc.gpsimd.tensor_tensor(Qb[par][:], bc(QP[0][:, bass.ds(b * HALF, S)], 1, [128, H, S]),
                                        bc(hmask1[:], 2, [128, H, S]), ALU.mult).then_inc(sem("q_ready"), 1)

            for b in range(2):
                key_part3(b, b)
            pool.wait_ge(sem("qp_ready"), 1)
            for b in range(2):
                queries(b, b, True)

            def pair1(i):
                for par in range(2):
                    b = 2 * i + par + 2
                    queries(b, par, False)
                    key_part3(b, par)

            pair1(0)
            with pool.Fori(1, B // 2 - 1) as i:
                pair1(i)

        @block.vector
        def _(dve):
            v = nc.vector
            steps = [0]

            def step(ins):
                steps[0] += 1
                ins.then_inc(sem("dve_step"), 1)
                dve.wait_ge(sem("dve_step"), steps[0])

            def layernorm(n, src, dst, signal=None):
                for t in range(NT):
                    ins = v.bn_stats(stats[:, t, :], src[:, t, :])
                step(ins)
                for t in range(NT):
                    ins = v.bn_aggr(mv[:, t, :], stats[:, t, :])
                ins.then_inc(sem("ln_var"), 1)
                dve.wait_ge(sem("ln_std"), n)
                step(v.reciprocal(rstd[:], sd[:]))
                for t in range(NT):
                    ins = v.tensor_scalar(dst[:, t, :], src[:, t, :], mv[:, t, 0:1], rstd[:, t:t + 1],
                                          ALU.subtract, ALU.mult)
                if signal:
                    ins.then_inc(sem(signal), 1)
                else:
                    step(ins)

            def rows_of(k):
                return bc(row[:, k, :], 1, [128, NT, D])

            v.memset(onesf[:], 1.0)
            v.memset(eps_ln[:], EPS_LN)
            v.memset(eps_in[:], EPS_IN)
            for n in range(2):
                v.memset(Vp[n][:], 0.0)
            step(v.memset(att[:], 0.0))
            for n in range(2):
                v.memset(Vp[n][:, :, :, 0:1], 1.0)
            for n in range(2):
                v.memset(QS[n][ONES:128, :], 0.0)
            v.memset(KS[0][:, NPAIR * S2:], 0.0)
            step(v.memset(KS[0][ONES:128, 0:NPAIR * S2], 1.0))
            v.memset(Qb[0][0:1, 0, 0:2], 0.0).then_inc(sem("setup_done"), 1)

            dve.wait_ge(sem("x_in"), 32)
            layernorm(1, x, xn, "ln_done")
            step(v.tensor_copy(identb[:], ident[:]))
            dve.wait_ge(sem("wkv_in"), 16)
            step(v.tensor_reduce(wkv_mean[:], wkv[:], AX.X, ALU.add, negate=True))
            step(v.tensor_scalar(wkv_mean[:], wkv_mean[:], 1.0 / D, None, ALU.mult))
            for k in range(2):
                ins = v.tensor_scalar(wkv[:, k, :], wkv[:, k, :], wkv_mean[:, k:k + 1], None, ALU.add)
            ins.then_inc(sem("wkv_ready"), 1)
            dve.wait_ge(sem("setup_in"), 80)
            step(v.tensor_tensor(em2[0:TK, :], em[0:TK, :], em[0:TK, :], ALU.mult))
            v.tensor_copy(emcat[0:TK, :, 0], em2[0:TK, :])
            v.tensor_copy(emcat[0:TK, :, 1], em[0:TK, :]).then_inc(sem("em_ready"), 1)
            hm3 = bc(hmask[:], 2, [128, H, DK])
            v.tensor_tensor(gmask[:].rearrange("p (h d) -> p h d", h=H),
                            row[:, GAMMA, :].rearrange("p (h d) -> p h d", h=H), hm3, ALU.mult)
            step(v.tensor_tensor(bmask[:].rearrange("p (h d) -> p h d", h=H),
                                 row[:, BETA, :].rearrange("p (h d) -> p h d", h=H), hm3, ALU.mult))
            dve.wait_ge(sem("q0_ps"), 1)
            layernorm(2, bank4(2), t0)
            step(v.tensor_tensor(t0[:], t0[:], rows_of(GAMMA), ALU.mult))
            step(v.tensor_tensor(t0[:], t0[:], rows_of(BETA), ALU.add))
            v.tensor_scalar(t0[:], t0[:], 0.0, EPS_IN, ALU.max, ALU.add).then_inc(sem("q0_ready"), 1)

            def norms(n, k):
                dve.wait_ge(sem("sq_ready"), n + 1)
                v.tensor_reduce(ss[0:TK, k % 2, :], SQ[0:TK, k % 2, :].rearrange("p (j d) -> p j d", d=D),
                                AX.X, ALU.add).then_inc(sem("ss_ready"), 1)

            def keys(b, n, k, first_pair):
                g = k % NG
                dve.wait_ge(sem("sdk_ready"), n + 1)
                r = rk[0:TK, k % 2, :, :]
                v.reciprocal(r.rearrange("p t j -> p (t j)"), sdk[0:TK, k % 2, :]).then_inc(sem("rk_ready"), 1)
                dve.wait_ge(sem("rk_ready"), n + 1)
                if not (first_pair and k < 2):
                    dve.wait_ge(sem("vn_ready"), n - 1)
                v.tensor_tensor(wv[0:TK, k % 2, :], r[:, :, 1], em2[0:TK, bass.ds(b * T + GT * g, GT)],
                                ALU.mult)
                dve.wait_ge(sem("kv_done"), n + 1)
                y = ps2[0:TK, 1024 * g:1024 * g + 1024].rearrange("p (t n) -> p t n", t=GT)[:, :, 0:D]
                v.tensor_tensor(KN[0:TK, k, :, :], y, bc(r[:, :, 0], 2, [TK, GT, D]),
                                ALU.mult).then_inc(sem("kn_ready"), 1)

            def relu(n, k):
                dve.wait_ge(sem("kb0_ready"), n + 1)
                kn = KN[0:TK, k, :, :]
                v.tensor_scalar(kn, kn, 0.0, EPS_IN, ALU.max, ALU.add).then_inc(sem("kp_ready"), 1)

            def state(b, par):
                dve.wait_ge(sem("kv_done"), NG * (b + 1) + SLOTS)
                kv = ps[:, 6 + par, :]
                v.tensor_tensor(kvtmp[:, par, :], kv[:, 0:D], gmask[:], ALU.mult).then_inc(sem("kvt_ready"), 1)
                v.tensor_scalar(kvall[:, bass.ds(b, 1), D:KVW], hmask[:].unsqueeze(1), kv[:, D + 1:D + 2], None,
                                ALU.mult)
                dve.wait_ge(sem("kvt_ready"), b + 1)
                v.scalar_tensor_tensor(kvall[:, bass.ds(b, 1), 0:D], bmask[:].unsqueeze(1), kv[:, D:D + 1],
                                       kvtmp[:, par, :].unsqueeze(1), ALU.mult, ALU.add).then_inc(sem("kv_read"), 1)

            def pair(i):
                first = isinstance(i, int) and i == 0
                for par in range(2):
                    b = 2 * i + par
                    for g in range(NG):
                        n, k = NG * b + g, NG * par + g
                        norms(n, k)
                        if not (first and k < 2):
                            relu(n - 2, (k - 2) % SLOTS)
                        if g == 0 and not first:
                            state(b - 2, par)
                        keys(b, n, k, first)

            in_pairs(dve, pair, B // 2)
            last = NG * B - 1
            relu(last - 1, SLOTS - 2)
            relu(last, SLOTS - 1)
            state(B - 2, 0)
            state(B - 1, 1)

            dve.wait_ge(sem("nd_ready"), 1)

            def nd(t):
                return ps[:, t // 3, KVW * (t % 3):KVW * (t % 3) + KVW]

        
            for t in range(NT):
                ins = v.tensor_scalar(xn[:, t, 0:H], nd(t)[:, D:KVW], EPS_IN, None, ALU.add)
            step(ins)
            step(v.reciprocal(xn[:, :, H:2 * H], xn[:, :, 0:H]))
            for t in range(NT):
                ins = v.tensor_tensor(att[:, t, :].rearrange("p (h d) -> p h d", h=H),
                                      nd(t)[:, 0:D].rearrange("p (h d) -> p h d", h=H),
                                      bc(xn[:, t, H:2 * H], 2, [128, H, DK]), ALU.mult)
            ins.then_inc(sem("att0_ready"), 1)
            def key_rest(w, unit, b, par):
                k = int(unit[1])
                dve.wait_ge(sem("kp1_ready"), KC * b + k + 1)
                if k == 0 and not (isinstance(b, int) and b == 0):
                    dve.wait_ge(sem("kp3_ready"), b)
                cols = slice(KCW * k, KCW * k + KCW)
                v.scalar_tensor_tensor(krest[:, cols], ps[:, bank_of(w, unit), 0:KCW], bk_sb[:], KP[par][0][:, cols],
                                       ALU.add, ALU.subtract).then_inc(sem("side_free"), 1)

            for unit in EARLY[0:6]:
                b = 1 if unit[-1] == "'" else 0
                key_rest(-1, unit, b, b)

            dve.wait_ge(sem("late_in"), LATE)
            v.tensor_reduce(wabs[:, 0:2], wgu[:], AX.X, ALU.add, apply_absolute_value=True)
            v.tensor_reduce(wabs[:, 2:3], wdn[:].rearrange("p c n -> p (c n)"), AX.X, ALU.add,
                            apply_absolute_value=True).then_inc(sem("wabs_ready"), 1)
            step(v.tensor_scalar(keep[0:TK, :], mi[0:TK, :], 0.0, None, ALU.not_equal))
            v.tensor_reduce(kept[0:TK, :], keep[0:TK, :].rearrange("p (b t) -> p b t", b=B), AX.X,
                            ALU.max).then_inc(sem("kept_ready"), 1)
            dve.wait_ge(sem("kept_ps"), 1)
            step(v.tensor_scalar(anykept[:], ps[:, 0, 0:B], 0.0, 1e9, ALU.is_gt, ALU.mult))
            v.tensor_scalar(kscale[0:TK, :], keep[0:TK, :], SCALE, None, ALU.mult)
            step(v.tensor_scalar(keep[0:TK, :], keep[0:TK, :], 1.0, None, ALU.subtract))
            v.tensor_tensor(kbias[0:TK, :].rearrange("p (b t) -> p b t", b=B),
                            keep[0:TK, :].rearrange("p (b t) -> p b t", b=B),
                            bc(anykept[0:TK, :], 2, [TK, B, T]), ALU.mult).then_inc(sem("kb_ready"), 1)
            dve.wait_ge(sem("wsum_ps"), 1)
            step(v.tensor_scalar(wmean[:], ps[:, 3, 0:3], 1.0 / (INNER * D), 1e-5, ALU.mult, ALU.max))
            step(v.reciprocal(wscale[:], wmean[:]))
            for k in range(2):
                v.tensor_scalar(wgu[:, k, :], wgu[:, k, :], wscale[:, k:k + 1], ROUND, ALU.mult, ALU.add)
            step(v.tensor_scalar(wdn[:], wdn[:], wscale[:, 2:3], ROUND, ALU.mult, ALU.add))
            v.tensor_scalar(wgu[:], wgu[:], ROUND, -1.0, ALU.subtract, ALU.max)
            step(v.tensor_scalar(wdn[:], wdn[:], ROUND, -1.0, ALU.subtract, ALU.max))
            v.tensor_scalar(wgub[:], wgu[:], 1.0, None, ALU.min)
            v.tensor_scalar(wdnb[:], wdn[:], 1.0, None, ALU.min).then_inc(sem("wq_ready"), 1)

            dve.wait_ge(sem("dense_ps"), 1)
            step(v.tensor_tensor(t0[:], bank4(6), rows_of(DENSE_B), ALU.add))
            layernorm(3, t0, t0)
            step(v.tensor_tensor(t0[:], t0[:], rows_of(GAMMA), ALU.mult))
            step(v.tensor_tensor(t0[:], t0[:], rows_of(BETA), ALU.add))
            dve.wait_ge(sem("th_ready"), 1)
            step(v.scalar_tensor_tensor(x[:], t0[:], th[:, 0:1], x[:], ALU.mult, ALU.add))

            def quantise(src, dst, n0, n1, scratch, signal):
                a = amax[:, n0:n1]
                step(v.tensor_reduce(a, src, AX.X, ALU.max, apply_absolute_value=True))
                step(v.tensor_scalar(a, a, 1e-5, None, ALU.max))
                step(v.reciprocal(qs[:, n0:n1], a))
                step(v.tensor_scalar(qs[:, n0:n1], qs[:, n0:n1], 127.0, None, ALU.mult))
                v.tensor_scalar(a, a, 1.0 / 127.0, None, ALU.mult)
                for t in range(n0, n1):
                    ins = v.tensor_scalar(scratch[:, t - n0, :], src[:, t - n0, :], qs[:, t:t + 1], ROUND,
                                          ALU.mult, ALU.add)
                step(ins)
                step(v.tensor_scalar(scratch, scratch, ROUND, -128.0, ALU.subtract, ALU.max))
                v.tensor_scalar(dst, scratch, 127.0, None, ALU.min).then_inc(sem(signal), 1)

            layernorm(4, x, xn)
            quantise(xn[:], xqb[:], 0, NT, t0[:], "xq_ready")
            dve.wait_ge(sem("xq_ready"), 1)
            v.tensor_scalar(cg[:], amax[:], wmean[:, 0:1], None, ALU.mult)
            v.tensor_scalar(cu[:], amax[:], wmean[:, 1:2], None, ALU.mult).then_inc(sem("cgu_ready"), 1)
            for t in range(NT):
                dve.wait_ge(sem("silu_ready"), t + 1)
                v.scalar_tensor_tensor(hid[:, t, :], ps[:, 2 + t % 2, :], cu[:, t:t + 1], silu[:, t % 2, :],
                                       ALU.mult, ALU.mult).then_inc(sem("hid_ready"), 1)
            dve.wait_ge(sem("hid_ready"), NT)
            for t in range(NT):
                quantise(hid[:, t:t + 1, :], hqb[:, t:t + 1, :], t, t + 1, hid[:, t:t + 1, :], "hq_ready")
            step(v.tensor_scalar(cd[:], amax[:], wmean[:, 2:3], th[:, 2:3], ALU.mult, ALU.mult))
            dve.wait_ge(sem("ffn_ps"), 1)
            for t in range(NT):
                ins = v.scalar_tensor_tensor(x[:, t, :], bank4(6)[:, t, :], cd[:, t:t + 1], x[:, t, :],
                                             ALU.mult, ALU.add)
            step(ins)
            layernorm(5, x, xn, "ln_done")

            dve.wait_ge(sem("q1T_ready"), 1)
            step(v.tensor_copy(QP[0], qT[:]))
            step(v.tensor_tensor(qT[:], qT[:], QP[0], ALU.subtract))
            step(v.tensor_copy(QP[1], qT[:]))
            v.tensor_tensor(QP[2], qT[:], QP[1], ALU.subtract).then_inc(sem("qp_ready"), 1)
            v.memset(KS[1][:, NPAIR * S2:], 0.0)
            v.memset(KS[1][ONES:128, 0:NPAIR * S2], 1.0).then_inc(sem("ks1_ready"), 1)

            def empty(w, unit, b, par):
                bank = bank_of(w, unit)
                dve.wait_ge(sem("aux_ready"), filled(w, unit))
                if unit[:2] == "MX":
                    c, k = divmod(int(unit[2:]), KC)
                    if c == 0 and k == 0 and not (isinstance(b, int) and b == 0):
                        dve.wait_ge(sem("mneg_ready"), b)
                    ins = v.tensor_reduce(mx[:, c, k:k + 1], ps[:, bank, 0:KCW], AX.X, ALU.max)
                elif unit == "SH":
                    if not (isinstance(b, int) and b < 2):
                        dve.wait_ge(sem("sc_ready"), T * (b - 1))
                    for k in range(2):
                        r = ONES - 32 * k
                        ins = v.tensor_copy(QS[par][ONES:ONES + 1, HQ2 * k:HQ2 * k + HQ2],
                                            ps[r:r + 1, bank, 0:HQ2])
                elif unit == "DEN":
                    ins = v.reciprocal(rden[:], ps[:, bank, 0:2 * PAIRW])
                else:
                    dst = att[HALF * par:HALF * par + S, bass.ds(b // 2, 1), :]
                    ins = v.tensor_copy(dst, ps[HALF * par:HALF * par + S, bank, 0:D].unsqueeze(1))
                ins.then_inc(sem(free_of(w, unit)), 1)
                if unit == "DEN":
                    dve.wait_ge(sem(free_of(w, unit)), emptied(w, unit))
                    v.tensor_tensor(On[:], O[:], rden[:], ALU.mult).then_inc(sem("on_mul"), 1)
                    dve.wait_ge(sem("on_mul"), b + 1)
                    on3 = On[:].rearrange("p (c n) -> p c n", c=2)
                    v.tensor_tensor(on3, on3, bc(bv_sb[:], 2, [128, 2, PAIRW]), ALU.add).then_inc(sem("on_ready"), 1)

            def maxima(w):
                for unit in MXS[-2:]:
                    dve.wait_ge(sem(free_of(w, unit)), emptied(w, unit))
                v.tensor_reduce(mneg[:], mx[:], AX.X, ALU.max, negate=True).then_inc(sem("mneg_ready"), 1)

            def window(w, par):
                todo = [unit for unit in units(w) if unit[0] != "V"]
                for k in range(KC):
                    if f"K{k}" in todo:
                        n = todo.index(f"K{k}")
                        todo.insert(n + REST_LATER, todo.pop(n))
                for unit in todo:
                    if unit == "SH":
                        maxima(w)
                    if unit[0] == "K":
                        key_rest(w, unit, w + 2, par)
                    elif unit in ENDS:
                        empty(w, unit, w - 1, 1 - par)
                    else:
                        empty(w, unit, w + 1, 1 - par)

            for unit in MXS + ["SH"]:
                if unit == "SH":
                    maxima(-1)
                empty(-1, unit, 0, 0)

            def pair1(i):
                for par in range(2):
                    window(2 * i + par, par)

            in_pairs(dve, pair1, B // 2)
            empty(B, "DEN", B - 1, 1)
            empty(B, "WO", B - 1, 1)
            dve.wait_ge(sem(free_of(B, "WO")), emptied(B, "WO"))
            step(v.tensor_tensor(att[:], att[:], rows_of(B_O), ALU.add))
            step(v.scalar_tensor_tensor(x[:], att[:], th[:, 1:2], x[:], ALU.mult, ALU.add))

            layernorm(6, x, xn, "ln_done")
            v.memset(hT[:, :, :, :].rearrange("p s c (b q) -> p (s c b) q", q=HALF)[:, :, S:HALF],
                     0.0).then_inc(sem("pads_ready"), 1)
            dve.wait_ge(sem("logit_ps"), 1)
            lg = ps[:, 2, 0:NT * E].rearrange("p (t e) -> p t e", e=E)
            full3 = [128, NT, E]
            step(v.tensor_reduce(pm[:], lg, AX.X, ALU.max))
            v.tensor_tensor(pr[:], lg, bc(pm[:], 2, full3), ALU.subtract).then_inc(sem("logit_ready"), 1)
            dve.wait_ge(sem("pexp_ready"), 1)
            step(v.tensor_reduce(pd[:], pr[:], AX.X, ALU.add))
            step(v.reciprocal(pd[:], pd[:]))
            step(v.tensor_tensor(pr[:], pr[:], bc(pd[:], 2, full3), ALU.mult))
            step(v.tensor_copy(pc[:], pr[:]))
            for k in range(2):
                step(v.tensor_reduce(pm[:], pc[:], AX.X, ALU.max))
                step(v.tensor_tensor(ph[:], pc[:], bc(pm[:], 2, full3), ALU.is_equal))
                step(v.tensor_tensor(ph[:], ph[:], rank[:], ALU.mult))
                step(v.tensor_reduce(pm[:], ph[:], AX.X, ALU.max))
                step(v.tensor_tensor(ph[:], rank[:], bc(pm[:], 2, full3), ALU.is_equal))
                if k == 0:
                    step(v.tensor_copy(pg[:], ph[:]))
                    step(v.scalar_tensor_tensor(pc[:], ph[:], -2.0, pc[:], ALU.mult, ALU.add))
            step(v.tensor_tensor(pg[:], pg[:], ph[:], ALU.add))
            step(v.tensor_tensor(pg[:], pg[:], pr[:], ALU.mult))
            v.tensor_scalar(pg[:], pg[:], th[:, 3:4], None, ALU.mult).then_inc(sem("pg_ready"), 1)
            dve.wait_ge(sem("pgT_ps"), 1)
            v.tensor_copy(pgT[:], ps[0:64, 3, 0:128]).then_inc(sem("pgT_ready"), 1)
            dve.wait_ge(sem("b2_ps"), 1)
            v.tensor_tensor(x[:], x[:], bank4(4), ALU.add).then_inc(sem("b2_done"), 1)

            def add_expert(e, par, first_pair):
                for k in range(2):
                    dve.wait_ge(sem("down_ready"), 2 * e + k + 1)
                    if first_pair and par == 0:
                        dve.wait_ge(sem("b2_done"), 1)
                    else:
                        dve.wait_ge(sem("moe_done"), 2 * e + k - 1)
                    for t in range(4):
                        ins = v.scalar_tensor_tensor(x[:, 4 * k + t, :], ps[:, 4 + 2 * par + k, 128 * t:128 * t + 128],
                                                     pg[:, 4 * k + t, bass.ds(e, 1)], x[:, 4 * k + t, :],
                                                     ALU.mult, ALU.add)
                    ins.then_inc(sem("moe_done"), 1)

            def pair2(i):
                for par in range(2):
                    add_expert(2 * i + par, par, isinstance(i, int) and i == 0)

            in_pairs(dve, pair2, E // 2)


def _layout(v):
    import numpy as np
    f = np.float32
    xh = np.zeros((128, NT, D), f)
    x4 = v["x"].reshape(NT, 2, S, D)
    xh[0:S] = x4[:, 0].transpose(1, 0, 2)
    xh[HALF:HALF + S] = x4[:, 1].transpose(1, 0, 2)

    def rep(a):
        return np.broadcast_to(a, (128,) + a.shape)

    wo = np.zeros((4, PW, 2, 2, D), f)
    woT = v["L1_xattn_W_o"].T.reshape(2, 4, 2, DK, D)
    for k in range(2):
        wo[:, 1 + DK * k:1 + DK * k + DK, :, k, :] = woT[:, :, k].transpose(1, 2, 0, 3)
    bv = np.zeros((4, PW, 2), f)
    bv[:, 1:1 + 2 * DK] = v["L1_xattn_b_v"].reshape(2, 4, 2 * DK).transpose(1, 2, 0)
    order = np.arange(D).reshape(NPAIR, 2 * DK).T.reshape(D)
    b2 = np.zeros((NT, E, NT, D), f)
    for t in range(NT):
        b2[t, :, t] = v["L1_ffn_b2"]
    sel = np.zeros((128, 128), f)
    for j in range(4):
        sel[PW * j, PW * j:PW * j + PW] = 1.0
    mask = lambda m: m.reshape(B, T, TK).transpose(2, 0, 1).reshape(TK, B * T)
    return {
        "xh": xh,
        "ctxT": v["ctx_1024"].reshape(B * S2, D).T,
        "m0": mask(v["mask_BxS2_ff1"]),
        "m1": mask(v["mask_BxS2_if1"]),
        "gates": rep(np.concatenate([v["g_xattn"], v["g_ffn"]])),
        "rows": rep(np.stack([v["L0_xattn_ln_gamma"], v["L0_xattn_ln_beta"], v["L0_xattn_dense_b"],
                              v["L1_xattn_b_o"]])),
        "bq": v["L1_xattn_b_q"][order].reshape(D, 1),
        "bk": v["L1_xattn_b_k"][order].reshape(D, 1),
        "bv": bv.reshape(128, 2),
        "wkv0": np.stack([v["L0_xattn_wk"], v["L0_xattn_wv"]], axis=1),
        "wq0": v["L0_xattn_wq"],
        "dense0": v["L0_xattn_dense_w"],
        "wg0": v["L0_ffn_w_gate"].T,
        "wu0": v["L0_ffn_w_up"].T,
        "wd0": v["L0_ffn_w_down"].T.reshape(FC, 128, D).transpose(1, 0, 2),
        "wq1": v["L1_xattn_W_q"][order].T,
        "wk1": v["L1_xattn_W_k"][order].T,
        "wv1": v["L1_xattn_W_v"].T,
        "wo1": wo.reshape(128, 4, D),
        "gatew": v["L1_ffn_gate_w"].T,
        "w1": v["L1_ffn_w1"].transpose(2, 1, 0).reshape(D, E * INNER),
        "b1": v["L1_ffn_b1"].reshape(E * FC, 128).T,
        "w2": v["L1_ffn_w2"].transpose(1, 2, 0).reshape(E, FC, 128, D).transpose(2, 0, 1, 3).reshape(128, E * INNER),
        "b2": b2.reshape(NT * E, NT, D),
        "ident_in": np.eye(128, dtype=f),
        "hmask_in": np.repeat(np.eye(H, dtype=f), DK, axis=0),
        "hmask1_in": np.repeat(np.eye(H, dtype=f), DK, axis=0)[order],
        "pmask_in": np.repeat(np.eye(2, dtype=f), HALF, axis=0),
        "den_sel_in": sel,
        "rank_in": np.broadcast_to(np.arange(E, 0, -1).astype(f), (128, NT, E)),
    }


def kernel(**inputs):
    import numpy as np
    import concourse.bacc as bacc
    from concourse.bass_utils import run_bass_kernel_spmd

    laid = {n: np.ascontiguousarray(a) for n, a in _layout({k: np.asarray(a) for k, a in inputs.items()}).items()}
    nc = bacc.Bacc("TRN2", target_bir_lowering=False, num_devices=1)
    args = {n: nc.dram_tensor(n + "_dram", a.shape, mybir.dt.from_np(a.dtype), kind="ExternalInput").ap()
            for n, a in laid.items()}
    out = nc.dram_tensor("out_dram", (B, S, D), F32, kind="ExternalOutput").ap()
    build(nc, out=out, **args)
    r = run_bass_kernel_spmd(nc, [{n + "_dram": a for n, a in laid.items()}], core_ids=[0])
    return r.results[0]["out_dram"]
```

```python
from contextlib import ExitStack

import concourse.bass as bass
from concourse import mybir

ALU = mybir.AluOpType
ACT = mybir.ActivationFunctionType
AX = mybir.AxisListType
F32 = mybir.dt.float32
BF16 = mybir.dt.bfloat16
I32 = mybir.dt.int32

B, S, D = 16, 56, 128
S2 = 1500
H, DK = 16, 8
T, TK = 12, 125
GT, NG = 4, 3
NT = B // 2
HALF = 64
ND = B * S // 128
COLS = NT * 128
INNER = 512
FC = INNER // 128
E = 8
HQ = H * S
HQ2 = HQ // 2
CH = HQ // 128
KC = 3
KCW = S2 // KC
PAIRW = 2 * S
PW = 32
NPAIR = H // 2
SLOTS = 2 * NG
KVW = D + H
EPS_LN, EPS_IN = 1e-5, 1e-6
ROUND = 12582912.0
SCALE = 1.0 / float(DK) ** 0.5

KEY_PART = (0, 0, 0, 1, 1, 2)
QUERY_PART = (0, 1, 2, 0, 1, 0)
STACK = len(KEY_PART)
ROWS = 2 * DK
ONES = STACK * ROWS
KSW = NPAIR * S2 + 128 - TK

MXS = [f"MX{n}" for n in range(CH * KC)]
PLACES = [["MX0", "MX1", "V0"], ["MX2", "MX3", "MX4"], ["DEN", None, "V1"], ["MX5", "MX6", "V2"],
          ["MX7", "WO", "K0"], ["MX8", "MX9", "MX10"], ["MX11", "MX12", "K1"], ["MX13", "MX14", "MX15"],
          ["MX16", "MX17", "K2"], ["MX18", "MX19", "MX20"], [None, None, None], ["SH", None, None]]
ALL = [u for places in PLACES for u in places if u]
ENDS = ["DEN", "WO"]
EARLY = ["K0", "K1", "K2", "V0", "V1", "V2", "K0'", "K1'", "K2'"]
REST_LATER = 3


def kind(unit):
    return "side" if unit[0] in "KV" else "aux"


def units(w, of=None):
    if not isinstance(w, int):
        now = ALL
    elif w < 0:
        now = EARLY + MXS + ["SH"]
    elif w >= B - 1:
        now = ENDS
    else:
        now = [u for u in ALL if not (w == 0 and u in ENDS) and not (w == B - 2 and u[0] == "K")]
    return [u for u in now if of is None or kind(u) == of]


def count_at(w, unit):
    k = kind(unit)
    n = units(w, k).index(unit)
    if isinstance(w, int):
        return 0, n + sum(len(units(j, k)) for j in range(-1, w))
    each = len(units(w, k))
    return each, n + len(units(-1, k)) + len(units(0, k)) - each


def filled(w, unit):
    m, c = count_at(w, unit)
    return c + 1 if m == 0 else w * m + (c + 1)


def bank_of(w, unit):
    return 6 if kind(unit) == "side" else 4 + count_at(w, unit)[1] % 2


def free_of(w, unit):
    return "side_free" if kind(unit) == "side" else f"aux_free{bank_of(w, unit)}"


def emptied(w, unit):
    m, c = count_at(w, unit)
    if kind(unit) == "aux":
        m, c = m // 2, c // 2
    return c + 1 if m == 0 else w * m + (c + 1)


def loads(b, par, n=1):
    return 8 * n * b + (16 - 8 * par) * n


def in_pairs(eng, body, pairs):
    body(0)
    with eng.Fori(1, pairs - 1) as i:
        body(i)
    body(pairs - 1)


def build(nc, xh, ctxT, m0, m1, gates, rows, bq, bk, wkv0, wq0, dense0, wg0, wu0, wd0, wq1, wk1, wv1, wo1,
          gatew, w1, b1, w2, b2, bv, ident_in, hmask_in, hmask1_in, pmask_in,
          den_sel_in, rank_in, out):
    with ExitStack() as ctx:
        def sb(name, shape, dt=F32):
            return ctx.enter_context(nc.sbuf_tensor(name, shape, dt))

        sems = {}

        def sem(name):
            if name not in sems:
                sems[name] = ctx.enter_context(nc.semaphore(name))
            return sems[name]

        x = sb("x", [128, NT, D])
        xn = sb("xn", [128, NT, D])
        t0 = sb("t0", [128, NT, D])
        att = sb("att", [128, NT, D])
        xT = sb("xT", [128, COLS])
        qT = sb("qT", [128, COLS])
        stats = sb("stats", [128, NT, 6])
        mv = sb("mv", [128, NT, 2])
        sd = sb("sd", [128, NT])
        rstd = sb("rstd", [128, NT])
        ident = sb("ident", [128, 128])
        identb = sb("identb", [128, 128], BF16)
        onesf = sb("onesf", [128, 128])
        hmask = sb("hmask", [128, H])
        hmask1 = sb("hmask1", [128, H])
        pmask = sb("pmask", [128, 2])
        bv_sb = sb("bv_sb", [128, 2])
        den_sel = sb("den_sel", [128, 128])
        rank = sb("rank", [128, NT, E])
        eps_ln = sb("eps_ln", [128, 1])
        eps_in = sb("eps_in", [128, 1])
        gate_sb = sb("gate_sb", [128, 4])
        th = sb("th", [128, 4])
        row = sb("row", [128, 4, D])
        GAMMA, BETA, DENSE_B, B_O = range(4)
        gmask = sb("gmask", [128, D])
        bmask = sb("bmask", [128, D])
        wkv = sb("wkv", [128, 2, D])
        wkv_mean = sb("wkv_mean", [128, 2])
        wq0_sb = sb("wq0_sb", [128, D])
        dense_sb = sb("dense_sb", [128, D])
        bq_sb = sb("bq_sb", [128, 1])
        bk_sb = sb("bk_sb", [128, 1])
        wq1_sb = sb("wq1_sb", [128, D])
        wk1_sb = sb("wk1_sb", [128, D])
        wv1_sb = sb("wv1_sb", [128, D])
        wo1_sb = sb("wo1_sb", [128, 4, D])
        em = sb("em", [128, B * T])
        em2 = sb("em2", [128, B * T])
        emcat = sb("emcat", [128, B * T, 2])
        mi = sb("mi", [128, B * T], I32)
        keep = sb("keep", [128, B * T])
        kscale = sb("kscale", [128, B * T])
        kbias = sb("kbias", [128, B * T])
        kept = sb("kept", [128, B])
        anykept = sb("anykept", [128, B])
        cT = [sb(f"cT{n}", [128, S2]) for n in range(2)]
        kvall = sb("kvall", [128, B, KVW])
        kvtmp = sb("kvtmp", [128, 2, D])
        ss = sb("ss", [128, 2, 2 * GT])
        sdk = sb("sdk", [128, 2, 2 * GT])
        rk = sb("rk", [128, 2, GT, 2])
        wv = sb("wv", [128, 2, GT])
        arena = sb("arena", [128, 8240])
        KN = arena[:, 0:3072].rearrange("p (s t d) -> p s t d", s=6, t=GT)
        VN = arena[:, 3072:6192].rearrange("p (s t d) -> p s t d", s=6, t=GT)
        SQ = arena[:, 6192:8240].rearrange("p (s n) -> p s n", s=2)
        hid = arena[:, 0:4096].rearrange("p (t n) -> p t n", t=NT)
        hqb = arena[:, 4096:6144].bitcast(BF16).rearrange("p (t n) -> p t n", t=NT)
        hqT = arena[:, 6144:8192].bitcast(BF16).rearrange("p (t c n) -> p t c n", t=NT, c=FC)
        hT = arena[:, 0:2 * FC * B * S].rearrange("p (s c n) -> p s c n", s=2, c=FC)
        wgu = sb("wgu", [128, 2, INNER])
        wdn = sb("wdn", [128, FC, D])
        wgub = sb("wgub", [128, 2, INNER], BF16)
        wdnb = sb("wdnb", [128, FC, D], BF16)
        wabs = sb("wabs", [128, 3])
        wmean = sb("wmean", [128, 3])
        wscale = sb("wscale", [128, 3])
        xqb = sb("xqb", [128, NT, D], BF16)
        xqT = sb("xqT", [128, COLS], BF16)
        amax = sb("amax", [128, NT])
        qs = sb("qs", [128, NT])
        cg = sb("cg", [128, NT])
        cu = sb("cu", [128, NT])
        cd = sb("cd", [128, NT])
        silu = sb("silu", [128, 2, INNER])
        KP = [[sb(f"KP{n}_{k}", [128, S2], BF16) for k in range(3)] for n in range(2)]
        krest = kvall[:, :, :].rearrange("p b n -> p (b n)")[:, 0:S2]
        QP = [wgub[:].rearrange("p k n -> p (k n)"), xqb[:].rearrange("p t d -> p (t d)"), xqT[:]]
        QD = [[sb(f"QD{n}_{k}", [128, 2, S], BF16) for k in range(3)] for n in range(2)]
        KS = [sb("KS0", [128, KSW], BF16)[:], arena[:, 0:KSW // 2 + 1].bitcast(BF16)[:, 0:KSW]]
        QS = [sb(f"QS{n}", [128, HQ], BF16) for n in range(2)]
        Qb = [sb(f"Qb{n}", [128, H, S], BF16) for n in range(2)]
        Vp = [sb(f"Vp{n}", [128, T, NPAIR, PW]) for n in range(2)]
        P = [sb(f"P{n}", [128, HQ]) for n in range(2)]
        mx = sb("mx", [128, CH, KC])
        mneg = sb("mneg", [128, CH], BF16)
        O = sb("O", [128, 2 * PAIRW])
        rden = sb("rden", [128, 2 * PAIRW])
        On = sb("On", [128, 2 * PAIRW])
        gw_sb = sb("gw_sb", [128, E])
        b1_sb = [sb(f"b1_{n}", [128, FC]) for n in range(2)]
        b2_sb = sb("b2_sb", [ND * E, ND, D])
        w1_sb = [wgu[:, n, :] for n in range(2)]
        w2_sb = [silu[:, n, :].rearrange("p (c d) -> p c d", c=FC) for n in range(2)]
        pr = sb("pr", [128, NT, E])
        pc = sb("pc", [128, NT, E])
        ph = sb("ph", [128, NT, E])
        pg = sb("pg", [128, NT, E])
        pm = sb("pm", [128, NT])
        pd = sb("pd", [128, NT])
        pgT = sb("pgT", [ND * E, 128])
        pgd = sb("pgd", [128, ND, E])
        xd = t0[:, 0:ND, :]

        ps = ctx.enter_context(nc.psum_tensor("ps", [128, 8, 512], F32))
        ps2 = ps[:, :, :].rearrange("p b n -> p (b n)")

        def bank4(k):
            return ps2[:, 512 * k:512 * k + 1024].rearrange("p (t d) -> p t d", t=NT)

        mixed = nc.dram_tensor("mixed", (B, H * S, DK), F32, kind="Internal").ap()

        x_flat = nc.dram_tensor("x_flat", (B * S, D), F32, kind="Internal").ap()
        pg_flat = nc.dram_tensor("pg_flat", (B * S, E), F32, kind="Internal").ap()

        block = ctx.enter_context(nc.Block())

        def bc(ap, n, shape):
            return ap.unsqueeze(n).broadcast_to(shape)

        @block.sync
        def _(sp):
            sp.dma_start(x[:], xh).then_inc(sem("x_in"), 16)
            sp.dma_start(ident[:], ident_in).then_inc(sem("x_in"), 16)
            sp.dma_start(wkv[:], wkv0).then_inc(sem("wkv_in"), 16)
            sp.dma_start(row[:], rows).then_inc(sem("setup_in"), 16)
            sp.dma_start(wq0_sb[:], wq0).then_inc(sem("setup_in"), 16)
            sp.dma_start(em[0:TK, :], m0).then_inc(sem("setup_in"), 16)
            sp.dma_start(hmask[:], hmask_in).then_inc(sem("setup_in"), 16)
            sp.dma_start(gate_sb[:], gates).then_inc(sem("setup_in"), 16)

            def load_ctx0(b, par, wait):
                if wait:
                    sp.wait_ge(sem("y_ready"), NG * (b - 1))
                sp.dma_start(cT[par][:], ctxT[:, bass.ds(b * S2, S2)]).then_inc(sem(f"ctx0_in{par}"), 16)

            def pair0(i):
                for par in range(2):
                    load_ctx0(2 * i + par, par, not (isinstance(i, int) and i == 0))

            pair0(0)
            with sp.Fori(1, B // 2) as i:
                pair0(i)
            for dst, src in ((dense_sb[:], dense0), (wgu[:, 0, :], wg0), (wgu[:, 1, :], wu0), (wdn[:], wd0),
                             (mi[0:TK, :], m1), (hmask1[:], hmask1_in), (pmask[:], pmask_in),
                             (bv_sb[:], bv), (bq_sb[:], bq), (bk_sb[:], bk), (wq1_sb[:], wq1), (wk1_sb[:], wk1),
                             (wv1_sb[:], wv1), (wo1_sb[:], wo1), (den_sel[:], den_sel_in), (rank[:], rank_in),
                             (gw_sb[:], gatew), (b2_sb[:], b2)):
                sp.dma_start(dst, src).then_inc(sem("late_in"), 16)

            for par in range(2):
                sp.wait_ge(sem("y_ready"), NG * (B - 1 + par))
                sp.dma_start(cT[par][:], ctxT[:, S2 * par:S2 * par + S2]).then_inc(sem(f"ctx1_in{par}"), 16)

            sp.wait_ge(sem("att0_ready"), 1)
            for par in range(2):
                for i in range(NT):
                    sp.dma_start(mixed[2 * i + par].rearrange("(h s) e -> s h e", h=H),
                                 att[HALF * par:HALF * par + S, i, :].rearrange("s (h e) -> s h e", h=H)
                                 ).then_inc(sem("mix_out"), 16)
            sp.wait_ge(sem("mix_out"), 16 * B)
            for par in range(2):
                sp.dma_start(att[HALF * par:HALF * par + S, :, :],
                             mixed.rearrange("(i two) (s j) e -> two s i (j e)", two=2, s=S)[par]
                             ).then_inc(sem("mix_in"), 16)

            def load_ctx1(w, par):
                sp.wait_ge(sem("side_ready"), filled(w - 1, "V2"))
                sp.dma_start(cT[par][:], ctxT[:, bass.ds((w + 2) * S2, S2)]).then_inc(sem(f"ctx1_in{par}"), 16)

            def stack(b, par, first_pair):
                if not first_pair:
                    sp.wait_ge(sem("sc_ready"), T * (b - 1))
                sp.wait_ge(sem("kp3_ready"), b + 1)
                for j, part in enumerate(KEY_PART):
                    sp.dma_start(KS[par][ROWS * j:ROWS * j + ROWS, 0:NPAIR * S2].rearrange("r (p n) -> r p n", p=NPAIR),
                                 KP[par][part][:]).then_inc(sem(f"stacked{par}"), 16)
                sp.wait_ge(sem("q_ready"), b + 1)
                for j, part in enumerate(QUERY_PART):
                    sp.dma_start(QS[par][ROWS * j:ROWS * j + ROWS, :].rearrange("r (p n) -> r p n", p=NPAIR),
                                 QD[par][part][:].rearrange("p k s -> p (k s)")).then_inc(sem(f"stacked{par}"), 16)

            def pair1(i):
                fixed = isinstance(i, int)
                for par in range(2):
                    w = 2 * i + par
                    if not (fixed and w + 2 >= B):
                        load_ctx1(w, par)
                    if not (fixed and w == B - 1):
                        if fixed and w == 0:
                            sp.wait_ge(sem("ks1_ready"), 1)
                        stack(w + 1, 1 - par, fixed and w == 0)

            stack(0, 0, True)
            in_pairs(sp, pair1, B // 2)

            def experts(i):
                for par in range(2):
                    e = 2 * i + par
                    first = isinstance(i, int) and i == 0
                    if not first:
                        sp.wait_ge(sem("h_ready"), 8 * (e - 1))
                    sp.dma_start(w1_sb[par], w1[:, bass.ds(e * INNER, INNER)]).then_inc(sem(f"w1_in{par}"), 16)
                    sp.dma_start(b1_sb[par][:], b1[:, bass.ds(e * FC, FC)]).then_inc(sem(f"b1_in{par}"), 16)
                    if not first:
                        sp.wait_ge(sem("down_ready"), 2 * (e - 1))
                    sp.dma_start(w2_sb[par], w2[:, bass.ds(e * INNER, INNER)]).then_inc(sem(f"w2_in{par}"), 16)

            experts(0)
            for ready, count, src, flat, dst, name in (("ln_done", 3, x, x_flat, xd, "xd"),
                                                       ("pg_ready", 1, pg, pg_flat, pgd[:], "pgd")):
                sp.wait_ge(sem(ready), count)
                for par in range(2):
                    sp.dma_start(flat.rearrange("(i two s) d -> two s i d", two=2, s=S)[par],
                                 src[HALF * par:HALF * par + S, :, :]).then_inc(sem(name + "_out"), 16)
                sp.wait_ge(sem(name + "_out"), 32)
                sp.dma_start(dst, flat.rearrange("(t p) d -> p t d", p=128)).then_inc(sem(name + "_in"), 16)
            with sp.Fori(1, E // 2) as i:
                experts(i)
            sp.wait_ge(sem("moe_done"), 2 * E)
            sp.dma_start(out.rearrange("b s d -> (b s) d").rearrange("(t p) d -> p t d", p=128),
                         xd).then_inc(sem("out_done"), 16)
            sp.wait_ge(sem("out_done"), 16)

        LATE = 18 * 16

        @block.tensor
        def _(pe):
            def transpose_tiles(src, bank, done):
                for t in range(NT):
                    ins = nc.tensor.transpose(bank4(bank)[:, t, :], src[:, t, :], ident[:])
                    if t % 4 == 3:
                        ins.then_inc(sem(done), 1)

            def project_tiles(lhs, ready, w, bank, done):
                for t in range(NT):
                    if t % 4 == 0:
                        pe.wait_ge(sem(ready), t // 4 + 1)
                    ins = nc.tensor.matmul(bank4(bank)[:, t, :], lhs[:, 128 * t:128 * t + 128], w,
                                           start=True, stop=True)
                ins.then_inc(sem(done), 1)

            pe.wait_ge(sem("x_in"), 32)
            pe.wait_ge(sem("ln_done"), 1)
            transpose_tiles(xn, 0, "xT0_ps")
            pe.wait_ge(sem("setup_in"), 80)
            project_tiles(xT, "xT0_ready", wq0_sb[:], 2, "q0_ps")

            def y_group(b, par, g, first):
                n = NG * b + g
                if g == 0:
                    pe.wait_ge(sem(f"ctx0_in{par}"), loads(b, par))
                if first:
                    if g == 0:
                        pe.wait_ge(sem("wkv_ready"), 1)
                    if g == 2:
                        pe.wait_ge(sem("q0T_ready"), 2)
                else:
                    pe.wait_ge(sem("kn_ready"), n - 2)
                    pe.wait_ge(sem("vn_ready"), n - 2)
                for t in range(GT):
                    c0 = (GT * g + t) * TK
                    ins = nc.tensor.matmul(ps2[0:TK, 1024 * g + 256 * t:1024 * g + 256 * t + 256],
                                           cT[par][:, c0:c0 + TK], wkv[:].rearrange("p k d -> p (k d)"),
                                           start=True, stop=True)
                ins.then_inc(sem("y_ready"), 1)

            def kv_group(b, par, g, first):
                n = NG * b + g
                if g == 0 and not first:
                    pe.wait_ge(sem("kv_read"), b - 1)
                pe.wait_ge(sem("kp_ready"), n + 1)
                pe.wait_ge(sem("vn_ready"), n + 1)
                pe.wait_ge(sem("emc_ready"), n + 1)
                s6 = NG * par + g
                for t in range(GT):
                    ins = nc.tensor.matmul(ps[:, 6 + par, 0:D + 2], KN[0:TK, s6, t, :], VN[0:TK, s6, t, :],
                                           start=(g == 0 and t == 0), stop=(g == NG - 1 and t == GT - 1))
                ins.then_inc(sem("kv_done"), 1)

            pe.sem_inc(sem("kv_done"), SLOTS)
            y_group(0, 0, 0, True)
            pe.wait_ge(sem("q0_ready"), 1)
            transpose_tiles(t0, 4, "q0T_ps")
            for g in range(1, NG):
                y_group(0, 0, g, True)

            def pair(i):
                first = isinstance(i, int) and i == 0
                last = isinstance(i, int) and i == B // 2 - 1
                for g in range(NG):
                    y_group(2 * i + 1, 1, g, False)
                    kv_group(2 * i, 0, g, first)
                for g in range(NG):
                    if not last:
                        y_group(2 * i + 2, 0, g, False)
                    kv_group(2 * i + 1, 1, g, first)

            in_pairs(pe, pair, B // 2)

            def fill(w, unit, b, par):
                bank = bank_of(w, unit)
                before = emptied(w, unit) - 1
                if not isinstance(before, int) or before > 0:
                    pe.wait_ge(sem(free_of(w, unit)), before)
                if unit[0] == "K":
                    k = int(unit[1])
                    if k == 0:
                        if isinstance(b, int) and b == 0:
                            pe.wait_ge(sem("late_in"), LATE)
                        pe.wait_ge(sem(f"ctx1_in{par}"), loads(b, par))
                    ins = nc.tensor.matmul(ps[:, bank, 0:KCW], wk1_sb[:], cT[par][:, KCW * k:KCW * k + KCW],
                                           start=True, stop=True)
                elif unit[0] == "V":
                    g = int(unit[1])
                    for t in range(GT):
                        c0 = (GT * g + t) * TK
                        ins = nc.tensor.matmul(ps[0:TK, bank, 128 * t:128 * t + 128], cT[par][:, c0:c0 + TK],
                                               wv1_sb[:], start=True, stop=True)
                elif unit[:2] == "MX":
                    c, k = divmod(int(unit[2:]), KC)
                    if c == 0 and k == 0:
                        pe.wait_ge(sem("qb_ready"), b + 1)
                        pe.wait_ge(sem("kp1_ready"), KC * (b + 1))
                    q = Qb[par][:].rearrange("p h s -> p (h s)")
                    ins = nc.tensor.matmul(ps[:, bank, 0:KCW], q[:, 128 * c:128 * c + 128],
                                           KP[par][0][:, KCW * k:KCW * k + KCW], start=True, stop=True)
                elif unit == "SH":
                    pe.wait_ge(sem("mneg_ready"), b + 1)
                    for c in range(CH):
                        for k in range(2):
                            lo, hi = max(128 * c, HQ2 * k), min(128 * c + 128, HQ2 * k + HQ2)
                            if lo < hi:
                                r = ONES - 32 * k
                                ins = nc.tensor.matmul(ps[r:r + 1, bank, lo - HQ2 * k:hi - HQ2 * k],
                                                       mneg[:, c:c + 1], identb[:, lo - 128 * c:hi - 128 * c],
                                                       start=True, stop=True)
                elif unit == "DEN":
                    pe.wait_ge(sem("o_ready"), b + 1)
                    ins = nc.tensor.matmul(ps[:, bank, 0:2 * PAIRW], den_sel[:], O[:], start=True, stop=True)
                else:
                    pe.wait_ge(sem("on_ready"), b + 1)
                    for c in range(2):
                        for k in range(2):
                            lhs = On[:, PAIRW * c + S * k:PAIRW * c + S * k + S]
                            ins = nc.tensor.matmul(ps[HALF * par:HALF * par + S, bank, 0:D], lhs,
                                                   wo1_sb[:, 2 * c + k, :], start=(c + k == 0), stop=(c + k == 2))
                ins.then_inc(sem(kind(unit) + "_ready"), 1)

            pe.wait_ge(sem("kv_read"), B)
            for b in range(B):
                t, r = b // 2, HALF * (b % 2)
                ins = nc.tensor.matmul(ps[r:r + HALF, t // 3, KVW * (t % 3):KVW * (t % 3) + KVW],
                                       qT[:, HALF * b:HALF * b + HALF], kvall[:, b, :], start=True, stop=True)
            ins.then_inc(sem("nd_ready"), 1)
            pe.wait_ge(sem("wabs_ready"), 1)
            nc.tensor.matmul(ps[:, 3, 0:3], onesf[:], wabs[:], start=True, stop=True).then_inc(sem("wsum_ps"), 1)
            pe.wait_ge(sem("kept_ready"), 1)
            nc.tensor.matmul(ps[:, 0, 0:B], onesf[0:TK, :], kept[0:TK, :], start=True,
                             stop=True).then_inc(sem("kept_ps"), 1)
            for unit in EARLY[0:3]:
                fill(-1, unit, 0, 0)
            pe.wait_ge(sem("mix_in"), 32)
            transpose_tiles(att, 4, "attT_ps")
            project_tiles(xT, "attT_ready", dense_sb[:], 1, "dense_ps")
            for unit in EARLY[3:6]:
                fill(-1, unit, 0, 0)

            pe.wait_ge(sem("xq_ready"), 1)
            for t in range(NT):
                ins = nc.tensor.transpose(ps[:, 4, :].bitcast(BF16)[:, 128 * t:128 * t + 128], xqb[:, t, :], identb[:])
            ins.then_inc(sem("xqT_ps"), 1)
            pe.wait_ge(sem("side_free"), emptied(-1, "V2"))
            fill(-1, EARLY[6], 1, 1)
            pe.wait_ge(sem("xqT_ready"), 1)
            pe.wait_ge(sem("wq_ready"), 1)
            for t in range(NT):
                for k in range(2):
                    if t >= 2:
                        pe.wait_ge(sem("hid_ready"), t - 1)
                    ins = nc.tensor.matmul(ps[:, 2 * k + t % 2, :], xqT[:, 128 * t:128 * t + 128], wgub[:, k, :],
                                           start=True, stop=True)
                ins.then_inc(sem("gu_ps"), 1)
            fill(-1, EARLY[7], 1, 1)
            for t in range(NT):
                pe.wait_ge(sem("hq_ready"), t + 1)
                if t >= 2:
                    pe.wait_ge(sem("hqT_ready"), t - 1)
                for c in range(FC):
                    ins = nc.tensor.transpose(ps[:, 4 + t % 2, :].bitcast(BF16)[:, 128 * c:128 * c + 128],
                                              hqb[:, t, 128 * c:128 * c + 128], identb[:])
                ins.then_inc(sem("hqT_ps"), 1)
            for t in range(NT):
                pe.wait_ge(sem("hqT_ready"), t + 1)
                for c in range(FC):
                    ins = nc.tensor.matmul(bank4(0)[:, t, :], hqT[:, t, c, :], wdnb[:, c, :],
                                           start=(c == 0), stop=(c == FC - 1), skip_group_check=True)
            ins.then_inc(sem("ffn_ps"), 1)
            fill(-1, EARLY[8], 1, 1)

            pe.wait_ge(sem("ln_done"), 2)
            transpose_tiles(xn, 0, "xT1_ps")
            for k in range(2):
                pe.wait_ge(sem("xT1_ready"), k + 1)
                ins = nc.tensor.matmul(ps[:, 2 + k, :], wq1_sb[:], xT[:, 512 * k:512 * k + 512], start=True,
                                       stop=True).then_inc(sem("q1_ps"), 1)

            def scores(b, par, t, k, first):
                n = b * T + t
                if t == 0 and k == 0:
                    pe.wait_ge(sem(f"stacked{par}"), loads(b, par, 2 * STACK))
                    pe.wait_ge(sem(free_of(b - 1, "SH")), emptied(b - 1, "SH"))
                if k == 0 and not (first and t < 2):
                    pe.wait_ge(sem("p_ready"), n - 1)
                for p in range(4 * k, 4 * k + 4):
                    c0 = S2 * p + TK * t
                    ins = nc.tensor.matmul(ps[:, 2 * (t % 2) + k, PAIRW * (p % 4):PAIRW * (p % 4) + PAIRW],
                                           KS[par][:, c0:c0 + 128], QS[par][:, PAIRW * p:PAIRW * p + PAIRW],
                                           start=True, stop=True)
                if k == 1:
                    ins.then_inc(sem("sc_ready"), 1)

            def weigh(b, par, t, first):
                n = b * T + t
                pe.wait_ge(sem("p_ready"), n + 1)
                if t == 0 and not (first and par == 0):
                    pe.wait_ge(sem("o_ready"), b)
                for p in range(NPAIR):
                    r, c = PW * (p % 4), PAIRW * (p // 4)
                    ins = nc.tensor.matmul(ps[r:r + PW, 7, c:c + PAIRW], Vp[par][0:TK, t, p, :],
                                           P[t % 2][0:TK, PAIRW * p:PAIRW * p + PAIRW],
                                           start=(t == 0 and p < 4), stop=(t == T - 1), skip_group_check=True)
                ins.then_inc(sem("pv_done"), 1)

            def window(w, par, first_pair):
                def unit_at(t, place):
                    unit = PLACES[t][place]
                    if unit in units(w):
                        b = w - 1 if unit in ENDS else w + 2 if unit[0] == "K" else w + 1
                        fill(w, unit, b, par if unit[0] == "K" else 1 - par)

                first = first_pair and par == 0
                for t in range(T):
                    scores(w, par, t, 0, first)
                    unit_at(t, 0)
                    scores(w, par, t, 1, first)
                    unit_at(t, 1)
                    if t > 0:
                        weigh(w, par, t - 1, first_pair)
                    elif not first:
                        weigh(w - 1, 1 - par, T - 1, first_pair)
                    unit_at(t, 2)

            pe.wait_ge(sem("filled"), 1)
            for unit in MXS + ["SH"]:
                fill(-1, unit, 0, 0)

            def pair1(i):
                fixed = isinstance(i, int)
                for par in range(2):
                    window(2 * i + par, par, fixed and i == 0)

            in_pairs(pe, pair1, B // 2)
            weigh(B - 1, 1, T - 1, False)
            fill(B, "DEN", B - 1, 1)
            fill(B, "WO", B - 1, 1)

            pe.wait_ge(sem("ln_done"), 3)
            transpose_tiles(xn, 0, "xT2_ps")
            for t in range(NT):
                if t % 4 == 0:
                    pe.wait_ge(sem("xT2_ready"), t // 4 + 1)
                ins = nc.tensor.matmul(ps[:, 6, E * t:E * t + E], xT[:, 128 * t:128 * t + 128], gw_sb[:],
                                       start=True, stop=True)
            ins.then_inc(sem("logit_ps"), 1)

            def up(e, par, first):
                pe.wait_ge(sem(f"w1_in{par}"), loads(e, par))
                xv = xT[:].rearrange("p (b q) -> p b q", q=HALF)
                for c in range(FC):
                    for k in range(2):
                        u = 2 * c + k
                        if not (first and u < 4):
                            pe.wait_ge(sem("h_ready"), 8 * e + u - 3)
                        nc.tensor.matmul(ps[:, u % 4, 0:8 * S], w1_sb[par][:, 128 * c:128 * c + 128],
                                         xv[:, 8 * k:8 * k + 8, 0:S], start=True, stop=True).then_inc(sem("up_ps"), 1)

            def down(e, par, first):
                pe.wait_ge(sem(f"w2_in{par}"), loads(e, par))
                pe.wait_ge(sem("h_ready"), 8 * e + 8)
                for k in range(2):
                    if not first:
                        pe.wait_ge(sem("moe_done"), 2 * e + k - 3)
                    for t in range(min(4, ND - 4 * k)):
                        for c in range(FC):
                            lhs = hT[:, par, c, 512 * k + 128 * t:512 * k + 128 * t + 128]
                            ins = nc.tensor.matmul(ps[:, 4 + 2 * par + k, 128 * t:128 * t + 128], lhs,
                                                   w2_sb[par][:, c, :], start=(c == 0), stop=(c == FC - 1),
                                                   skip_group_check=True)
                    ins.then_inc(sem("down_ready"), 1)

            def second_biases():
                pe.wait_ge(sem("pgd_in"), 16)
                pe.wait_ge(sem("pg_ready"), 1)
                nc.tensor.transpose(ps[0:ND * E, 7, 0:128], pgd[:].rearrange("p t e -> p (t e)"),
                                    ident[:]).then_inc(sem("pgT_ps"), 1)
                pe.wait_ge(sem("pgT_ready"), 1)
                for k in range(2):
                    ins = nc.tensor.matmul(ps[:, 6 + k, 0:128 * min(4, ND - 4 * k)], pgT[:], b2_sb[:, 4 * k:min(ND, 4 * k + 4), :],
                                           start=True, stop=True)
                ins.then_inc(sem("b2_ps"), 1)

            up(0, 0, True)

            def pair2(i):
                fixed = isinstance(i, int)
                first, last = fixed and i == 0, fixed and i == E // 2 - 1
                up(2 * i + 1, 1, False)
                if first:
                    second_biases()
                down(2 * i, 0, first)
                if not last:
                    up(2 * i + 2, 0, False)
                if first:
                    pe.wait_ge(sem("b2_done"), 1)
                down(2 * i + 1, 1, first)

            in_pairs(pe, pair2, E // 2)

        @block.scalar
        def _(act):
            def ln_std(n, eps):
                act.wait_ge(sem("ln_var"), n)
                nc.scalar.activation(sd[:], mv[:, :, 1], ACT.Sqrt, bias=eps[:]).then_inc(sem("ln_std"), 1)

            def copy_halves(dst, bank, done, ready):
                for k in range(2):
                    act.wait_ge(sem(done), k + 1)
                    nc.scalar.copy(dst[:, 512 * k:512 * k + 512], ps[:, bank + k, :]).then_inc(sem(ready), 1)

            act.wait_ge(sem("setup_done"), 1)
            ln_std(1, eps_ln)
            copy_halves(xT, 0, "xT0_ps", "xT0_ready")
            ln_std(2, eps_in)
            copy_halves(qT, 4, "q0T_ps", "q0T_ready")

            def square(b, par, g, first_pair):
                n, k = NG * b + g, NG * par + g
                act.wait_ge(sem("y_ready"), n + 1)
                if not (first_pair and k < 2):
                    act.wait_ge(sem("ss_ready"), n - 1)
                nc.scalar.activation(SQ[0:TK, k % 2, :], ps2[0:TK, 1024 * g:1024 * g + 1024], ACT.Square,
                                     scale=float(D) ** -0.5).then_inc(sem("sq_ready"), 1)

            def deviation(n, k):
                act.wait_ge(sem("ss_ready"), n + 1)
                nc.scalar.activation(sdk[0:TK, k % 2, :], ss[0:TK, k % 2, :], ACT.Sqrt,
                                     bias=eps_in[0:TK, :]).then_inc(sem("sdk_ready"), 1)

            def values(n, k):
                act.wait_ge(sem("kn_ready"), n + 1)
                act.wait_ge(sem("kv_done"), n + 1)
                for t in range(GT):
                    c0 = 1024 * (k % NG) + 256 * t + D
                    ins = nc.scalar.activation(VN[0:TK, k, t, 0:D], ps2[0:TK, c0:c0 + D], ACT.Copy,
                                               scale=wv[0:TK, k % 2, t:t + 1])
                ins.then_inc(sem("vn_ready"), 1)

            def pair(i):
                first = isinstance(i, int) and i == 0
                for par in range(2):
                    for g in range(NG):
                        k = NG * par + g
                        n = NG * (2 * i + par) + g
                        square(2 * i + par, par, g, first)
                        if not (first and k < 1):
                            values(n - 1, (k - 1) % SLOTS)
                        deviation(n, k)

            in_pairs(act, pair, B // 2)
            values(NG * B - 1, SLOTS - 1)
            act.wait_ge(sem("setup_in"), 80)
            nc.scalar.activation(th[:], gate_sb[:], ACT.Tanh).then_inc(sem("th_ready"), 1)

            def values1(w, g, b, par):
                act.wait_ge(sem("side_ready"), filled(w, f"V{g}"))
                if g == 0 and not (isinstance(b, int) and b < 2):
                    act.wait_ge(sem("pv_done"), T * (b - 1))
                nc.scalar.copy(Vp[par][0:TK, GT * g:GT * g + GT, :, 1:1 + 2 * DK],
                               ps[0:TK, bank_of(w, f"V{g}"), :].rearrange("p (t j d) -> p t j d", t=GT, j=NPAIR)
                               ).then_inc(sem("side_free"), 1)

            def key_part1(w, unit, b, par):
                k = int(unit[1])
                act.wait_ge(sem("side_ready"), filled(w, unit))
                nc.scalar.activation(KP[par][0][:, KCW * k:KCW * k + KCW], ps[:, bank_of(w, unit), 0:KCW],
                                     ACT.Identity, bias=bk_sb[:]).then_inc(sem("kp1_ready"), 1)

            def key_part2(w, prime, b, par):
                act.wait_ge(sem("side_free"), emptied(w, "K2" + prime))
                nc.scalar.copy(KP[par][1][:], krest).then_inc(sem("kp2_ready"), 1)

            act.wait_ge(sem("filled"), 1)
            for unit in EARLY[0:3]:
                key_part1(-1, unit, 0, 0)
            key_part2(-1, "", 0, 0)
            copy_halves(xT, 4, "attT_ps", "attT_ready")
            values1(-1, 0, 0, 0)
            ln_std(3, eps_in)
            values1(-1, 1, 0, 0)
            values1(-1, 2, 0, 0)
            ln_std(4, eps_ln)
            act.wait_ge(sem("xqT_ps"), 1)
            nc.scalar.copy(xqT[:], ps[:, 4, :].bitcast(BF16)).then_inc(sem("xqT_ready"), 1)
            key_part1(-1, EARLY[6], 1, 1)
            act.wait_ge(sem("cgu_ready"), 1)
            for t in range(NT):
                act.wait_ge(sem("gu_ps"), t + 1)
                if t >= 2:
                    act.wait_ge(sem("hid_ready"), t - 1)
                nc.scalar.activation(silu[:, t % 2, :], ps[:, t % 2, :], ACT.Silu,
                                     scale=cg[:, t:t + 1]).then_inc(sem("silu_ready"), 1)
            key_part1(-1, EARLY[7], 1, 1)
            for t in range(NT):
                act.wait_ge(sem("hqT_ps"), t + 1)
                nc.scalar.copy(hqT[:, t, :, :].rearrange("p c n -> p (c n)"),
                               ps[:, 4 + t % 2, :].bitcast(BF16)[:, 0:INNER]).then_inc(sem("hqT_ready"), 1)
            key_part1(-1, EARLY[8], 1, 1)
            ln_std(5, eps_ln)
            copy_halves(xT, 0, "xT1_ps", "xT1_ready")
            for k in range(2):
                act.wait_ge(sem("q1_ps"), k + 1)
                nc.scalar.activation(qT[:, 512 * k:512 * k + 512], ps[:, 2 + k, :], ACT.Identity,
                                     bias=bq_sb[:]).then_inc(sem("q1T_ready"), 1)
            key_part2(-1, "'", 1, 1)

            def exponentials(b, par, t, first):
                n = b * T + t
                act.wait_ge(sem("sc_ready"), n + 1)
                if not (first and t < 2):
                    act.wait_ge(sem("pv_done"), n - 1)
                act.wait_ge(sem("kb_ready"), 1)
                src = ps[0:TK, 2 * (t % 2):2 * (t % 2) + 2, 0:HQ2]
                nc.scalar.activation(P[t % 2][0:TK, :].rearrange("p (k n) -> p k n", k=2), src, ACT.Exp,
                                     scale=kscale[0:TK, bass.ds(n, 1)],
                                     bias=kbias[0:TK, bass.ds(n, 1)]).then_inc(sem("p_ready"), 1)

            def take_sums(b):
                act.wait_ge(sem("pv_done"), T * (b + 1))
                if not (isinstance(b, int) and b == 0):
                    act.wait_ge(sem("on_ready"), b)
                nc.scalar.copy(O[:], ps[:, 7, 0:2 * PAIRW]).then_inc(sem("o_ready"), 1)

            def pair1(i):
                fixed = isinstance(i, int)
                for par in range(2):
                    w = 2 * i + par
                    has = units(w)
                    for t in range(T):
                        exponentials(w, par, t, fixed and w == 0)
                        if t == 0 and "DEN" in has:
                            take_sums(w - 1)
                        unit = PLACES[t][2]
                        if t == 10 and "K2" in has:
                            key_part2(w, "", w + 2, par)
                        elif unit not in has:
                            continue
                        elif unit[0] == "V":
                            values1(w, int(unit[1]), w + 1, 1 - par)
                        elif unit[0] == "K":
                            key_part1(w, unit, w + 2, par)

            in_pairs(act, pair1, B // 2)
            take_sums(B - 1)

            ln_std(6, eps_ln)
            copy_halves(xT, 0, "xT2_ps", "xT2_ready")
            act.wait_ge(sem("logit_ready"), 1)
            nc.scalar.activation(pr[:], pr[:], ACT.Exp).then_inc(sem("pexp_ready"), 1)

            def inner(e, par, first_pair):
                act.wait_ge(sem(f"b1_in{par}"), loads(e, par))
                for u in range(8):
                    c, k = divmod(u, 2)
                    act.wait_ge(sem("up_ps"), 8 * e + u + 1)
                    if u == 0 and not first_pair:
                        act.wait_ge(sem("down_ready"), 2 * (e - 1))
                    nc.scalar.activation(hT[:, par, c, 8 * S * k:8 * S * k + 8 * S], ps[:, u % 4, 0:8 * S],
                                         ACT.Gelu_apprx_tanh,
                                         bias=b1_sb[par][:, c:c + 1]).then_inc(sem("h_ready"), 1)

            def pair2(i):
                for par in range(2):
                    inner(2 * i + par, par, isinstance(i, int) and i == 0)

            in_pairs(act, pair2, E // 2)

        @block.gpsimd
        def _(pool):
            for n in range(2):
                nc.gpsimd.memset(Vp[n][:], 0.0)
            for n in range(2):
                nc.gpsimd.memset(QS[n][:], 0.0)
            nc.gpsimd.memset(KS[0], 1.0).then_inc(sem("zeroed"), 1)
            pool.wait_ge(sem("zeroed"), 1)
            for n in range(2):
                ins = nc.gpsimd.memset(Vp[n][:, :, :, 0:1], 1.0)
            ins.then_inc(sem("filled"), 1)

            def keys(b, par, g, first):
                n, k = NG * b + g, NG * par + g
                pool.wait_ge(sem("kv_done"), n + 1)
                pool.wait_ge(sem("em_ready"), 1)
                nc.gpsimd.tensor_copy(VN[0:TK, k, :, D:D + 2],
                                      emcat[0:TK, bass.ds(b * T + GT * g, GT), :]).then_inc(sem("emc_ready"), 1)
                pool.wait_ge(sem("kn_ready"), n + 1)
                kn = KN[0:TK, k, :, :]
                nc.gpsimd.tensor_tensor(kn, kn, bc(row[0:TK, GAMMA, :], 1, [TK, GT, D]),
                                        ALU.mult).then_inc(sem("kg_ready"), 1)
                pool.wait_ge(sem("kg_ready"), n + 1)
                nc.gpsimd.tensor_tensor(kn, kn, bc(row[0:TK, BETA, :], 1, [TK, GT, D]),
                                        ALU.add).then_inc(sem("kb0_ready"), 1)

            def pair(i):
                for par in range(2):
                    for g in range(NG):
                        keys(2 * i + par, par, g, isinstance(i, int) and i == 0)

            in_pairs(pool, pair, B // 2)

            def key_part3(b, par):
                pool.wait_ge(sem("kp2_ready"), b + 1)
                nc.gpsimd.tensor_tensor(KP[par][2][:], krest, KP[par][1][:], ALU.subtract).then_inc(sem("kp3_ready"), 1)

            def queries(b, par, first_pair):
                if not first_pair:
                    pool.wait_ge(sem("aux_ready"), filled(b - 3, MXS[-1]))
                    pool.wait_ge(sem(f"stacked{par}"), loads(b - 2, par, 2 * STACK))
                nc.gpsimd.tensor_tensor(Qb[par][:], bc(QP[0][:, bass.ds(b * HALF, S)], 1, [128, H, S]),
                                        bc(hmask1[:], 2, [128, H, S]), ALU.mult).then_inc(sem("qb_ready"), 1)
                pool.wait_ge(sem("qp_ready"), 1)
                for k in range(3):
                    ins = nc.gpsimd.tensor_tensor(QD[par][k][:], bc(QP[k][:, bass.ds(b * HALF, S)], 1, [128, 2, S]),
                                                  bc(pmask[:], 2, [128, 2, S]), ALU.mult)
                ins.then_inc(sem("q_ready"), 1)

            key_part3(0, 0)
            pool.wait_ge(sem("hqT_ps"), NT)
            pool.wait_ge(sem("hq_ready"), NT)
            nc.gpsimd.memset(KS[1], 1.0).then_inc(sem("ks1_ready"), 1)
            pool.wait_ge(sem("qp1_ready"), 1)
            for b in range(2):
                queries(b, b, True)
            key_part3(1, 1)

            def pair1(i):
                for par in range(2):
                    b = 2 * i + par + 2
                    queries(b, par, False)
                    key_part3(b, par)

            pair1(0)
            with pool.Fori(1, B // 2 - 1) as i:
                pair1(i)

        @block.vector
        def _(dve):
            v = nc.vector
            steps = [0]

            def step(ins):
                steps[0] += 1
                ins.then_inc(sem("dve_step"), 1)
                dve.wait_ge(sem("dve_step"), steps[0])

            def layernorm(n, src, dst, signal=None):
                for t in range(NT):
                    ins = v.bn_stats(stats[:, t, :], src[:, t, :])
                step(ins)
                for t in range(NT):
                    ins = v.bn_aggr(mv[:, t, :], stats[:, t, :])
                ins.then_inc(sem("ln_var"), 1)
                dve.wait_ge(sem("ln_std"), n)
                step(v.reciprocal(rstd[:], sd[:]))
                for t in range(NT):
                    ins = v.tensor_scalar(dst[:, t, :], src[:, t, :], mv[:, t, 0:1], rstd[:, t:t + 1],
                                          ALU.subtract, ALU.mult)
                if signal:
                    ins.then_inc(sem(signal), 1)
                else:
                    step(ins)

            def rows_of(k):
                return bc(row[:, k, :], 1, [128, NT, D])

            v.memset(onesf[:], 1.0)
            v.memset(eps_ln[:], EPS_LN)
            v.memset(eps_in[:], EPS_IN)
            v.memset(att[:], 0.0).then_inc(sem("setup_done"), 1)

            dve.wait_ge(sem("x_in"), 32)
            layernorm(1, x, xn, "ln_done")
            step(v.tensor_copy(identb[:], ident[:]))
            dve.wait_ge(sem("wkv_in"), 16)
            step(v.tensor_reduce(wkv_mean[:], wkv[:], AX.X, ALU.add, negate=True))
            step(v.tensor_scalar(wkv_mean[:], wkv_mean[:], 1.0 / D, None, ALU.mult))
            for k in range(2):
                ins = v.tensor_scalar(wkv[:, k, :], wkv[:, k, :], wkv_mean[:, k:k + 1], None, ALU.add)
            ins.then_inc(sem("wkv_ready"), 1)
            dve.wait_ge(sem("setup_in"), 80)
            step(v.tensor_tensor(em2[0:TK, :], em[0:TK, :], em[0:TK, :], ALU.mult))
            v.tensor_copy(emcat[0:TK, :, 0], em2[0:TK, :])
            v.tensor_copy(emcat[0:TK, :, 1], em[0:TK, :]).then_inc(sem("em_ready"), 1)
            hm3 = bc(hmask[:], 2, [128, H, DK])
            v.tensor_tensor(gmask[:].rearrange("p (h d) -> p h d", h=H),
                            row[:, GAMMA, :].rearrange("p (h d) -> p h d", h=H), hm3, ALU.mult)
            step(v.tensor_tensor(bmask[:].rearrange("p (h d) -> p h d", h=H),
                                 row[:, BETA, :].rearrange("p (h d) -> p h d", h=H), hm3, ALU.mult))
            dve.wait_ge(sem("q0_ps"), 1)
            layernorm(2, bank4(2), t0)
            step(v.tensor_tensor(t0[:], t0[:], rows_of(GAMMA), ALU.mult))
            step(v.tensor_tensor(t0[:], t0[:], rows_of(BETA), ALU.add))
            v.tensor_scalar(t0[:], t0[:], 0.0, EPS_IN, ALU.max, ALU.add).then_inc(sem("q0_ready"), 1)

            def norms(n, k):
                dve.wait_ge(sem("sq_ready"), n + 1)
                v.tensor_reduce(ss[0:TK, k % 2, :], SQ[0:TK, k % 2, :].rearrange("p (j d) -> p j d", d=D),
                                AX.X, ALU.add).then_inc(sem("ss_ready"), 1)

            def keys(b, n, k, first_pair):
                g = k % NG
                dve.wait_ge(sem("sdk_ready"), n + 1)
                r = rk[0:TK, k % 2, :, :]
                v.reciprocal(r.rearrange("p t j -> p (t j)"), sdk[0:TK, k % 2, :]).then_inc(sem("rk_ready"), 1)
                dve.wait_ge(sem("rk_ready"), n + 1)
                if not (first_pair and k < 2):
                    dve.wait_ge(sem("vn_ready"), n - 1)
                v.tensor_tensor(wv[0:TK, k % 2, :], r[:, :, 1], em2[0:TK, bass.ds(b * T + GT * g, GT)],
                                ALU.mult)
                dve.wait_ge(sem("kv_done"), n + 1)
                y = ps2[0:TK, 1024 * g:1024 * g + 1024].rearrange("p (t n) -> p t n", t=GT)[:, :, 0:D]
                v.tensor_tensor(KN[0:TK, k, :, :], y, bc(r[:, :, 0], 2, [TK, GT, D]),
                                ALU.mult).then_inc(sem("kn_ready"), 1)

            def relu(n, k):
                dve.wait_ge(sem("kb0_ready"), n + 1)
                kn = KN[0:TK, k, :, :]
                v.tensor_scalar(kn, kn, 0.0, EPS_IN, ALU.max, ALU.add).then_inc(sem("kp_ready"), 1)

            def state(b, par):
                dve.wait_ge(sem("kv_done"), NG * (b + 1) + SLOTS)
                kv = ps[:, 6 + par, :]
                v.tensor_tensor(kvtmp[:, par, :], kv[:, 0:D], gmask[:], ALU.mult).then_inc(sem("kvt_ready"), 1)
                v.tensor_scalar(kvall[:, bass.ds(b, 1), D:KVW], hmask[:].unsqueeze(1), kv[:, D + 1:D + 2], None,
                                ALU.mult)
                dve.wait_ge(sem("kvt_ready"), b + 1)
                v.scalar_tensor_tensor(kvall[:, bass.ds(b, 1), 0:D], bmask[:].unsqueeze(1), kv[:, D:D + 1],
                                       kvtmp[:, par, :].unsqueeze(1), ALU.mult, ALU.add).then_inc(sem("kv_read"), 1)

            def pair(i):
                first = isinstance(i, int) and i == 0
                for par in range(2):
                    b = 2 * i + par
                    for g in range(NG):
                        n, k = NG * b + g, NG * par + g
                        norms(n, k)
                        if not (first and k < 2):
                            relu(n - 2, (k - 2) % SLOTS)
                        if g == 0 and not first:
                            state(b - 2, par)
                        keys(b, n, k, first)

            in_pairs(dve, pair, B // 2)
            last = NG * B - 1
            relu(last - 1, SLOTS - 2)
            relu(last, SLOTS - 1)
            state(B - 2, 0)
            state(B - 1, 1)

            dve.wait_ge(sem("nd_ready"), 1)

            def nd(t):
                return ps[:, t // 3, KVW * (t % 3):KVW * (t % 3) + KVW]

            for t in range(NT):
                ins = v.tensor_scalar(xn[:, t, 0:H], nd(t)[:, D:KVW], EPS_IN, None, ALU.add)
            step(ins)
            step(v.reciprocal(xn[:, :, H:2 * H], xn[:, :, 0:H]))
            for t in range(NT):
                ins = v.tensor_tensor(att[:, t, :].rearrange("p (h d) -> p h d", h=H),
                                      nd(t)[:, 0:D].rearrange("p (h d) -> p h d", h=H),
                                      bc(xn[:, t, H:2 * H], 2, [128, H, DK]), ALU.mult)
            ins.then_inc(sem("att0_ready"), 1)
            def key_rest(w, unit, b, par):
                k = int(unit[1])
                dve.wait_ge(sem("kp1_ready"), KC * b + k + 1)
                if k == 0 and not (isinstance(b, int) and b == 0):
                    dve.wait_ge(sem("kp3_ready"), b)
                cols = slice(KCW * k, KCW * k + KCW)
                v.scalar_tensor_tensor(krest[:, cols], ps[:, bank_of(w, unit), 0:KCW], bk_sb[:], KP[par][0][:, cols],
                                       ALU.add, ALU.subtract).then_inc(sem("side_free"), 1)

            dve.wait_ge(sem("late_in"), LATE)
            v.tensor_reduce(wabs[:, 0:2], wgu[:], AX.X, ALU.add, apply_absolute_value=True)
            v.tensor_reduce(wabs[:, 2:3], wdn[:].rearrange("p c n -> p (c n)"), AX.X, ALU.add,
                            apply_absolute_value=True).then_inc(sem("wabs_ready"), 1)
            step(v.tensor_scalar(keep[0:TK, :], mi[0:TK, :], 0.0, None, ALU.not_equal))
            v.tensor_reduce(kept[0:TK, :], keep[0:TK, :].rearrange("p (b t) -> p b t", b=B), AX.X,
                            ALU.max).then_inc(sem("kept_ready"), 1)
            dve.wait_ge(sem("kept_ps"), 1)
            step(v.tensor_scalar(anykept[:], ps[:, 0, 0:B], 0.0, 1e9, ALU.is_gt, ALU.mult))
            v.tensor_scalar(kscale[0:TK, :], keep[0:TK, :], SCALE, None, ALU.mult)
            step(v.tensor_scalar(keep[0:TK, :], keep[0:TK, :], 1.0, None, ALU.subtract))
            v.tensor_tensor(kbias[0:TK, :].rearrange("p (b t) -> p b t", b=B),
                            keep[0:TK, :].rearrange("p (b t) -> p b t", b=B),
                            bc(anykept[0:TK, :], 2, [TK, B, T]), ALU.mult).then_inc(sem("kb_ready"), 1)
            for unit in EARLY[0:3]:
                key_rest(-1, unit, 0, 0)
            dve.wait_ge(sem("wsum_ps"), 1)
            step(v.tensor_scalar(wmean[:], ps[:, 3, 0:3], 1.0 / (INNER * D), 1e-5, ALU.mult, ALU.max))
            step(v.reciprocal(wscale[:], wmean[:]))
            for k in range(2):
                v.tensor_scalar(wgu[:, k, :], wgu[:, k, :], wscale[:, k:k + 1], ROUND, ALU.mult, ALU.add)
            step(v.tensor_scalar(wdn[:], wdn[:], wscale[:, 2:3], ROUND, ALU.mult, ALU.add))
            v.tensor_scalar(wgu[:], wgu[:], ROUND, -1.0, ALU.subtract, ALU.max)
            step(v.tensor_scalar(wdn[:], wdn[:], ROUND, -1.0, ALU.subtract, ALU.max))
            v.tensor_scalar(wgub[:], wgu[:], 1.0, None, ALU.min)
            v.tensor_scalar(wdnb[:], wdn[:], 1.0, None, ALU.min).then_inc(sem("wq_ready"), 1)

            dve.wait_ge(sem("th_ready"), 1)
            v.tensor_scalar(gmask[:], row[:, GAMMA, :], th[:, 0:1], None, ALU.mult)
            step(v.tensor_scalar(bmask[:], row[:, BETA, :], th[:, 0:1], None, ALU.mult))
            step(v.tensor_tensor(x[:], x[:], bc(bmask[:], 1, [128, NT, D]), ALU.add))
            dve.wait_ge(sem("dense_ps"), 1)
            step(v.tensor_tensor(t0[:], bank4(1), rows_of(DENSE_B), ALU.add))
            for t in range(NT):
                ins = v.bn_stats(stats[:, t, :], t0[:, t, :])
            step(ins)
            for t in range(NT):
                ins = v.bn_aggr(mv[:, t, :], stats[:, t, :])
            ins.then_inc(sem("ln_var"), 1)
            dve.wait_ge(sem("ln_var"), 3)
            for t in range(NT):
                ins = v.scalar_tensor_tensor(t0[:, t, :], t0[:, t, :], mv[:, t, 0:1], gmask[:], ALU.subtract, ALU.mult)
            step(ins)
            dve.wait_ge(sem("ln_std"), 3)
            step(v.reciprocal(rstd[:], sd[:]))
            for t in range(NT):
                ins = v.scalar_tensor_tensor(x[:, t, :], t0[:, t, :], rstd[:, t:t + 1], x[:, t, :], ALU.mult, ALU.add)
            step(ins)

            def steps_of():
                step(v.tensor_scalar(amax[:], amax[:], 1e-5, None, ALU.max))
                step(v.reciprocal(qs[:], amax[:]))
                v.tensor_scalar(qs[:], qs[:], 127.0, None, ALU.mult)
                step(v.tensor_scalar(amax[:], amax[:], 1.0 / 127.0, None, ALU.mult))

            layernorm(4, x, xn)
            step(v.tensor_reduce(amax[:], xn[:], AX.X, ALU.max, apply_absolute_value=True))
            steps_of()
            for t in range(NT):
                ins = v.tensor_scalar(t0[:, t, :], xn[:, t, :], qs[:, t:t + 1], ROUND, ALU.mult, ALU.add)
            step(ins)
            v.tensor_scalar(xqb[:], t0[:], ROUND, None, ALU.subtract).then_inc(sem("xq_ready"), 1)
            v.tensor_scalar(cg[:], amax[:], wmean[:, 0:1], None, ALU.mult)
            v.tensor_scalar(cu[:], amax[:], wmean[:, 1:2], None, ALU.mult).then_inc(sem("cgu_ready"), 1)
            key_rest(-1, EARLY[6], 1, 1)
            for t in range(NT + 1):
                if t < NT:
                    dve.wait_ge(sem("silu_ready"), t + 1)
                    if t == 0:
                        dve.wait_ge(sem("cgu_ready"), 1)
                    v.scalar_tensor_tensor(hid[:, t, :], ps[:, 2 + t % 2, :], cu[:, t:t + 1], silu[:, t % 2, :],
                                           ALU.mult, ALU.mult).then_inc(sem("hid_ready"), 1)
                if t > 0:
                    dve.wait_ge(sem("hid_ready"), t)
                    ins = v.tensor_reduce(amax[:, t - 1:t], hid[:, t - 1, :], AX.X, ALU.max, apply_absolute_value=True)
            step(ins)
            steps_of()
            for t in range(NT + 1):
                if t < NT:
                    v.tensor_scalar(hid[:, t, :], hid[:, t, :], qs[:, t:t + 1], ROUND, ALU.mult,
                                    ALU.add).then_inc(sem("hr_ready"), 1)
                if t > 0:
                    dve.wait_ge(sem("hr_ready"), t)
                    v.tensor_scalar(hqb[:, t - 1, :], hid[:, t - 1, :], ROUND, None,
                                    ALU.subtract).then_inc(sem("hq_ready"), 1)
            step(v.tensor_scalar(cd[:], amax[:], wmean[:, 2:3], th[:, 2:3], ALU.mult, ALU.mult))
            key_rest(-1, EARLY[7], 1, 1)
            dve.wait_ge(sem("ffn_ps"), 1)
            for t in range(NT):
                ins = v.scalar_tensor_tensor(x[:, t, :], bank4(0)[:, t, :], cd[:, t:t + 1], x[:, t, :],
                                             ALU.mult, ALU.add)
            step(ins)
            layernorm(5, x, xn, "ln_done")

            key_rest(-1, EARLY[8], 1, 1)
            step(v.tensor_scalar(bmask[:], row[:, B_O, :], th[:, 1:2], None, ALU.mult))
            step(v.tensor_tensor(x[:], x[:], bc(bmask[:], 1, [128, NT, D]), ALU.add))
            dve.wait_ge(sem("q1T_ready"), 2)
            v.tensor_copy(QP[0], qT[:]).then_inc(sem("qp1_ready"), 1)
            dve.wait_ge(sem("qp1_ready"), 1)
            step(v.tensor_tensor(qT[:], qT[:], QP[0], ALU.subtract))
            step(v.tensor_copy(QP[1], qT[:]))
            v.tensor_tensor(QP[2], qT[:], QP[1], ALU.subtract).then_inc(sem("qp_ready"), 1)

            def empty(w, unit, b, par):
                bank = bank_of(w, unit)
                dve.wait_ge(sem("aux_ready"), filled(w, unit))
                if unit[:2] == "MX":
                    c, k = divmod(int(unit[2:]), KC)
                    if c == 0 and k == 0 and not (isinstance(b, int) and b == 0):
                        dve.wait_ge(sem("mneg_ready"), b)
                    ins = v.tensor_reduce(mx[:, c, k:k + 1], ps[:, bank, 0:KCW], AX.X, ALU.max)
                elif unit == "SH":
                    if not (isinstance(b, int) and b < 2):
                        dve.wait_ge(sem("sc_ready"), T * (b - 1))
                    for k in range(2):
                        r = ONES - 32 * k
                        ins = v.tensor_copy(QS[par][ONES:ONES + 1, HQ2 * k:HQ2 * k + HQ2],
                                            ps[r:r + 1, bank, 0:HQ2])
                elif unit == "DEN":
                    ins = v.reciprocal(rden[:], ps[:, bank, 0:2 * PAIRW])
                else:
                    dst = att[HALF * par:HALF * par + S, bass.ds(b // 2, 1), :]
                    ins = v.tensor_copy(dst, ps[HALF * par:HALF * par + S, bank, 0:D].unsqueeze(1))
                ins.then_inc(sem(free_of(w, unit)), 1)
                if unit == "DEN":
                    dve.wait_ge(sem(free_of(w, unit)), emptied(w, unit))
                    v.tensor_tensor(On[:], O[:], rden[:], ALU.mult).then_inc(sem("on_mul"), 1)
                    dve.wait_ge(sem("on_mul"), b + 1)
                    on3 = On[:].rearrange("p (c n) -> p c n", c=2)
                    v.tensor_tensor(on3, on3, bc(bv_sb[:], 2, [128, 2, PAIRW]), ALU.add).then_inc(sem("on_ready"), 1)

            def maxima(w):
                for unit in MXS[-2:]:
                    dve.wait_ge(sem(free_of(w, unit)), emptied(w, unit))
                v.tensor_reduce(mneg[:], mx[:], AX.X, ALU.max, negate=True).then_inc(sem("mneg_ready"), 1)

            def window(w, par):
                todo = [unit for unit in units(w) if unit[0] != "V"]
                for k in range(KC):
                    if f"K{k}" in todo:
                        n = todo.index(f"K{k}")
                        todo.insert(n + REST_LATER, todo.pop(n))
                for unit in todo:
                    if unit == "SH":
                        maxima(w)
                    if unit[0] == "K":
                        key_rest(w, unit, w + 2, par)
                    elif unit in ENDS:
                        empty(w, unit, w - 1, 1 - par)
                    else:
                        empty(w, unit, w + 1, 1 - par)

            for unit in MXS + ["SH"]:
                if unit == "SH":
                    maxima(-1)
                empty(-1, unit, 0, 0)

            def pair1(i):
                for par in range(2):
                    window(2 * i + par, par)

            in_pairs(dve, pair1, B // 2)

            def residual(tiles):
                step(v.scalar_tensor_tensor(x[:, tiles, :], att[:, tiles, :], th[:, 1:2], x[:, tiles, :],
                                            ALU.mult, ALU.add))
                for t in range(tiles.start, tiles.stop):
                    ins = v.bn_stats(stats[:, t, :], x[:, t, :])
                step(ins)
                for t in range(tiles.start, tiles.stop):
                    ins = v.bn_aggr(mv[:, t, :], stats[:, t, :])
                return ins

            for w in (B - 2, B - 1):
                dve.wait_ge(sem(free_of(w, "WO")), emptied(w, "WO"))
            step(residual(slice(0, NT - 1)))
            empty(B, "DEN", B - 1, 1)
            empty(B, "WO", B - 1, 1)
            dve.wait_ge(sem(free_of(B, "WO")), emptied(B, "WO"))
            residual(slice(NT - 1, NT)).then_inc(sem("ln_var"), 1)
            dve.wait_ge(sem("ln_std"), 6)
            step(v.reciprocal(rstd[:], sd[:]))
            for t in range(NT):
                ins = v.tensor_scalar(xn[:, t, :], x[:, t, :], mv[:, t, 0:1], rstd[:, t:t + 1],
                                      ALU.subtract, ALU.mult)
            ins.then_inc(sem("ln_done"), 1)

            dve.wait_ge(sem("logit_ps"), 1)
            lg = ps[:, 6, 0:NT * E].rearrange("p (t e) -> p t e", e=E)
            full3 = [128, NT, E]
            step(v.tensor_reduce(pm[:], lg, AX.X, ALU.max))
            v.tensor_tensor(pr[:], lg, bc(pm[:], 2, full3), ALU.subtract).then_inc(sem("logit_ready"), 1)
            dve.wait_ge(sem("pexp_ready"), 1)
            step(v.tensor_reduce(pd[:], pr[:], AX.X, ALU.add))
            step(v.reciprocal(pd[:], pd[:]))
            step(v.tensor_tensor(pr[:], pr[:], bc(pd[:], 2, full3), ALU.mult))
            step(v.tensor_copy(pc[:], pr[:]))
            for k in range(2):
                step(v.tensor_reduce(pm[:], pc[:], AX.X, ALU.max))
                step(v.tensor_tensor(ph[:], pc[:], bc(pm[:], 2, full3), ALU.is_equal))
                step(v.tensor_tensor(ph[:], ph[:], rank[:], ALU.mult))
                step(v.tensor_reduce(pm[:], ph[:], AX.X, ALU.max))
                step(v.tensor_tensor(ph[:], rank[:], bc(pm[:], 2, full3), ALU.is_equal))
                if k == 0:
                    step(v.tensor_copy(pg[:], ph[:]))
                    step(v.scalar_tensor_tensor(pc[:], ph[:], -2.0, pc[:], ALU.mult, ALU.add))
            step(v.tensor_tensor(pg[:], pg[:], ph[:], ALU.add))
            step(v.tensor_tensor(pg[:], pg[:], pr[:], ALU.mult))
            v.tensor_scalar(pg[:], pg[:], th[:, 3:4], None, ALU.mult).then_inc(sem("pg_ready"), 1)
            dve.wait_ge(sem("pgT_ps"), 1)
            v.tensor_copy(pgT[:], ps[0:ND * E, 7, 0:128]).then_inc(sem("pgT_ready"), 1)
            dve.wait_ge(sem("b2_ps"), 1)
            dve.wait_ge(sem("xd_in"), 16)
            dve.wait_ge(sem("pgd_in"), 16)
            v.tensor_tensor(xd, xd, bank4(6)[:, 0:ND, :], ALU.add).then_inc(sem("b2_done"), 1)

            def add_expert(e, par, first_pair):
                for k in range(2):
                    dve.wait_ge(sem("down_ready"), 2 * e + k + 1)
                    if first_pair and par == 0:
                        dve.wait_ge(sem("b2_done"), 1)
                    else:
                        dve.wait_ge(sem("moe_done"), 2 * e + k - 1)
                    for t in range(min(4, ND - 4 * k)):
                        ins = v.scalar_tensor_tensor(xd[:, 4 * k + t, :], ps[:, 4 + 2 * par + k, 128 * t:128 * t + 128],
                                                     pgd[:, 4 * k + t, bass.ds(e, 1)], xd[:, 4 * k + t, :],
                                                     ALU.mult, ALU.add)
                    ins.then_inc(sem("moe_done"), 1)

            def pair2(i):
                for par in range(2):
                    add_expert(2 * i + par, par, isinstance(i, int) and i == 0)

            in_pairs(dve, pair2, E // 2)


def _layout(v):
    import numpy as np
    f = np.float32
    xh = np.zeros((128, NT, D), f)
    x4 = v["x"].reshape(NT, 2, S, D)
    xh[0:S] = x4[:, 0].transpose(1, 0, 2)
    xh[HALF:HALF + S] = x4[:, 1].transpose(1, 0, 2)

    def rep(a):
        return np.broadcast_to(a, (128,) + a.shape)

    wo = np.zeros((4, PW, 2, 2, D), f)
    woT = v["L1_xattn_W_o"].T.reshape(2, 4, 2, DK, D)
    for k in range(2):
        wo[:, 1 + DK * k:1 + DK * k + DK, :, k, :] = woT[:, :, k].transpose(1, 2, 0, 3)
    bv = np.zeros((4, PW, 2), f)
    bv[:, 1:1 + 2 * DK] = v["L1_xattn_b_v"].reshape(2, 4, 2 * DK).transpose(1, 2, 0)
    order = np.arange(D).reshape(NPAIR, 2 * DK).T.reshape(D)
    b2 = np.zeros((ND, E, ND, D), f)
    for t in range(ND):
        b2[t, :, t] = v["L1_ffn_b2"]
    sel = np.zeros((128, 128), f)
    for j in range(4):
        sel[PW * j, PW * j:PW * j + PW] = 1.0
    mask = lambda m: m.reshape(B, T, TK).transpose(2, 0, 1).reshape(TK, B * T)
    return {
        "xh": xh,
        "ctxT": v["ctx_1024"].reshape(B * S2, D).T,
        "m0": mask(v["mask_BxS2_ff1"]),
        "m1": mask(v["mask_BxS2_if1"]),
        "gates": rep(np.concatenate([v["g_xattn"], v["g_ffn"]])),
        "rows": rep(np.stack([v["L0_xattn_ln_gamma"], v["L0_xattn_ln_beta"], v["L0_xattn_dense_b"],
                              v["L1_xattn_b_o"]])),
        "bq": v["L1_xattn_b_q"][order].reshape(D, 1),
        "bk": v["L1_xattn_b_k"][order].reshape(D, 1),
        "bv": bv.reshape(128, 2),
        "wkv0": np.stack([v["L0_xattn_wk"], v["L0_xattn_wv"]], axis=1),
        "wq0": v["L0_xattn_wq"],
        "dense0": v["L0_xattn_dense_w"],
        "wg0": v["L0_ffn_w_gate"].T,
        "wu0": v["L0_ffn_w_up"].T,
        "wd0": v["L0_ffn_w_down"].T.reshape(FC, 128, D).transpose(1, 0, 2),
        "wq1": v["L1_xattn_W_q"][order].T,
        "wk1": v["L1_xattn_W_k"][order].T,
        "wv1": v["L1_xattn_W_v"].T,
        "wo1": wo.reshape(128, 4, D),
        "gatew": v["L1_ffn_gate_w"].T,
        "w1": v["L1_ffn_w1"].transpose(2, 1, 0).reshape(D, E * INNER),
        "b1": v["L1_ffn_b1"].reshape(E * FC, 128).T,
        "w2": v["L1_ffn_w2"].transpose(1, 2, 0).reshape(E, FC, 128, D).transpose(2, 0, 1, 3).reshape(128, E * INNER),
        "b2": b2.reshape(ND * E, ND, D),
        "ident_in": np.eye(128, dtype=f),
        "hmask_in": np.repeat(np.eye(H, dtype=f), DK, axis=0),
        "hmask1_in": np.repeat(np.eye(H, dtype=f), DK, axis=0)[order],
        "pmask_in": np.repeat(np.eye(2, dtype=f), HALF, axis=0),
        "den_sel_in": sel,
        "rank_in": np.broadcast_to(np.arange(E, 0, -1).astype(f), (128, NT, E)),
    }


def kernel(**inputs):
    import numpy as np
    import concourse.bacc as bacc
    from concourse.bass_utils import run_bass_kernel_spmd

    laid = {n: np.ascontiguousarray(a) for n, a in _layout({k: np.asarray(a) for k, a in inputs.items()}).items()}
    nc = bacc.Bacc("TRN2", target_bir_lowering=False, num_devices=1)
    args = {n: nc.dram_tensor(n + "_dram", a.shape, mybir.dt.from_np(a.dtype), kind="ExternalInput").ap()
            for n, a in laid.items()}
    out = nc.dram_tensor("out_dram", (B, S, D), F32, kind="ExternalOutput").ap()
    build(nc, out=out, **args)
    r = run_bass_kernel_spmd(nc, [{n + "_dram": a for n, a in laid.items()}], core_ids=[0])
    return r.results[0]["out_dram"]
```
